# Optimizing a Trainium2 kernel written in Bass

```python
import numpy as np
import jax
import jax.numpy as jnp

def _softmax(x, axis=-1):
    return jax.nn.softmax(x, axis=axis)

def _gelu(x):
    return jax.nn.gelu(x, approximate=True)

def _silu(x):
    return jax.nn.silu(x)

def _sigmoid(x):
    return jax.nn.sigmoid(x)

def _layernorm(x, axis=-1, eps=1e-05):
    m = jnp.mean(x, axis=axis, keepdims=True)
    v = jnp.var(x, axis=axis, keepdims=True)
    return (x - m) / jnp.sqrt(v + eps)

def _scatter_add(tgt, idx, src, axis=0):
    return tgt.at[idx].add(src)

def _segment_sum(src, seg, n):
    return jax.ops.segment_sum(src, seg, n)
kernel_name = 'mk_xattn_ffn_d2_seqx_r8_a52261'

def setup_inputs(seed: int=0):
    np.random.seed(seed)
    _w = jnp.asarray

    def _rec_inputs():
        import jax
        import jax.numpy as jnp
        _rk = jax.random.key(seed)
        x = -0.0003929 + 0.9999 * jax.random.normal(jax.random.fold_in(_rk, 1), (16, 64, 512), jnp.float32)
        _lenS = 64 - jax.random.randint(jax.random.fold_in(_rk, 7), (16,), 0, max(1, 64 // 4) + 1, jnp.int32)
        _lenS2 = 64 - jax.random.randint(jax.random.fold_in(_rk, 8), (16,), 0, max(1, 64 // 4) + 1, jnp.int32)
        _ctx_4096P = jax.random.normal(jax.random.fold_in(_rk, 11), (16, 16, 512), jnp.float32)
        _ctx_4096c = jax.random.dirichlet(jax.random.fold_in(_rk, 511), 0.3 * jnp.ones((16,), jnp.float32), (16, 64))
        _ctx_4096t = jnp.einsum('bsk,bkd->bsd', _ctx_4096c, _ctx_4096P)
        _ctx_4096t = _ctx_4096t * jax.lax.rsqrt(jnp.mean(jnp.square(_ctx_4096t)) + 1e-12) * 0.953939
        ctx_4096 = 2.81802e-05 + 1.00001 * (_ctx_4096t + 0.3 * jax.random.normal(jax.random.fold_in(_rk, 611), (16, 64, 512), jnp.float32))
        pos_BxS2 = jnp.broadcast_to(jnp.arange(64, dtype=jnp.int32), (16, 64))
        _validS = jnp.arange(64)[None, :] < _lenS[:, None]
        _validS2 = jnp.arange(64)[None, :] < _lenS2[:, None]
        _causal = jnp.tril(jnp.ones((64, 64), dtype=bool))
        mask_BxSxS2_ik0 = jnp.where(jnp.broadcast_to(_validS2[:, None, :], (16, 64, 64)), 0, 1).astype(jnp.int32)
        return (x, ctx_4096, pos_BxS2, mask_BxSxS2_ik0)
    x, ctx_4096, pos_BxS2, mask_BxSxS2_ik0 = _rec_inputs()

    def _L0_xattn_setup():
        import jax, jax.numpy as jnp
        import numpy as np
        HID = 512
        NHEAD = 32
        NKV = 8
        HDIM = 128
        G = NHEAD // NKV
        key = jax.random.key(seed)
        ks = jax.random.split(key, 6)
        s = 0.02
        B, L = (2, 256)
        return {'query': jax.random.normal(ks[0], (B, L, HID), jnp.float32), 'kv': jax.random.normal(ks[1], (B, L, HID), jnp.float32), 'Wq': jax.random.normal(ks[2], (HID, NHEAD * HDIM), jnp.float32) * s, 'bq': jnp.zeros((NHEAD * HDIM,), jnp.float32), 'Wkv': jax.random.normal(ks[3], (HID, 2 * NKV * HDIM), jnp.float32) * s, 'bkv': jnp.zeros((2 * NKV * HDIM,), jnp.float32), 'Wo': jax.random.normal(ks[4], (NHEAD * HDIM, HID), jnp.float32) * s, 'bo': jnp.zeros((HID,), jnp.float32)}
    _L0_xattn_all = _L0_xattn_setup()
    _L0_xattn_in = {k: v for k, v in _L0_xattn_all.items() if k in ('Wq', 'bq', 'Wkv', 'bkv', 'Wo', 'bo')}
    del _L0_xattn_all

    def _L0_ffn_setup():
        import jax, jax.numpy as jnp
        import numpy as np
        MAX_THRESHOLD = 1.0 / 8.0
        SCALING = 32.0 / 16.0
        key = jax.random.key(seed)
        ks = jax.random.split(key, 8)
        B_, S, D, O, E, R = (4, 256, 512, 512, 8, 16)
        sd = 1.0 / np.sqrt(D)
        return {'x': jax.random.normal(ks[0], (B_, S, D), jnp.float32), 'W_base': jax.random.normal(ks[1], (O, D), jnp.float32) * sd, 'b_base': jax.random.normal(ks[2], (O,), jnp.float32) * 0.01, 'W_gate': jax.random.normal(ks[3], (E, D), jnp.float32) * sd, 'W_thr': jax.random.normal(ks[4], (1, D), jnp.float32) * sd, 'b_thr': jax.random.normal(ks[5], (1,), jnp.float32) * 0.01, 'A': jax.random.normal(ks[6], (E, R, D), jnp.float32) * sd, 'B': jax.random.normal(ks[7], (O,), jnp.float32)[None, :, None] * jnp.zeros((E, O, R), jnp.float32) + jax.random.normal(jax.random.fold_in(key, 7), (E, O, R), jnp.float32) * (1.0 / np.sqrt(R))}
    _L0_ffn_all = _L0_ffn_setup()
    _L0_ffn_in = {k: v for k, v in _L0_ffn_all.items() if k in ('W_base', 'b_base', 'W_gate', 'W_thr', 'b_thr', 'A', 'B')}
    del _L0_ffn_all

    def _L1_xattn_setup():
        import jax, jax.numpy as jnp
        import numpy as np
        B, S, E = (2, 256, 512)
        H, KVH, D = (32, 8, 128)
        GROUPS = H // KVH
        MAX_POS = 512
        ROPE_THETA = 10000.0

        def _rope_tables(max_pos, dim, theta):
            inv_freq = 1.0 / theta ** (jnp.arange(0, dim, 2, dtype=jnp.float32) / dim)
            t = jnp.arange(max_pos, dtype=jnp.float32)
            freqs = jnp.einsum('i,j->ij', t, inv_freq)
            emb = jnp.concatenate([freqs, freqs], axis=-1)
            return (jnp.cos(emb), jnp.sin(emb))

        def _rotate_half(x):
            x1, x2 = (x[..., :x.shape[-1] // 2], x[..., x.shape[-1] // 2:])
            return jnp.concatenate([-x2, x1], axis=-1)
        key = jax.random.key(seed)
        ks = jax.random.split(key, 8)
        scale_w = 1.0 / np.sqrt(E)
        query = jax.random.normal(ks[0], (B, S, E), dtype=jnp.float32)
        k_in = jax.random.normal(ks[1], (B, S, E), dtype=jnp.float32)
        v_in = jax.random.normal(ks[2], (B, S, E), dtype=jnp.float32)
        position_ids = jnp.broadcast_to(jnp.arange(S, dtype=jnp.int64), (B, S))
        src_mask = jnp.tril(jnp.ones((S, S), dtype=jnp.int32))
        src_mask = jnp.broadcast_to(src_mask, (B, S, S))
        Wq = jax.random.normal(ks[3], (E, H * D), dtype=jnp.float32) * scale_w
        Wk = jax.random.normal(ks[4], (E, KVH * D), dtype=jnp.float32) * scale_w
        Wv = jax.random.normal(ks[5], (E, KVH * D), dtype=jnp.float32) * scale_w
        Wo = jax.random.normal(ks[6], (H * D, E), dtype=jnp.float32) * scale_w
        return {'query': query, 'key': k_in, 'value': v_in, 'position_ids': position_ids, 'src_mask': src_mask, 'Wq': Wq, 'Wk': Wk, 'Wv': Wv, 'Wo': Wo}
    _L1_xattn_all = _L1_xattn_setup()
    _L1_xattn_in = {k: v for k, v in _L1_xattn_all.items() if k in ('Wq', 'Wk', 'Wv', 'Wo')}
    del _L1_xattn_all

    def _L1_ffn_setup():
        import jax, jax.numpy as jnp
        import numpy as np
        N_STREAMS = 4
        DIM = 128
        SINKHORN_ITERS = 50
        SINKHORN_TAU = 0.1
        RMS_EPS = 1.1920929e-07

        def sinkhorn_log(logits, num_iters=SINKHORN_ITERS, tau=SINKHORN_TAU):
            Z = logits / tau
            u0 = jnp.zeros(Z.shape[:-1], Z.dtype)
            v0 = jnp.zeros_like(u0)

            def step(carry, _):
                u, v = carry
                u = -jax.nn.logsumexp(Z + v[..., None, :], axis=-1)
                v = -jax.nn.logsumexp(Z + u[..., :, None], axis=-2)
                return ((u, v), None)
            (u, v), _ = jax.lax.scan(step, (u0, v0), None, length=num_iters)
            return jnp.exp(Z + u[..., :, None] + v[..., None, :])
        key = jax.random.key(seed)
        ks = jax.random.split(key, 6)
        B, T = (4, 256)
        n, C = (N_STREAMS, DIM)
        wd = n * C
        x = jax.random.normal(ks[0], (B, T, wd), dtype=jnp.float32)
        W_res = 0.01 * jax.random.normal(ks[1], (n * n, wd), dtype=jnp.float32)
        W_pre = 0.01 * jax.random.normal(ks[2], (n, wd), dtype=jnp.float32)
        W_post = 0.01 * jax.random.normal(ks[3], (n, wd), dtype=jnp.float32)
        H_res_base = jnp.full((n, n), -0.5, dtype=jnp.float32)
        H_res_base = H_res_base.at[jnp.arange(n), jnp.arange(n)].set(0.0)
        H_pre_base = jnp.zeros((n,), dtype=jnp.float32).at[0].set(1.0)
        H_post_base = jnp.zeros((n,), dtype=jnp.float32)
        gate = jnp.array([5.0], dtype=jnp.float32)
        W_branch = 1.0 / np.sqrt(C) * jax.random.normal(ks[4], (C, C), dtype=jnp.float32)
        return {'x': x, 'W_res': W_res, 'W_pre': W_pre, 'W_post': W_post, 'H_res_base': H_res_base, 'H_pre_base': H_pre_base, 'H_post_base': H_post_base, 'gate': gate, 'W_branch': W_branch}
    _L1_ffn_all = _L1_ffn_setup()
    _L1_ffn_in = {k: v for k, v in _L1_ffn_all.items() if k in ('W_res', 'W_pre', 'W_post', 'H_res_base', 'H_pre_base', 'H_post_base', 'gate', 'W_branch')}
    del _L1_ffn_all
    return {'x': x, 'ctx_4096': ctx_4096, 'pos_BxS2': pos_BxS2, 'mask_BxSxS2_ik0': mask_BxSxS2_ik0, 'L0_xattn_Wq': _L0_xattn_in['Wq'], 'L0_xattn_bq': _L0_xattn_in['bq'], 'L0_xattn_Wkv': _L0_xattn_in['Wkv'], 'L0_xattn_bkv': _L0_xattn_in['bkv'], 'L0_xattn_Wo': _L0_xattn_in['Wo'], 'L0_xattn_bo': _L0_xattn_in['bo'], 'L0_ffn_W_base': _L0_ffn_in['W_base'], 'L0_ffn_b_base': _L0_ffn_in['b_base'], 'L0_ffn_W_gate': _L0_ffn_in['W_gate'], 'L0_ffn_W_thr': _L0_ffn_in['W_thr'], 'L0_ffn_b_thr': _L0_ffn_in['b_thr'], 'L0_ffn_A': _L0_ffn_in['A'], 'L0_ffn_B': _L0_ffn_in['B'], 'L1_xattn_Wq': _L1_xattn_in['Wq'], 'L1_xattn_Wk': _L1_xattn_in['Wk'], 'L1_xattn_Wv': _L1_xattn_in['Wv'], 'L1_xattn_Wo': _L1_xattn_in['Wo'], 'L1_ffn_W_res': _L1_ffn_in['W_res'], 'L1_ffn_W_pre': _L1_ffn_in['W_pre'], 'L1_ffn_W_post': _L1_ffn_in['W_post'], 'L1_ffn_H_res_base': _L1_ffn_in['H_res_base'], 'L1_ffn_H_pre_base': _L1_ffn_in['H_pre_base'], 'L1_ffn_H_post_base': _L1_ffn_in['H_post_base'], 'L1_ffn_gate': _L1_ffn_in['gate'], 'L1_ffn_W_branch': _L1_ffn_in['W_branch']}

def reference(x, ctx_4096, pos_BxS2, mask_BxSxS2_ik0, L0_xattn_Wq, L0_xattn_bq, L0_xattn_Wkv, L0_xattn_bkv, L0_xattn_Wo, L0_xattn_bo, L0_ffn_W_base, L0_ffn_b_base, L0_ffn_W_gate, L0_ffn_W_thr, L0_ffn_b_thr, L0_ffn_A, L0_ffn_B, L1_xattn_Wq, L1_xattn_Wk, L1_xattn_Wv, L1_xattn_Wo, L1_ffn_W_res, L1_ffn_W_pre, L1_ffn_W_post, L1_ffn_H_res_base, L1_ffn_H_pre_base, L1_ffn_H_post_base, L1_ffn_gate, L1_ffn_W_branch):
    import jax
    import jax.numpy as jnp

    def _L0_xattn_ref(query, kv, Wq, bq, Wkv, bkv, Wo, bo):
        import jax, jax.numpy as jnp
        import numpy as np
        HID = 512
        NHEAD = 32
        NKV = 8
        HDIM = 128
        G = NHEAD // NKV
        B, L, _ = query.shape
        Lk = kv.shape[1]
        scale = jnp.asarray(1.0 / np.sqrt(HDIM), query.dtype)
        q = (query @ Wq + bq).reshape(B, L, NKV, G, HDIM)
        k_, v_ = jnp.split(kv @ Wkv + bkv, 2, axis=-1)
        k = k_.reshape(B, Lk, NKV, HDIM)
        v = v_.reshape(B, Lk, NKV, HDIM)
        scores = jnp.einsum('blkgd,bmkd->bkglm', q, k) * scale
        attn = jax.nn.softmax(scores, axis=-1)
        o = jnp.einsum('bkglm,bmkd->blkgd', attn, v).reshape(B, L, NHEAD * HDIM)
        return o @ Wo + bo

    def _L0_ffn_ref(x, W_base, b_base, W_gate, W_thr, b_thr, A, B):
        import jax, jax.numpy as jnp
        import numpy as np
        MAX_THRESHOLD = 1.0 / 8.0
        SCALING = 32.0 / 16.0
        base = jnp.einsum('bsd,od->bso', x, W_base) + b_base
        D = x.shape[-1]
        xf = x.reshape(-1, D)
        gate_logits = jax.nn.softmax(xf @ W_gate.T, axis=-1)
        thresholds = jax.nn.sigmoid(xf @ W_thr.T + b_thr) * MAX_THRESHOLD
        adapted = gate_logits - thresholds
        selected = (adapted >= 0).astype(x.dtype)
        weights = adapted * selected
        wsum = jnp.sum(weights, axis=-1, keepdims=True)
        wsum = jnp.where(wsum == 0, jnp.ones_like(wsum), wsum)
        weights = weights / wsum
        h = jnp.einsum('nd,erd->ner', xf, A)
        moe = jnp.einsum('ner,ne,eor->no', h, weights, B) * SCALING
        out = base + moe.reshape(base.shape)
        return out

    def _L1_xattn_ref(query, key, value, position_ids, src_mask, Wq, Wk, Wv, Wo):
        import jax, jax.numpy as jnp
        import numpy as np
        B, S, E = (2, 256, 512)
        H, KVH, D = (32, 8, 128)
        GROUPS = H // KVH
        MAX_POS = 512
        ROPE_THETA = 10000.0

        def _rope_tables(max_pos, dim, theta):
            inv_freq = 1.0 / theta ** (jnp.arange(0, dim, 2, dtype=jnp.float32) / dim)
            t = jnp.arange(max_pos, dtype=jnp.float32)
            freqs = jnp.einsum('i,j->ij', t, inv_freq)
            emb = jnp.concatenate([freqs, freqs], axis=-1)
            return (jnp.cos(emb), jnp.sin(emb))

        def _rotate_half(x):
            x1, x2 = (x[..., :x.shape[-1] // 2], x[..., x.shape[-1] // 2:])
            return jnp.concatenate([-x2, x1], axis=-1)
        nb, q_len, _ = query.shape
        q = (query @ Wq).reshape(nb, q_len, H, D).transpose(0, 2, 1, 3)
        k = (key @ Wk).reshape(nb, q_len, KVH, D).transpose(0, 2, 1, 3)
        v = (value @ Wv).reshape(nb, q_len, KVH, D).transpose(0, 2, 1, 3)
        cos_t, sin_t = _rope_tables(MAX_POS, D, ROPE_THETA)
        cos = cos_t[position_ids][:, None]
        sin = sin_t[position_ids][:, None]
        q = q * cos + _rotate_half(q) * sin
        k = k * cos + _rotate_half(k) * sin
        k = jnp.repeat(k, GROUPS, axis=1)
        v = jnp.repeat(v, GROUPS, axis=1)
        scores = jnp.einsum('bhqd,bhkd->bhqk', q, k) / jnp.sqrt(jnp.float32(D))
        mask = src_mask[:, None]
        scores = jnp.where(mask == 0, jnp.float32(-1000000000.0), scores)
        attn = jax.nn.softmax(scores, axis=-1)
        x = jnp.einsum('bhqk,bhkd->bhqd', attn, v)
        x = x.transpose(0, 2, 1, 3).reshape(nb, q_len, H * D)
        return x @ Wo

    def _L1_ffn_ref(x, W_res, W_pre, W_post, H_res_base, H_pre_base, H_post_base, gate, W_branch):
        import jax, jax.numpy as jnp
        import numpy as np
        N_STREAMS = 4
        DIM = 128
        SINKHORN_ITERS = 50
        SINKHORN_TAU = 0.1
        RMS_EPS = 1.1920929e-07

        def sinkhorn_log(logits, num_iters=SINKHORN_ITERS, tau=SINKHORN_TAU):
            Z = logits / tau
            u0 = jnp.zeros(Z.shape[:-1], Z.dtype)
            v0 = jnp.zeros_like(u0)

            def step(carry, _):
                u, v = carry
                u = -jax.nn.logsumexp(Z + v[..., None, :], axis=-1)
                v = -jax.nn.logsumexp(Z + u[..., :, None], axis=-2)
                return ((u, v), None)
            (u, v), _ = jax.lax.scan(step, (u0, v0), None, length=num_iters)
            return jnp.exp(Z + u[..., :, None] + v[..., None, :])
        B, T, nC = x.shape
        n = N_STREAMS
        C = nC // n
        x_norm = x * jax.lax.rsqrt(jnp.mean(x * x, axis=-1, keepdims=True) + RMS_EPS)
        H_res_logits = (x_norm @ W_res.T).reshape(B, T, n, n) + H_res_base
        H_pre_logits = x_norm @ W_pre.T + H_pre_base
        H_post_logits = x_norm @ W_post.T + H_post_base
        H_res = sinkhorn_log(H_res_logits)
        H_pre = jax.nn.softmax(H_pre_logits, axis=-1)
        H_post = jax.nn.softmax(H_post_logits, axis=-1)
        g = jax.nn.sigmoid(gate)[0]
        I = jnp.eye(n, dtype=H_res.dtype)
        H_res = (1.0 - g) * I + g * H_res
        x_streams = x.reshape(B, T, n, C)
        x_pre = jnp.einsum('btnc,btn->btc', x_streams, H_pre)
        y = x_pre @ W_branch
        x_mixed = jnp.einsum('btij,btjc->btic', H_res, x_streams)
        y_distributed = jnp.einsum('btc,btn->btnc', y, H_post)
        return (x_mixed + y_distributed).reshape(B, T, nC)
    x = x + _L0_xattn_ref(_layernorm(x, axis=-1), ctx_4096, L0_xattn_Wq, L0_xattn_bq, L0_xattn_Wkv, L0_xattn_bkv, L0_xattn_Wo, L0_xattn_bo)
    x = x + _L0_ffn_ref(_layernorm(x, axis=-1), L0_ffn_W_base, L0_ffn_b_base, L0_ffn_W_gate, L0_ffn_W_thr, L0_ffn_b_thr, L0_ffn_A, L0_ffn_B)
    x = x + _L1_xattn_ref(_layernorm(x, axis=-1), ctx_4096, ctx_4096, pos_BxS2, mask_BxSxS2_ik0, L1_xattn_Wq, L1_xattn_Wk, L1_xattn_Wv, L1_xattn_Wo)
    x = x + _L1_ffn_ref(_layernorm(x, axis=-1), L1_ffn_W_res, L1_ffn_W_pre, L1_ffn_W_post, L1_ffn_H_res_base, L1_ffn_H_pre_base, L1_ffn_H_post_base, L1_ffn_gate, L1_ffn_W_branch)
    return x

_drawn_inputs = setup_inputs


def setup_inputs(seed=0):
    import zlib

    import numpy as np

    out = dict(_drawn_inputs(seed))
    spreads = {'L0_xattn_bq': (0.0, 0.8),
     'L0_xattn_bkv': (0.0, 0.1),
     'L0_xattn_bo': (0.0, 0.1),
     'L1_ffn_H_post_base': (0.0, 0.8)}
    factors = {'L0_xattn_Wq': 2.755, 'L0_ffn_b_base': 8.0, 'L1_ffn_W_pre': 8.0, 'L1_ffn_W_post': 6.853}
    for name, (base, spread) in spreads.items():
        noise = np.random.default_rng([zlib.crc32(name.encode()), seed]).standard_normal(out[name].shape)
        drawn = base * np.exp(spread * noise) if base else spread * noise
        out[name] = jnp.asarray(drawn.astype(out[name].dtype))
    for name, factor in factors.items():
        out[name] = (out[name] * factor).astype(out[name].dtype)
    return out
```

```python
from contextlib import ExitStack

import numpy as np

import concourse.bass as bass
from concourse import mybir

ALU = mybir.AluOpType
ACT = mybir.ActivationFunctionType
AX = mybir.AxisListType
F32 = mybir.dt.float32
F32R = mybir.dt.float32r
I32 = mybir.dt.int32
U8 = mybir.dt.uint8

P = 128
B, S = 16, 64
D = 512
NT = B * S
TILES = NT // P
HALF = NT // 2
HT = TILES // 2
HB = B // 2
KC = D // P
GROUPS, GH, DH = 8, 4, 128
PAIRS = HB // 2
EXPERTS, RANK = 8, 16
STREAMS, CH = 4, 128
MAX_POS = 512
SCALE = 1.0 / float(np.sqrt(np.float32(DH)))
MASKED = float(np.float32(-1e9) * np.sqrt(np.float32(DH)))
LN_EPS = 1e-5
RMS_EPS = 1.1920929e-07
TAU = 0.1
CYCLES, INNER = 5, 9
RING = 6
FFN0_SET = GROUPS
L1_SET = GROUPS + 1


def bass_two_layers(nc, x_in_ap, ctx_t, pos, mask, wq0, bqkv0, wkv0, wo0, bo0, wbase_t, bbase, gates_t,
                    b_thr, a_t, b_mat, wq1, wk1, wv1, wo1, mix_t, mix_base, gate, w_branch, tables, out):
    with ExitStack() as ctx:
        def sb(name, shape, dt=F32):
            return ctx.enter_context(nc.sbuf_tensor(name, shape, dt))

        def sem(name):
            return ctx.enter_context(nc.semaphore(name))

        x = sb("x", [P, TILES, D])
        ctx_hi = sb("ctx_hi", [P, KC, NT], F32R)
        ctx_lo = sb("ctx_lo", [P, KC, NT], F32R)
        z_hi = sb("z_hi", [P, KC, NT], F32R)
        z_lo = sb("z_lo", [P, KC, NT], F32R)
        wq_raw, wq_hi, wq_lo = sb("wq_raw", [P, KC, D]), sb("wq_hi", [P, KC, D], F32R), sb("wq_lo", [P, KC, D], F32R)
        wk_raw, wk_hi, wk_lo = sb("wk_raw", [P, KC, DH]), sb("wk_hi", [P, KC, DH], F32R), sb("wk_lo", [P, KC, DH], F32R)
        wv_raw, wv_hi, wv_lo = sb("wv_raw", [P, KC, DH]), sb("wv_hi", [P, KC, DH], F32R), sb("wv_lo", [P, KC, DH], F32R)
        wo_raw, wo_hi, wo_lo = sb("wo_raw", [P, GH, D]), sb("wo_hi", [P, GH, D], F32R), sb("wo_lo", [P, GH, D], F32R)
        q = sb("q", [P, GH, HALF])
        k = sb("k", [P, HALF])
        v_t = sb("v_t", [P, HALF])
        v = sb("v", [P, PAIRS, DH])
        probs = sb("probs", [P, 2, HB, S])
        probs_t = sb("probs_t", [P, PAIRS, 2, GH * S])
        o_hi = sb("o_hi", [P, GH, HALF], F32R)
        o_lo = sb("o_lo", [P, GH, HALF], F32R)
        row_max_sb = sb("row_max_sb", [P, 2, HB])
        row_sum_sb = sb("row_sum_sb", [P, 2, HB])
        row_inv_sb = sb("row_inv_sb", [P, 2, HB])
        cos = sb("cos", [P, NT])
        sin = sb("sin", [P, NT])
        rot = sb("rot", [P, 4, HALF])
        masked_out = sb("masked_out", [P, B, S], U8)
        masked_value = sb("masked_value", [P, 1])
        ident = sb("ident", [P, P])
        qk_bias = sb("qk_bias", [P, GH + 1])
        v_bias = sb("v_bias", [P, 2])
        bias_row = sb("bias_row", [P, D])
        pos_col = sb("pos_col", [P, KC])
        stats = sb("stats", [P, HT, 6])
        mean_var = sb("mean_var", [P, HT, 2])
        rstd = sb("rstd", [P, HT])

        gate_w = sb("gate_w", [P, HT, EXPERTS + 1])
        gate_s = sb("gate_s", [P, HT, 4])
        logits = sb("logits", [P, TILES, 24])
        mix_base_sb = sb("mix_base_sb", [P, 24])
        rms = sb("rms", [P, TILES])
        pp = sb("pp", [P, TILES, 2])
        scalars = sb("scalars", [P, 4])

        ring = ctx.enter_context(nc.psum_tensor("ring", [P, RING, 512], F32))
        scores = ctx.enter_context(nc.psum_tensor("scores", [P, 2, 512], F32))

        ident_cleared, ident_made = sem("ident_cleared"), sem("ident_made")
        x_in = [sem(f"x_in{h}") for h in range(2)]
        ctx_in = [sem(f"ctx_in{h}") for h in range(2)]
        tables_in, pos_in, mask_in, small_in = sem("tables_in"), sem("pos_in"), sem("mask_in"), sem("small_in")
        row_in = sem("row_in")
        wq_in, wk_in, wv_in, wo_in = sem("wq_in"), sem("wk_in"), sem("wv_in"), sem("wo_in")
        wq_hi_done, wk_hi_done, wv_hi_done, wo_hi_done = [sem(f"w{c}_hi_done") for c in "qkvo"]
        wq_lo_done, wk_lo_done, wv_lo_done, wo_lo_done = [sem(f"w{c}_lo_done") for c in "qkvo"]
        qk_bias_in, v_bias_in = sem("qk_bias_in"), sem("v_bias_in")
        pads_made = sem("pads_made")
        ctx_hi_done, ctx_lo_done = sem("ctx_hi_done"), sem("ctx_lo_done")
        zeros_made = sem("zeros_made")
        pos_order, onehot_ready, onehot_used = sem("pos_order"), sem("onehot_ready"), sem("onehot_used")
        tables_out, mask_done = sem("tables_out"), sem("mask_done")
        var_ready, std_ready, norm_order = sem("var_ready"), sem("std_ready"), sem("norm_order")
        z_nat_ready, zt_ready, z_hi_ready, z_split = [sem(n) for n in ("z_nat_ready", "zt_ready", "z_hi_ready", "z_split")]
        bias_added = sem("bias_added")
        ffn_hg_ready, ffn_hg_out, gate_cols, gate_order = [
            sem(n) for n in ("ffn_hg_ready", "ffn_hg_out", "gate_cols", "gate_order")]
        gate_exp_in, gate_exp_out, gate_wide, gate_wide_t, hw_ready, ffn_sum, ffn_added = [
            sem(n) for n in ("gate_exp_in", "gate_exp_out", "gate_wide", "gate_wide_t", "hw_ready", "ffn_sum", "ffn_added")]
        sq_done, ms_ready, rms_root = sem("sq_done"), sem("ms_ready"), sem("rms_root")
        mix_ready, mix_out, mix_cols, mix_order = [sem(n) for n in ("mix_ready", "mix_out", "mix_cols", "mix_order")]
        pp_exp_in, pp_exp_out, pp_ready, gate_scalar = [
            sem(n) for n in ("pp_exp_in", "pp_exp_out", "pp_ready", "gate_scalar")]
        sink_order, sink_to_act, sink_from_act = sem("sink_order"), sem("sink_to_act"), sem("sink_from_act")
        pre_terms, pre_sum, pre_t_ready, pre_t_out, y_ready, y_out, y_terms, y_added = [
            sem(n) for n in ("pre_terms", "pre_sum", "pre_t_ready", "pre_t_out", "y_ready", "y_out", "y_terms", "y_added")]
        mixed, out_done = sem("mixed"), sem("out_done")

        att = [{n: sem(f"{n}{layer}") for n in (
            "scores_ready",
            "masked",
            "row_max",
            "shifted",
            "exp_done",
            "row_sum",
            "row_inv",
            "probs_ready",
            "pt_ready",
            "pt_out_act",
            "pt_out_dve",
            "vt_ready",
            "vt_out",
            "vtr_ready",
            "v_out",
            "qk_ready",
            "qk_read",
            "qk_out",
            "pv_ready",
            "o_hi_ready",
            "o_split",
            "op_ready",
            "o_added",
        )} for layer in range(2)]

        def layer_of(a):
            return 1 if a is att[1] else 0

        def bank(s, j):
            return ring[:, (15 * (s % 2) + j) % RING, :]

        def tok(t):
            return slice(t * P, (t + 1) * P)

        def half(h):
            return slice(h * HALF, (h + 1) * HALF)

        def qk_done(a):
            return a["qk_out"] if layer_of(a) else a["qk_read"]

        def probs_t_of(heads, second):
            rows = slice(S * second, S * second + S)
            return probs_t[rows, :, second, heads * P:(heads + 1) * P]

        q_by_seq = q[:].rearrange("p a n -> p (a n)").rearrange("p (b h s) -> p b h s", b=HB, h=GH)

        def by_seq(ap):
            return ap.rearrange("p (b s) -> p b s", s=S)

        def o_view(o, b):
            return o[:, :, tok(b)].rearrange("p h (b q) -> p b h q", b=2)

        z_nat_of = [q, rot, q, rot, q, wo_raw, wq_raw, wo_raw]
        Z, T, K = (rot[:, 2, i * P:(i + 1) * P].rearrange("p (t i j) -> p t i j", i=STREAMS, j=STREAMS) for i in range(3))
        lse = rot[:, 3, 0:2 * TILES * STREAMS].rearrange("p (a t n) -> p a t n", a=2, n=STREAMS)
        fac = rot[:, 3, 64:64 + 2 * TILES * STREAMS].rearrange("p (a t n) -> p a t n", a=2, n=STREAMS)
        red = rot[:, 3, 128:128 + 2 * TILES * STREAMS].rearrange("p (a t n) -> p a t n", a=2, n=STREAMS)

        def halves(ap, h):
            return ap[:, h * HT:(h + 1) * HT]

        def over_rows(ap):
            return ap.unsqueeze(2).broadcast_to([P, HT, STREAMS, STREAMS])

        def over_cols(ap):
            return ap.unsqueeze(3).broadcast_to([P, HT, STREAMS, STREAMS])

        def turned(ap):
            return ap.rearrange("p t i j -> p t j i")

        block = ctx.enter_context(nc.Block())

        @block.sync
        def _(sp):
            wq_of = [w.rearrange("(c p) n -> p c n", p=P) for w in (wq0, wq1)]
            wk_of = [w.rearrange("(c p) n -> p c n", p=P) for w in (wkv0[:, 0:GROUPS * DH], wk1)]
            wv_of = [w.rearrange("(c p) n -> p c n", p=P) for w in (wkv0[:, GROUPS * DH:], wv1)]
            wo_of = [w.rearrange("(g h p) n -> p g h n", p=P, h=GH) for w in (wo0, wo1)]
            x_of = x_in_ap.rearrange("(t p) n -> p t n", p=P)
            out_of = out.rearrange("(t p) n -> p t n", p=P)
            ctx_of = ctx_t.rearrange("(c p) n -> p c n", p=P)

            def load_qkv(layer, g, split_sets):
                for raw, src, width, arrived, split in (
                        (wq_raw, wq_of[layer], D, wq_in, wq_lo_done),
                        (wk_raw, wk_of[layer], DH, wk_in, wk_lo_done),
                        (wv_raw, wv_of[layer], DH, wv_in, wv_lo_done)):
                    if split_sets is not None:
                        sp.wait_ge(split, split_sets)
                    sp.dma_start(raw[:], src[:, :, bass.ds(g * width, width)]).then_inc(arrived, 16)

            def load_qk_bias(g):
                sp.dma_start(qk_bias[:], bqkv0[:, bass.ds(g * (GH + 2), GH + 1)]).then_inc(qk_bias_in, 16)

            def load_v_bias(g):
                sp.dma_start(v_bias[:], bqkv0[:, bass.ds(g * (GH + 2) + GH, 2)]).then_inc(v_bias_in, 16)

            def load_wo(layer, g):
                sp.dma_start(wo_raw[:], wo_of[layer][:, bass.ds(g, 1), :, :].rearrange("p a h n -> p (a h) n")).then_inc(wo_in, 16)

            sp.dma_start(x[:, 0:HT, :], x_of[:, 0:HT, :]).then_inc(x_in[0], 16)
            sp.dma_start(probs_t[:].rearrange("p a b n -> p a (b n)"), ctx_of[:, :, half(0)]).then_inc(ctx_in[0], 16)
            load_qkv(0, 0, None)
            sp.dma_start(wo_raw[:], ctx_of[:, :, half(1)]).then_inc(ctx_in[1], 16)
            sp.dma_start(x[:, HT:, :], x_of[:, HT:, :]).then_inc(x_in[1], 16)
            load_qk_bias(0)
            load_v_bias(0)
            sp.wait_ge(ctx_lo_done, 2)
            load_wo(0, 0)
            with sp.Fori(1, GROUPS) as g:
                load_qkv(0, g, g)
                sp.wait_ge(att[0]["qk_read"], g * 10)
                load_qk_bias(g)
                sp.wait_ge(wo_lo_done, g)
                load_wo(0, g)
                sp.wait_ge(att[0]["vt_out"], g * 2)
                load_v_bias(g)
            sp.wait_ge(wq_lo_done, GROUPS)
            sp.dma_start(wq_raw[:], wbase_t.rearrange("(c p) n -> p c n", p=P)).then_inc(wq_in, 16)
            sp.wait_ge(wk_lo_done, GROUPS)
            sp.dma_start(wk_raw[:], a_t.rearrange("(c p) n -> p c n", p=P)).then_inc(wk_in, 16)
            sp.wait_ge(pads_made, 1)
            sp.dma_start(wv_raw[:, :, 0:EXPERTS + 1], gates_t.rearrange("(c p) n -> p c n", p=P)).then_inc(wv_in, 16)
            sp.wait_ge(wo_lo_done, GROUPS)
            sp.dma_start(wo_raw[:, 0, :], b_mat).then_inc(wo_in, 16)
            sp.wait_ge(bias_added, TILES)
            sp.dma_start(bias_row[:], bbase.partition_broadcast(P)).then_inc(row_in, 16)
            load_qkv(1, 0, L1_SET)
            sp.wait_ge(zt_ready, HT * 6)
            load_wo(1, 0)
            with sp.Fori(1, GROUPS) as g:
                load_qkv(1, g, g + L1_SET)
                sp.wait_ge(wo_lo_done, g + GROUPS)
                load_wo(1, g)
            sp.wait_ge(wk_lo_done, L1_SET + GROUPS)
            sp.dma_start(wk_raw[:, 0, :], w_branch).then_inc(wk_in, 16)
            sp.wait_ge(pads_made, 2)
            sp.dma_start(wv_raw[:, :, 0:24], mix_t.rearrange("(c p) n -> p c n", p=P)).then_inc(wv_in, 16)
            for t in range(TILES):
                sp.wait_ge(mixed, 16 * (t + 1))
                sp.dma_start(out_of[:, t, :], x[:, t, :]).then_inc(out_done, 16)
            sp.wait_ge(out_done, 16 * TILES)

        @block.tensor
        def _(pe):
            def split_product(dst, hi_a, lo_a, hi_b, lo_b, stop=True):
                n = len(hi_a)
                for c in range(n):
                    pe.matmul(dst, hi_a[c], hi_b[c], start=(c == 0), stop=False)
                    pe.matmul(dst, hi_a[c], lo_b[c], start=False, stop=False)
                    last = pe.matmul(dst, lo_a[c], hi_b[c], start=False, stop=stop and c == n - 1)
                return last

            def chunks(w, cols=slice(0, DH)):
                return [w[:, c, cols] for c in range(w.shape[1])]

            def norm_turn(m):
                for t in range(HT):
                    pe.wait_ge(z_nat_ready, HT * m + t + 1)
                    if HT * m + t >= 2:
                        pe.wait_ge(z_split, HT * m + t - 1)
                    dst = scores[:, t % 2, :]
                    for c in range(KC):
                        last = pe.transpose(dst[:, tok(c)], z_nat_of[m][:, t, tok(c)], ident[:])
                    last.then_inc(zt_ready, 1)

            def project_qk(a, s, h, dst_of, new_set=None, previous=None):
                if new_set is not None:
                    pe.wait_ge(wq_hi_done, new_set + 1)
                    pe.wait_ge(wq_lo_done, new_set + 1)
                for i in range(GH):
                    if previous is not None and i >= 1:
                        pe.wait_ge(a["o_split"], previous + i)
                    split_product(dst_of(1 + i), chunks(wq_hi, tok(i)), chunks(wq_lo, tok(i)),
                                  chunks(z_hi, half(h)), chunks(z_lo, half(h))).then_inc(a["qk_ready"], 1)
                if new_set is not None:
                    pe.wait_ge(wk_hi_done, new_set + 1)
                    pe.wait_ge(wk_lo_done, new_set + 1)
                    pe.wait_ge(ctx_lo_done, 1)
                if previous is not None:
                    pe.wait_ge(a["o_split"], previous + GH)
                split_product(dst_of(1 + GH), chunks(wk_hi), chunks(wk_lo),
                              chunks(ctx_hi, half(h)), chunks(ctx_lo, half(h))).then_inc(a["qk_ready"], 1)

            def project_out(a, s, dst_of):
                for i in range(HT):
                    split_product(dst_of(7 + i), chunks(o_hi, tok(i)), chunks(o_lo, tok(i)),
                                  chunks(wo_hi, slice(0, D)), chunks(wo_lo, slice(0, D))).then_inc(a["op_ready"], 1)

            def step(a, g, h, first=False, last=False):
                s = g * 2 + h
                n = g + L1_SET * layer_of(a)
                pe.wait_ge(qk_done(a), s * 5 + 5)
                if first:
                    pe.wait_ge(z_split, HT * (4 * layer_of(a) + 2))
                else:
                    pe.wait_ge(a["pt_out_act"], s * 2)
                    pe.wait_ge(a["pt_out_dve"], s * 2)
                for hp in range(2):
                    for b in range(HB):
                        width = 2 * S if b < HB - 1 else S
                        mm = pe.matmul(scores[:, hp, b * S:b * S + width],
                                       q_by_seq[:, b, 2 * hp:2 * hp + 2, :].rearrange("p h s -> p (h s)"),
                                       k[:, b * S:b * S + width], start=True, stop=True)
                    mm.then_inc(a["scores_ready"], 1)
                if h == 0:
                    pe.wait_ge(wv_hi_done, n + 1)
                    pe.wait_ge(wv_lo_done, n + 1)
                if not first and not (isinstance(s, int) and s == 1):
                    pe.wait_ge(a["o_added"], s * 4 - 4)
                split_product(bank(h, 0), chunks(wv_hi), chunks(wv_lo),
                              chunks(ctx_hi, half(h)), chunks(ctx_lo, half(h))).then_inc(a["vt_ready"], 1)
                if not last:
                    project_qk(a, s, 1 - h, lambda j: bank(h, j), new_set=(n + 1 if h else None),
                               previous=(None if first else s * 4 - 4))
                for hp in range(2):
                    pe.wait_ge(a["probs_ready"], s * 2 + hp + 1)
                    for b in range(PAIRS):
                        mm = pe.transpose(scores[:, hp, tok(b)],
                                          probs[:, hp, 2 * b:2 * b + 2, :].rearrange("p b k -> p (b k)"), ident[:])
                    mm.then_inc(a["pt_ready"], 1)
                pe.wait_ge(a["vt_out"], s + 1)
                for b in range(PAIRS):
                    mm = pe.transpose(bank(h, 6)[:, tok(b)], v_t[:, tok(b)], ident[:])
                mm.then_inc(a["vtr_ready"], 1)
                if not first:
                    pe.wait_ge(a["o_split"], s * 4)
                    if h:
                        n_wo = g + GROUPS * layer_of(a)
                        pe.wait_ge(wo_hi_done, n_wo + 1)
                        pe.wait_ge(wo_lo_done, n_wo + 1)
                    if not last:
                        pe.wait_ge(a["qk_read"], s * 5 + 5 + GH)
                    project_out(a, s, lambda j: bank(h, j))
                if not last:
                    pe.wait_ge(a["qk_read"], s * 5 + 10)
                pe.wait_ge(a["pt_out_act"], s * 2 + 2)
                pe.wait_ge(a["pt_out_dve"], s * 2 + 2)
                pe.wait_ge(a["v_out"], s + 1)
                for b in range(PAIRS):
                    if b >= 2 and not first:
                        pe.wait_ge(a["o_added"], s * 4 - 4 + b - 1)
                    pe.matmul(bank(h, 11 + b), v[:, b, :], probs_t[:, b, :, :], start=True, stop=True)\
                        .then_inc(a["pv_ready"], 1)

            def attention(layer):
                a = att[layer]
                norm_turn(4 * layer)
                pe.wait_ge(z_split, HT * (4 * layer + 1))
                project_qk(a, -1, 0, lambda j: bank(1, j), new_set=L1_SET * layer)
                norm_turn(4 * layer + 1)
                pe.wait_ge(ctx_lo_done, 2)
                pe.wait_ge(zeros_made, 1)
                step(a, 0, 0, first=True)
                step(a, 0, 1)
                with pe.Fori(1, GROUPS - 1) as g:
                    step(a, g, 0)
                    step(a, g, 1)
                step(a, GROUPS - 1, 0)
                step(a, GROUPS - 1, 1, last=True)
                last = 2 * GROUPS
                pe.wait_ge(a["o_split"], 4 * last)
                pe.wait_ge(a["o_added"], 4 * last - 4)
                project_out(a, last, lambda j: bank(0, j))

            pe.wait_ge(tables_in, 16)
            for c in range(KC):
                pe.wait_ge(onehot_ready, c + 1)
                for i in range(4):
                    table = probs[:, :, :, :].rearrange("p a b k -> p (a b k)")[:, c * 256 + (i // 2) * P:c * 256 + (i // 2 + 1) * P]
                    mm = pe.matmul(ring[:, 2 + i, :], table, rot[:, 2 * (c % 2) + i % 2, :],
                                   start=(c == 0), stop=(c == KC - 1))
                mm.then_inc(onehot_used, 1)
            pe.wait_ge(ident_made, 2)
            pe.wait_ge(tables_out, 4)
            attention(0)

            norm_turn(2)
            pe.wait_ge(att[0]["o_added"], 8 * GROUPS)
            for h in range(2):
                pe.wait_ge(z_split, HT * (3 + h))
                if h == 0:
                    pe.wait_ge(wk_lo_done, FFN0_SET + 1)
                    pe.wait_ge(wv_lo_done, FFN0_SET + 1)
                else:
                    pe.wait_ge(hw_ready, 1)
                    pe.wait_ge(gate_wide, 1)
                split_product(ring[:, 2, :], chunks(wk_hi), chunks(wk_lo), chunks(z_hi, half(h)), chunks(z_lo, half(h)))\
                    .then_inc(ffn_hg_ready, 1)
                split_product(ring[:, 3, :], chunks(wv_hi), chunks(wv_lo), chunks(z_hi, half(h)), chunks(z_lo, half(h)))\
                    .then_inc(ffn_hg_ready, 1)
                base_bank = [ring[:, b, :] for b in (4, 5, 0, 1)]
                pe.wait_ge(wq_lo_done, FFN0_SET + 1)
                for t in range(HT):
                    if h:
                        pe.wait_ge(ffn_added, t + 1)
                    split_product(base_bank[t], chunks(z_hi, tok(HT * h + t)), chunks(z_lo, tok(HT * h + t)),
                                  chunks(wq_hi, slice(0, D)), chunks(wq_lo, slice(0, D)), stop=False)
                pe.wait_ge(ffn_hg_out, 2 * h + 2)
                for t in range(HT):
                    mm = pe.transpose(ring[:, 3, tok(t)], v_t[:, tok(t)], ident[:])
                mm.then_inc(gate_cols, 1)
                if h == 0:
                    norm_turn(3)
                pe.wait_ge(gate_wide, h + 1)
                for t in range(HT):
                    mm = pe.transpose(ring[:, 2, tok(t)], v[:, t, :], ident[:])
                mm.then_inc(gate_wide_t, 1)
                pe.wait_ge(hw_ready, h + 1)
                pe.wait_ge(wo_in, 16 * (FFN0_SET + 1))
                for t in range(HT):
                    pe.matmul(base_bank[t], rot[:, 0, tok(t)], wo_raw[:, 0, :], start=False, stop=True)\
                        .then_inc(ffn_sum, 1)

            pe.wait_ge(ffn_added, TILES)
            attention(1)

            for h in range(2):
                norm_turn(6 + h)
                pe.wait_ge(z_split, HT * (7 + h))
                if h == 0:
                    pe.wait_ge(wv_lo_done, L1_SET + GROUPS + 1)
                    pe.wait_ge(att[1]["o_added"], 8 * GROUPS)
                split_product(ring[:, 2 + h, :], chunks(wv_hi), chunks(wv_lo), chunks(z_hi, half(h)), chunks(z_lo, half(h)))\
                    .then_inc(mix_ready, 1)
            for h in range(2):
                pe.wait_ge(mix_out, h + 1)
                for t in range(HT):
                    mm = pe.transpose(ring[:, 4 + h, tok(t)], (k, v_t)[h][:, tok(t)], ident[:])
                mm.then_inc(mix_cols, 1)
            for h in range(2):
                pe.wait_ge(pre_sum, 2 * h + 2)
                for t in range(HT):
                    mm = pe.transpose(ring[:, 2 + h, tok(t)], rot[:, h, tok(t)], ident[:])
                mm.then_inc(pre_t_ready, 1)
                pe.wait_ge(pre_t_out, h + 1)
                pe.wait_ge(wk_in, 16 * (L1_SET + GROUPS + 1))
                for t in range(HT):
                    mm = pe.matmul(ring[:, h, tok(t)], cos[:, tok(HT * h + t)], wk_raw[:, 0, :], start=True, stop=True)
                mm.then_inc(y_ready, 1)

        @block.scalar
        def _(act):
            def norm_root(m):
                act.wait_ge(var_ready, m + 1)
                act.activation(rstd[:], rstd[:], ACT.Sqrt).then_inc(std_ready, 1)

            def norm_hi(m):
                for t in range(HT):
                    act.wait_ge(zt_ready, HT * m + t + 1)
                    act.activation(z_hi[:, :, tok(HT * (m % 2) + t)],
                                   scores[:, t % 2, :].rearrange("p (c n) -> p c n", c=KC), ACT.Copy)\
                        .then_inc(z_hi_ready, 1)

            def split_hi(raw, hi, arrived, loads, done):
                act.wait_ge(arrived, loads * 16)
                act.activation(hi[:], raw[:], ACT.Copy).then_inc(done, 1)

            def copy_qk(a, g, idx, parity):
                act.wait_ge(qk_bias_in, g * 16 + 16)
                for i in range(5):
                    act.wait_ge(a["qk_ready"], idx + i + 1)
                    src = bank(parity, 1 + i)
                    if i < GH:
                        act.activation(q_by_seq[:, :, i, :], by_seq(src), ACT.Identity, bias=qk_bias[:, i:i + 1])\
                            .then_inc(a["qk_read"], 1)
                    else:
                        act.activation(k[:], src, ACT.Identity, bias=qk_bias[:, GH:GH + 1]).then_inc(a["qk_read"], 1)

            def step(a, g, h, last=False):
                s = g * 2 + h
                n = g + L1_SET * layer_of(a)
                n_wo = g + GROUPS * layer_of(a)
                for hp in range(2):
                    act.wait_ge(a["shifted"], s * 2 + hp + 1)
                    act.activation(probs[:, hp], probs[:, hp], ACT.Exp, scale=SCALE).then_inc(a["exp_done"], 1)
                act.wait_ge(a["vt_ready"], s + 1)
                if layer_of(a):
                    act.activation(v_t[:], bank(h, 0), ACT.Copy).then_inc(a["vt_out"], 1)
                else:
                    act.wait_ge(v_bias_in, g * 16 + 16)
                    act.activation(v_t[:], bank(h, 0), ACT.Identity, bias=v_bias[:, 1:2]).then_inc(a["vt_out"], 1)
                if not layer_of(a) and not last:
                    copy_qk(a, g + h, s * 5 + 5, h)
                act.wait_ge(a["pt_ready"], s * 2 + 1)
                for second in range(2):
                    act.activation(probs_t_of(0, second),
                                   scores[S * second:S * second + S, 0, :].rearrange("p (b n) -> p b n", b=PAIRS),
                                   ACT.Copy).then_inc(a["pt_out_act"], 1)
                act.wait_ge(a["vtr_ready"], s + 1)
                act.activation(v[:], bank(h, 6).rearrange("p (b n) -> p b n", b=PAIRS), ACT.Copy).then_inc(a["v_out"], 1)
                if not last:
                    if h == 0:
                        if not (isinstance(g, int) and g == GROUPS - 1):
                            act.wait_ge(a["qk_ready"], s * 5 + 10)
                            split_hi(wq_raw, wq_hi, wq_in, n + 2, wq_hi_done)
                            split_hi(wk_raw, wk_hi, wk_in, n + 2, wk_hi_done)
                    else:
                        split_hi(wv_raw, wv_hi, wv_in, n + 2, wv_hi_done)
                for b in range(PAIRS):
                    act.wait_ge(a["pv_ready"], s * 4 + b + 1)
                    act.activation(o_view(o_hi, b), bank(h, 11 + b).rearrange("p (b h q) -> p b h q", b=2, h=GH), ACT.Copy)\
                        .then_inc(a["o_hi_ready"], 1)
                if h == 0:
                    split_hi(wo_raw, wo_hi, wo_in, n_wo + 1 + layer_of(a), wo_hi_done)

            def attention(layer):
                a = att[layer]
                if layer:
                    norm_root(4)
                    split_hi(wq_raw, wq_hi, wq_in, L1_SET + 1, wq_hi_done)
                    split_hi(wk_raw, wk_hi, wk_in, L1_SET + 1, wk_hi_done)
                    split_hi(wv_raw, wv_hi, wv_in, L1_SET + 1, wv_hi_done)
                    norm_hi(4)
                    norm_root(5)
                else:
                    norm_hi(0)
                    act.wait_ge(ctx_in[1], 16)
                    act.activation(ctx_hi[:, :, half(1)], wo_raw[:], ACT.Copy).then_inc(ctx_hi_done, 1)
                    copy_qk(a, 0, 0, 1)
                    norm_root(1)
                norm_hi(4 * layer + 1)
                step(a, 0, 0)
                step(a, 0, 1)
                with act.Fori(1, GROUPS - 1) as g:
                    step(a, g, 0)
                    step(a, g, 1)
                step(a, GROUPS - 1, 0)
                step(a, GROUPS - 1, 1, last=True)

            act.dma_start(cos[:].bitcast(I32), pos.partition_broadcast(P)).then_inc(pos_in, 16)
            act.dma_start(probs[:].rearrange("p a b k -> p (a b k)").rearrange("p (c n) -> p c n", c=KC),
                          tables.rearrange("(c p) n -> p c n", p=P)).then_inc(tables_in, 16)
            act.dma_start(scalars[:, 0:1], b_thr.partition_broadcast(P)).then_inc(small_in, 16)
            act.dma_start(scalars[:, 1:2], gate.partition_broadcast(P)).then_inc(small_in, 16)
            act.dma_start(mix_base_sb[:], mix_base.partition_broadcast(P)).then_inc(small_in, 16)
            act.dma_start(bias_row[:], bo0.partition_broadcast(P)).then_inc(row_in, 16)
            act.wait_ge(small_in, 48)
            norm_root(0)
            act.wait_ge(ctx_in[0], 16)
            act.activation(ctx_hi[:, :, half(0)], probs_t[:].rearrange("p a b n -> p a (b n)"), ACT.Copy).then_inc(ctx_hi_done, 1)
            split_hi(wq_raw, wq_hi, wq_in, 1, wq_hi_done)
            split_hi(wk_raw, wk_hi, wk_in, 1, wk_hi_done)
            split_hi(wv_raw, wv_hi, wv_in, 1, wv_hi_done)
            act.wait_ge(onehot_used, KC)
            for i in range(4):
                act.activation((cos, sin)[i // 2][:, half(i % 2)], ring[:, 2 + i, :], ACT.Copy).then_inc(tables_out, 1)
            for i in range(2):
                act.dma_start(probs[S * i:S * i + S].bitcast(I32).rearrange("p a b k -> p (a b) k"),
                              mask.rearrange("b q k -> q b k")).then_inc(mask_in, 16)
            attention(0)

            norm_root(2)
            split_hi(wq_raw, wq_hi, wq_in, FFN0_SET + 1, wq_hi_done)
            split_hi(wk_raw, wk_hi, wk_in, FFN0_SET + 1, wk_hi_done)
            split_hi(wv_raw, wv_hi, wv_in, FFN0_SET + 1, wv_hi_done)
            norm_root(3)
            norm_hi(2)
            for h in range(2):
                if h:
                    norm_hi(3)
                for i, dst in enumerate((k, v_t)):
                    act.wait_ge(ffn_hg_ready, 2 * h + i + 1)
                    act.activation(dst[:], ring[:, 2 + i, :], ACT.Copy).then_inc(ffn_hg_out, 1)
                act.wait_ge(gate_exp_in, h + 1)
                act.activation(gate_w[:], gate_w[:], ACT.Exp).then_inc(gate_exp_out, 1)

            act.wait_ge(ffn_sum, 1 + HT)
            attention(1)

            split_hi(wv_raw, wv_hi, wv_in, L1_SET + GROUPS + 1, wv_hi_done)
            norm_root(6)
            norm_root(7)
            norm_hi(6)
            norm_hi(7)
            for t in range(TILES):
                act.activation(probs[:].rearrange("p a b k -> p (a b k)")[:, (t % 2) * D:(t % 2 + 1) * D],
                               (wq_raw, wo_raw)[t // HT][:, t % HT, :], ACT.Square,
                               accum_out=rms[:, t:t + 1]).then_inc(sq_done, 1)
                if t >= 1:
                    act.wait_ge(sq_done, t)
            act.wait_ge(ms_ready, 1)
            act.activation(rms[:], rms[:], ACT.Sqrt).then_inc(rms_root, 1)
            for h in range(2):
                act.wait_ge(mix_ready, h + 1)
                act.activation((k, v_t)[h][:], ring[:, 2 + h, :], ACT.Copy).then_inc(mix_out, 1)
            act.wait_ge(pp_exp_in, 1)
            lp = logits[:, :, 16:24]
            act.activation(lp, lp, ACT.Exp).then_inc(pp_exp_out, 1)
            act.activation(scalars[:, 1:2], scalars[:, 1:2], ACT.Exp, scale=-1.0).then_inc(gate_scalar, 1)
            act.wait_ge(pp_ready, 1)

            def sinkhorn_act():
                with act.Fori(0, CYCLES) as c:
                    for stage in range(2):
                        for h in range(2):
                            act.wait_ge(sink_to_act, c * 12 + stage * 4 + h + 1)
                            act.activation(halves(K, h), halves(T, h), ACT.Exp).then_inc(sink_from_act, 1)
                        for h in range(2):
                            act.wait_ge(sink_to_act, c * 12 + stage * 4 + 2 + h + 1)
                            r = halves(red[:, 1], h)
                            act.activation(r, r, ACT.Ln).then_inc(sink_from_act, 1)
                    for h in range(2):
                        act.wait_ge(sink_to_act, c * 12 + 8 + h + 1)
                        act.activation(halves(K, h), halves(T, h), ACT.Exp).then_inc(sink_from_act, 1)
                    for h in range(2):
                        act.wait_ge(sink_to_act, c * 12 + 10 + h + 1)
                        for a in range(2):
                            f = halves(fac[:, a], h)
                            act.activation(f, f, ACT.Ln).then_inc(sink_from_act, 1)

            def branch_terms(h):
                for t in range(HT):
                    tile = HT * h + t
                    for n in range(STREAMS):
                        last = act.activation(q[:, t, tok(n)], (wq_raw, wo_raw)[h][:, t, tok(n)], ACT.Copy,
                                              scale=logits[:, tile, 16 + n:17 + n])
                last.then_inc(pre_terms, 1)

            def branch_out(h):
                for t in range(HT):
                    tile = HT * h + t
                    for n in range(STREAMS):
                        last = act.activation(o_terms[:, t, tok(n)], sin[:, tok(tile)], ACT.Copy,
                                              scale=logits[:, tile, 20 + n:21 + n])
                last.then_inc(y_terms, 1)

            o_terms = probs_t[:].rearrange("p a b n -> p a (b n)")
            for h in range(2):
                if h:
                    act.wait_ge(pre_sum, 2)
                branch_terms(h)
            for h in range(2):
                act.wait_ge(pre_t_ready, h + 1)
                act.activation(cos[:, half(h)], ring[:, 2 + h, :], ACT.Copy).then_inc(pre_t_out, 1)
                act.wait_ge(y_ready, h + 1)
                act.activation(sin[:, half(h)], ring[:, h, :], ACT.Copy).then_inc(y_out, 1)
                act.wait_ge(y_out, h + 1)
                if h:
                    act.wait_ge(y_added, 1)
                branch_out(h)
            sinkhorn_act()
            for h in range(2):
                act.wait_ge(sink_to_act, CYCLES * 12 + h + 1)
                act.activation(halves(K, h), halves(T, h), ACT.Exp).then_inc(sink_from_act, 1)

        @block.gpsimd
        def _(pool):
            def split_lo(raw, hi, lo, hi_done, sets, done):
                pool.wait_ge(hi_done, sets)
                pool.tensor_tensor(lo[:], raw[:], hi[:], ALU.subtract).then_inc(done, 1)

            def add_bias(m):
                for t in range(HT):
                    tile = HT * (m % 2) + t
                    pool.wait_ge(z_nat_ready, HT * m + t + 1)
                    pool.tensor_tensor(x[:, tile, :], x[:, tile, :], bias_row[:], ALU.add).then_inc(bias_added, 1)

            def turn_add(a, idx, parity):
                for i in range(5):
                    b = (parity + i) % 2
                    pool.wait_ge(a["qk_read"], idx + i + 1)
                    pool.tensor_tensor(q_by_seq[:, :, i, :] if i < GH else by_seq(k[:]),
                                       by_seq(rot[:, b, :]), by_seq(rot[:, 2 + b, :]), ALU.add)\
                        .then_inc(a["qk_out"], 1)

            def step(a, g, h, last=False):
                s = g * 2 + h
                n = g + L1_SET * layer_of(a)
                n_wo = g + GROUPS * layer_of(a)
                for hp in range(2):
                    pool.wait_ge(a["row_inv"], s * 2 + hp + 1)
                    pool.tensor_tensor(probs[:, hp], probs[:, hp],
                                       row_inv_sb[:, hp, :].unsqueeze(2).broadcast_to([P, HB, S]), ALU.mult)\
                        .then_inc(a["probs_ready"], 1)
                if layer_of(a) and not last:
                    turn_add(a, s * 5 + 5, 1 - h)
                if not last:
                    if h == 0:
                        if not (isinstance(g, int) and g == GROUPS - 1):
                            split_lo(wq_raw, wq_hi, wq_lo, wq_hi_done, n + 2, wq_lo_done)
                            split_lo(wk_raw, wk_hi, wk_lo, wk_hi_done, n + 2, wk_lo_done)
                    else:
                        split_lo(wv_raw, wv_hi, wv_lo, wv_hi_done, n + 2, wv_lo_done)
                if h == 0:
                    split_lo(wo_raw, wo_hi, wo_lo, wo_hi_done, n_wo + 1, wo_lo_done)

            def attention(layer):
                a = att[layer]
                if layer:
                    turn_add(a, 0, 0)
                step(a, 0, 0)
                step(a, 0, 1)
                with pool.Fori(1, GROUPS - 1) as g:
                    step(a, g, 0)
                    step(a, g, 1)
                step(a, GROUPS - 1, 0)
                step(a, GROUPS - 1, 1, last=True)

            pool.iota(pos_col[:], pattern=[[P, KC]], base=0, channel_multiplier=1,
                      allow_small_or_imprecise_dtypes=True).then_inc(ident_made, 1)
            pool.memset(ident[:], 0.0).then_inc(ident_cleared, 1)
            pool.wait_ge(ident_cleared, 1)
            pool.affine_select(out=ident[:], in_=ident[:], compare_op=ALU.not_equal, fill=1.0, base=0,
                               pattern=[[-1, P]], channel_multiplier=1).then_inc(ident_made, 1)
            split_lo(wq_raw, wq_hi, wq_lo, wq_hi_done, 1, wq_lo_done)
            split_lo(wk_raw, wk_hi, wk_lo, wk_hi_done, 1, wk_lo_done)
            split_lo(wv_raw, wv_hi, wv_lo, wv_hi_done, 1, wv_lo_done)
            pool.wait_ge(ctx_lo_done, 1)
            pool.memset(probs_t[:], 0.0).then_inc(zeros_made, 1)
            pool.wait_ge(row_in, 16)
            add_bias(0)
            add_bias(1)
            attention(0)

            pool.wait_ge(wv_lo_done, GROUPS)
            pool.memset(wv_raw[:], 0.0).then_inc(pads_made, 1)
            split_lo(wq_raw, wq_hi, wq_lo, wq_hi_done, FFN0_SET + 1, wq_lo_done)
            split_lo(wk_raw, wk_hi, wk_lo, wk_hi_done, FFN0_SET + 1, wk_lo_done)
            split_lo(wv_raw, wv_hi, wv_lo, wv_hi_done, FFN0_SET + 1, wv_lo_done)
            pool.wait_ge(row_in, 32)
            add_bias(2)
            add_bias(3)
            split_lo(wq_raw, wq_hi, wq_lo, wq_hi_done, L1_SET + 1, wq_lo_done)
            split_lo(wk_raw, wk_hi, wk_lo, wk_hi_done, L1_SET + 1, wk_lo_done)
            split_lo(wv_raw, wv_hi, wv_lo, wv_hi_done, L1_SET + 1, wv_lo_done)
            attention(1)

            pool.wait_ge(wv_lo_done, L1_SET + GROUPS)
            pool.memset(wv_raw[:], 0.0).then_inc(pads_made, 1)
            split_lo(wv_raw, wv_hi, wv_lo, wv_hi_done, L1_SET + GROUPS + 1, wv_lo_done)
            for h in range(2):
                pool.wait_ge(pre_terms, h + 1)
                pool.tensor_tensor(q[:, :, 0:2 * P], q[:, :, 0:2 * P], q[:, :, 2 * P:], ALU.add).then_inc(pre_sum, 1)
                pool.wait_ge(pre_sum, 2 * h + 1)
                pool.tensor_tensor(rot[:, h, :].rearrange("p (t n) -> p t n", n=P), q[:, :, 0:P], q[:, :, P:2 * P], ALU.add)\
                    .then_inc(pre_sum, 1)
            for h in range(2):
                pool.wait_ge(y_terms, h + 1)
                pool.tensor_tensor(x[:, h * HT:(h + 1) * HT, :], x[:, h * HT:(h + 1) * HT, :],
                                   probs_t[:].rearrange("p a b n -> p a (b n)"), ALU.add).then_inc(y_added, 1)

        @block.vector
        def _(dve):
            def norm_nat(m):
                base = (2 * HT + 1) * m
                h = m % 2
                if m:
                    dve.wait_ge(norm_order, base)
                    dve.wait_ge(z_nat_ready, HT * m)
                if m == 6:
                    dve.wait_ge(wq_lo_done, L1_SET + GROUPS)
                if m == 7:
                    dve.wait_ge(wo_lo_done, 2 * GROUPS)
                for t in range(HT):
                    if m < 2:
                        dve.wait_ge(x_in[h], 16)
                    elif m in (2, 3):
                        dve.wait_ge(att[0]["o_added"], 8 * GROUPS - 2 * HT + HT * (h + 1))
                    elif m in (4, 5):
                        dve.wait_ge(ffn_added, HT * (h + 1))
                    else:
                        dve.wait_ge(att[1]["o_added"], 8 * GROUPS - 2 * HT + HT * (h + 1))
                    dve.bn_stats(stats[:, t, :], x[:, HT * h + t, :]).then_inc(norm_order, 1)
                for t in range(HT):
                    dve.wait_ge(norm_order, base + t + 1)
                    dve.bn_aggr(mean_var[:, t, :], stats[:, t, :]).then_inc(norm_order, 1)
                dve.wait_ge(norm_order, base + 2 * HT)
                dve.tensor_scalar(rstd[:], mean_var[:, :, 1], LN_EPS, None, ALU.add).then_inc(var_ready, 1)
                dve.wait_ge(std_ready, m + 1)
                dve.reciprocal(rstd[:], rstd[:]).then_inc(norm_order, 1)
                dve.wait_ge(norm_order, base + 2 * HT + 1)
                for t in range(HT):
                    ins = dve.tensor_scalar(z_nat_of[m][:, t, :], x[:, HT * h + t, :], mean_var[:, t, 0:1], rstd[:, t:t + 1],
                                            ALU.subtract, ALU.mult)
                    ins.then_inc(z_nat_ready, 1)

            def norm_lo(m):
                for t in range(HT):
                    dve.wait_ge(z_hi_ready, HT * m + t + 1)
                    cols = tok(HT * (m % 2) + t)
                    dve.tensor_tensor(z_lo[:, :, cols], scores[:, t % 2, :].rearrange("p (c n) -> p c n", c=KC),
                                      z_hi[:, :, cols], ALU.subtract).then_inc(z_split, 1)

            def turn_qk(a, idx, parity_bank, parity, h):
                for i in range(5):
                    b = (parity + i) % 2
                    src = bank(parity_bank, 1 + i)
                    dve.wait_ge(a["qk_ready"], idx + i + 1)
                    if not (isinstance(idx, int) and idx + i < 2):
                        dve.wait_ge(a["qk_out"], idx + i - 1)
                    dve.tensor_tensor(rot[:, b, :], src, cos[:, half(h)], ALU.mult)
                    dve.tensor_tensor(rot[0:64, 2 + b, :], src[64:128, :], sin[64:128, half(h)], ALU.mult)
                    dve.tensor_tensor(rot[64:128, 2 + b, :], src[0:64, :], sin[0:64, half(h)], ALU.mult)\
                        .then_inc(a["qk_read"], 1)

            def add_out(a, s, h_prev):
                for i in range(HT):
                    tile = HT * h_prev + i
                    dve.wait_ge(a["op_ready"], s * 4 - 4 + i + 1)
                    dve.tensor_tensor(x[:, tile, :], bank(1 - h_prev, 7 + i), x[:, tile, :], ALU.add).then_inc(a["o_added"], 1)

            def step(a, g, h, first=False, last=False):
                s = g * 2 + h
                for hp in range(2):
                    dve.wait_ge(a["scores_ready"], s * 2 + hp + 1)
                    if layer_of(a):
                        dve.memset(row_max_sb[:, hp, :], 0.0)
                        dve.copy_predicated(scores[:, hp, :], masked_out[:, h * HB:(h + 1) * HB, :].rearrange("p b k -> p (b k)"),
                                            masked_value[:].broadcast_to([P, HB * S])).then_inc(a["masked"], 1)
                        dve.wait_ge(a["masked"], s * 2 + hp + 1)
                    dve.tensor_reduce(row_max_sb[:, hp, :], scores[:, hp, :].rearrange("p (b k) -> p b k", k=S), AX.X, ALU.max)\
                        .then_inc(a["row_max"], 1)
                for hp in range(2):
                    dve.wait_ge(a["row_max"], s * 2 + hp + 1)
                    if not first:
                        dve.wait_ge(a["pt_ready"], s * 2)
                    dve.tensor_tensor(probs[:, hp], scores[:, hp, :].rearrange("p (b k) -> p b k", k=S),
                                      row_max_sb[:, hp, :].unsqueeze(2).broadcast_to([P, HB, S]), ALU.subtract)\
                        .then_inc(a["shifted"], 1)
                for hp in range(2):
                    dve.wait_ge(a["exp_done"], s * 2 + hp + 1)
                    dve.tensor_reduce(row_sum_sb[:, hp, :], probs[:, hp], AX.X, ALU.add).then_inc(a["row_sum"], 1)
                for hp in range(2):
                    dve.wait_ge(a["row_sum"], s * 2 + hp + 1)
                    if not first:
                        dve.wait_ge(a["probs_ready"], s * 2)
                    dve.reciprocal(row_inv_sb[:, hp, :], row_sum_sb[:, hp, :]).then_inc(a["row_inv"], 1)
                if layer_of(a) and not last:
                    turn_qk(a, s * 5 + 5, h, 1 - h, 1 - h)
                dve.wait_ge(a["pt_ready"], s * 2 + 2)
                for second in range(2):
                    dve.tensor_copy(probs_t_of(1, second),
                                    scores[S * second:S * second + S, 1, :].rearrange("p (b n) -> p b n", b=PAIRS))\
                        .then_inc(a["pt_out_dve"], 1)
                if not first:
                    add_out(a, s, 1 - h)
                for b in range(PAIRS):
                    dve.wait_ge(a["o_hi_ready"], s * 4 + b + 1)
                    dve.tensor_tensor(o_view(o_lo, b), bank(h, 11 + b).rearrange("p (b h q) -> p b h q", b=2, h=GH),
                                      o_view(o_hi, b), ALU.subtract).then_inc(a["o_split"], 1)

            def attention(layer):
                a = att[layer]
                norm_nat(4 * layer)
                if not layer:
                    for c in (2, 3):
                        one_hot(c)
                    dve.wait_ge(mask_in, 32)
                    dve.tensor_scalar(masked_out[:], probs[:].bitcast(I32).rearrange("p a b k -> p (a b) k"), 0, None,
                                      ALU.is_equal).then_inc(mask_done, 1)
                norm_lo(4 * layer)
                if not layer:
                    split_ctx_lo(0)
                    split_ctx_lo(1)
                norm_nat(4 * layer + 1)
                if layer:
                    turn_qk(a, 0, 1, 0, 0)
                norm_lo(4 * layer + 1)
                dve.wait_ge(mask_done, 2)
                step(a, 0, 0, first=True)
                if not layer:
                    dve.wait_ge(bias_added, TILES)
                step(a, 0, 1)
                with dve.Fori(1, GROUPS - 1) as g:
                    step(a, g, 0)
                    step(a, g, 1)
                step(a, GROUPS - 1, 0)
                step(a, GROUPS - 1, 1, last=True)
                norm_nat(4 * layer + 2)
                add_out(a, 2 * GROUPS, 1)
                norm_nat(4 * layer + 3)
                norm_lo(4 * layer + 2)

            def one_hot(c):
                if c >= 2:
                    dve.wait_ge(onehot_used, c - 1)
                dve.tensor_scalar(rot[:, 2 * (c % 2):2 * (c % 2) + 2, :].rearrange("p a n -> p (a n)"), sin[:], pos_col[:, c:c + 1],
                                  None, ALU.is_equal).then_inc(onehot_ready, 1)

            def split_ctx_lo(h):
                raw = wo_raw[:] if h else probs_t[:].rearrange("p a b n -> p a (b n)")
                dve.wait_ge(ctx_hi_done, h + 1)
                dve.tensor_tensor(ctx_lo[:, :, half(h)], raw, ctx_hi[:, :, half(h)], ALU.subtract).then_inc(ctx_lo_done, 1)

            dve.memset(masked_value[:], MASKED).then_inc(mask_done, 1)
            dve.wait_ge(pos_in, 16)
            dve.tensor_copy(sin[:], cos[:].bitcast(I32)).then_inc(pos_order, 1)
            dve.wait_ge(pos_order, 1)
            dve.tensor_scalar(cos[:], sin[:], 0.0, float(MAX_POS), ALU.is_lt, ALU.mult).then_inc(pos_order, 1)
            dve.wait_ge(pos_order, 2)
            dve.tensor_tensor(sin[:], sin[:], cos[:], ALU.add).then_inc(pos_order, 1)
            dve.wait_ge(pos_order, 3)
            dve.tensor_scalar(sin[:], sin[:], 0.0, float(MAX_POS - 1), ALU.max, ALU.min).then_inc(pos_order, 1)
            dve.wait_ge(pos_order, 4)
            dve.wait_ge(ident_made, 1)
            one_hot(0)
            one_hot(1)
            attention(0)

            def gating(h):
                wide = v[:].rearrange("p t (e r) -> p t e r", r=RANK)
                w, wt = gate_w[:, :, 0:EXPERTS], gate_w[:, :, EXPERTS:EXPERTS + 1]
                top, thr, total = (gate_s[:, :, i:i + 1] for i in (0, 1, 2))

                def over_experts(ap):
                    return ap.broadcast_to([P, HT, EXPERTS])

                n = 14 * h
                dve.wait_ge(gate_cols, h + 1)
                dve.tensor_copy(gate_w[:], ring[:, 3, :].rearrange("p (t n) -> p t n", n=P)[:, :, 0:EXPERTS + 1]).then_inc(gate_order, 1)
                dve.wait_ge(gate_order, n + 1)
                dve.tensor_reduce(top, w, AX.X, ALU.max).then_inc(gate_order, 1)
                dve.wait_ge(gate_order, n + 2)
                dve.tensor_tensor(w, w, over_experts(top), ALU.subtract).then_inc(gate_order, 1)
                dve.tensor_scalar(wt, wt, scalars[:, 0:1], -1.0, ALU.add, ALU.mult).then_inc(gate_order, 1)
                dve.wait_ge(gate_order, n + 4)
                dve.tensor_copy(top, top).then_inc(gate_exp_in, 1)
                dve.wait_ge(gate_exp_out, h + 1)
                dve.tensor_reduce(total, w, AX.X, ALU.add).then_inc(gate_order, 1)
                dve.tensor_scalar(thr, wt, 1.0, None, ALU.add).then_inc(gate_order, 1)
                dve.wait_ge(gate_order, n + 6)
                dve.reciprocal(gate_s[:, :, 1:3], gate_s[:, :, 1:3]).then_inc(gate_order, 1)
                dve.wait_ge(gate_order, n + 7)
                dve.tensor_tensor(w, w, over_experts(total), ALU.mult).then_inc(gate_order, 1)
                dve.wait_ge(gate_order, n + 8)
                dve.scalar_tensor_tensor(out=w, in0=over_experts(thr), scalar=-0.125, in1=w, op0=ALU.mult, op1=ALU.add)\
                    .then_inc(gate_order, 1)
                dve.wait_ge(gate_order, n + 9)
                dve.tensor_scalar(w, w, 0.0, None, ALU.max).then_inc(gate_order, 1)
                dve.wait_ge(gate_order, n + 10)
                dve.tensor_reduce(total, w, AX.X, ALU.add).then_inc(gate_order, 1)
                dve.wait_ge(gate_order, n + 11)
                dve.scalar_tensor_tensor(out=total, in0=total, scalar=0.0, in1=total, op0=ALU.is_equal, op1=ALU.add)\
                    .then_inc(gate_order, 1)
                dve.wait_ge(gate_order, n + 12)
                dve.reciprocal(total, total).then_inc(gate_order, 1)
                dve.wait_ge(gate_order, n + 13)
                dve.scalar_tensor_tensor(out=w, in0=w, scalar=2.0, in1=over_experts(total), op0=ALU.mult, op1=ALU.mult)\
                    .then_inc(gate_order, 1)
                dve.wait_ge(gate_order, n + 14)
                dve.tensor_copy(wide, w.unsqueeze(3).broadcast_to([P, HT, EXPERTS, RANK])).then_inc(gate_wide, 1)

            dve.wait_ge(small_in, 48)
            for h in range(2):
                gating(h)
                if h == 0:
                    norm_lo(3)
                dve.wait_ge(gate_wide_t, h + 1)
                if h:
                    dve.wait_ge(ffn_sum, HT)
                dve.tensor_tensor(rot[:, 0, :], ring[:, 2, :], k[:], ALU.mult).then_inc(hw_ready, 1)
                for t in range(HT):
                    tile = HT * h + t
                    dve.wait_ge(ffn_sum, tile + 1)
                    dve.wait_ge(bias_added, TILES + tile + 1)
                    dve.tensor_tensor(x[:, tile, :], ring[:, (4, 5, 0, 1)[t], :], x[:, tile, :], ALU.add).then_inc(ffn_added, 1)

            attention(1)

            norm_lo(7)
            dve.wait_ge(sq_done, TILES)
            dve.tensor_scalar(rms[:], rms[:], 1.0 / D, RMS_EPS, ALU.mult, ALU.add).then_inc(ms_ready, 1)
            dve.wait_ge(rms_root, 1)
            dve.reciprocal(rms[:], rms[:]).then_inc(mix_order, 1)
            dve.wait_ge(mix_order, 1)
            for h in range(2):
                dve.wait_ge(mix_cols, h + 1)
                dve.tensor_tensor(halves(logits, h), ring[:, 4 + h, :].rearrange("p (t n) -> p t n", n=P)[:, :, 0:24],
                                  halves(rms, h).unsqueeze(2).broadcast_to([P, HT, 24]), ALU.mult).then_inc(mix_order, 1)
            dve.wait_ge(mix_order, 3)
            dve.tensor_tensor(logits[:], logits[:], mix_base_sb[:].unsqueeze(1).broadcast_to([P, TILES, 24]), ALU.add)\
                .then_inc(mix_order, 1)
            dve.wait_ge(mix_order, 4)
            lp = logits[:, :, 16:24].rearrange("p t (a n) -> p t a n", n=STREAMS)
            pp4 = pp[:].unsqueeze(3).broadcast_to([P, TILES, 2, STREAMS])
            dve.tensor_scalar(Z.rearrange("p t i j -> p t (i j)"), logits[:, :, 0:16], 1.0 / TAU, None, ALU.mult).then_inc(mix_order, 1)
            dve.memset(lse[:], 0.0).then_inc(sink_order, 1)
            dve.tensor_reduce(pp[:], lp, AX.X, ALU.max).then_inc(mix_order, 1)
            dve.wait_ge(mix_order, 6)
            dve.tensor_tensor(lp, lp, pp4, ALU.subtract).then_inc(pp_exp_in, 1)
            dve.wait_ge(pp_exp_out, 1)
            dve.tensor_reduce(pp[:], lp, AX.X, ALU.add).then_inc(mix_order, 1)
            dve.wait_ge(mix_order, 7)
            dve.reciprocal(pp[:], pp[:]).then_inc(mix_order, 1)
            dve.wait_ge(mix_order, 8)
            dve.tensor_tensor(lp, lp, pp4, ALU.mult).then_inc(pp_ready, 1)
            dve.wait_ge(gate_scalar, 1)
            dve.tensor_scalar(scalars[:, 1:2], scalars[:, 1:2], 1.0, None, ALU.add).then_inc(mix_order, 1)
            dve.wait_ge(mix_order, 9)
            dve.reciprocal(scalars[:, 1:2], scalars[:, 1:2]).then_inc(mix_order, 1)
            dve.wait_ge(mix_order, 10)
            dve.tensor_scalar(scalars[:, 2:3], scalars[:, 1:2], -1.0, 1.0, ALU.mult, ALU.add).then_inc(mix_order, 1)

            orders, acts = 120, 14

            def sinkhorn_cycle(c):
                levels = [0]

                def level(build, after_act=None, to_act=False):
                    for h in range(2):
                        if after_act is not None:
                            dve.wait_ge(sink_from_act, c * acts + after_act[h])
                        elif levels[0]:
                            dve.wait_ge(sink_order, c * orders + 2 * levels[0] + h)
                        else:
                            dve.wait_ge(sink_order, c * orders + 1)
                        build(h).then_inc(sink_to_act if to_act else sink_order, 1)
                    levels[0] += not to_act

                for side in range(2):
                    view = turned if side else (lambda ap: ap)
                    over, over_other = (over_rows, over_cols) if side else (over_cols, over_rows)
                    level(lambda h: dve.tensor_tensor(halves(T, h), halves(Z, h), over_other(halves(lse[:, 1 - side], h)), ALU.add))
                    level(lambda h: dve.tensor_reduce(halves(red[:, 0], h), view(halves(T, h)), AX.X, ALU.max))
                    level(lambda h: dve.tensor_tensor(halves(T, h), halves(T, h), over(halves(red[:, 0], h)), ALU.subtract),
                          to_act=True)
                    level(lambda h: dve.tensor_reduce(halves(red[:, 1], h), view(halves(K, h)), AX.X, ALU.add),
                          after_act=[4 * side + 1, 4 * side + 2], to_act=True)
                    level(lambda h: dve.scalar_tensor_tensor(out=halves(lse[:, side], h), in0=halves(red[:, 0], h), scalar=-1.0,
                                                             in1=halves(red[:, 1], h), op0=ALU.mult, op1=ALU.subtract),
                          after_act=[4 * side + 3, 4 * side + 4])
                level(lambda h: dve.tensor_tensor(halves(T, h), halves(T, h), over_rows(halves(red[:, 1], h)), ALU.subtract),
                      to_act=True)
                for it in range(INNER):
                    for side in range(2):
                        view = turned if side else (lambda ap: ap)
                        over_other = over_cols if side else over_rows
                        first = it == 0 and side == 0
                        if not first:
                            level(lambda h: dve.tensor_tensor(halves(T, h), halves(K, h), over_other(halves(fac[:, 1 - side], h)), ALU.mult))
                        level(lambda h: dve.tensor_reduce(halves(red[:, side], h), view(halves(K if first else T, h)), AX.X, ALU.add),
                              after_act=[9, 10] if first else None)
                        level(lambda h: dve.reciprocal(halves(fac[:, side], h), halves(red[:, side], h)),
                              to_act=it == INNER - 1 and side == 1)
                for side in range(2):
                    level(lambda h: dve.tensor_tensor(halves(lse[:, side], h), halves(lse[:, side], h), halves(fac[:, side], h), ALU.add),
                          after_act=[12, 14])
                assert 2 * levels[0] == orders

            dve.wait_ge(mix_order, 11)
            with dve.Fori(0, CYCLES) as c:
                sinkhorn_cycle(c)
            for h in range(2):
                dve.wait_ge(sink_order, orders * CYCLES + 1)
                dve.tensor_tensor(halves(T, h), halves(Z, h), over_cols(halves(lse[:, 0], h)), ALU.add).then_inc(sink_order, 1)
            for h in range(2):
                dve.wait_ge(sink_order, orders * CYCLES + h + 2)
                dve.tensor_tensor(halves(T, h), halves(T, h), over_rows(halves(lse[:, 1], h)), ALU.add).then_inc(sink_to_act, 1)
            dve.wait_ge(sink_from_act, acts * CYCLES + 2)
            H = K.rearrange("p t i j -> p t (i j)")
            dve.tensor_scalar(H, H, scalars[:, 1:2], None, ALU.mult).then_inc(mix_order, 1)
            dve.wait_ge(mix_order, 12)
            diagonal = H[:, :, 0:STREAMS * STREAMS:STREAMS + 1]
            dve.tensor_scalar(diagonal, diagonal, scalars[:, 2:3], None, ALU.add).then_inc(mix_order, 1)
            dve.wait_ge(mix_order, 13)
            dve.wait_ge(y_added, 2)
            for t in range(TILES):
                z = (wq_raw, wo_raw)[t // HT]
                for j in range(STREAMS):
                    for i in range(STREAMS):
                        count = (t * STREAMS + j) * STREAMS + i
                        if j:
                            dve.wait_ge(mixed, count - STREAMS + 1)
                        dve.scalar_tensor_tensor(out=x[:, t, tok(i)], in0=z[:, t % HT, tok(j)],
                                                 scalar=K[:, t, i, j:j + 1], in1=x[:, t, tok(i)],
                                                 op0=ALU.mult, op1=ALU.add).then_inc(mixed, 1)


def rotary_tables():
    inv = (np.float32(1.0) / np.float32(10000.0) ** (np.arange(0, DH, 2, dtype=np.float32) / np.float32(DH))).astype(np.float32)
    angle = np.arange(MAX_POS, dtype=np.float32)[:, None] * inv[None, :]
    c, s = np.cos(angle).astype(np.float32), np.sin(angle).astype(np.float32)
    return np.ascontiguousarray(np.concatenate([c, c, s, -s], axis=1))


def kernel(**inputs):
    import concourse.bacc as bacc
    from concourse.bass_utils import run_bass_kernel_spmd

    a = {name: np.asarray(value) for name, value in inputs.items()}
    bkv = a["L0_xattn_bkv"].reshape(2, GROUPS, 1, DH)
    bqkv0 = np.concatenate([a["L0_xattn_bq"].reshape(GROUPS, GH, DH), bkv[0], bkv[1]], axis=1).transpose(2, 0, 1).reshape(DH, -1)
    arrays = {
        "x": a["x"].reshape(NT, D),
        "ctx_t": a["ctx_4096"].reshape(NT, D).T,
        "pos": a["pos_BxS2"].reshape(NT),
        "mask": a["mask_BxSxS2_ik0"],
        "wq0": a["L0_xattn_Wq"], "bqkv0": bqkv0,
        "wkv0": a["L0_xattn_Wkv"],
        "wo0": a["L0_xattn_Wo"], "bo0": a["L0_xattn_bo"],
        "wbase_t": a["L0_ffn_W_base"].T, "bbase": a["L0_ffn_b_base"],
        "gates_t": np.concatenate([a["L0_ffn_W_gate"], a["L0_ffn_W_thr"]]).T,
        "b_thr": a["L0_ffn_b_thr"],
        "a_t": a["L0_ffn_A"].reshape(EXPERTS * RANK, D).T,
        "b_mat": a["L0_ffn_B"].transpose(0, 2, 1).reshape(EXPERTS * RANK, D),
        "wq1": a["L1_xattn_Wq"], "wk1": a["L1_xattn_Wk"], "wv1": a["L1_xattn_Wv"], "wo1": a["L1_xattn_Wo"],
        "mix_t": np.concatenate([a["L1_ffn_W_res"], a["L1_ffn_W_pre"], a["L1_ffn_W_post"]]).T,
        "mix_base": np.concatenate([a["L1_ffn_H_res_base"].reshape(-1), a["L1_ffn_H_pre_base"], a["L1_ffn_H_post_base"]]),
        "gate": a["L1_ffn_gate"], "w_branch": a["L1_ffn_W_branch"],
        "tables": rotary_tables(),
    }
    arrays = {f"in_{name}": np.ascontiguousarray(value) for name, value in arrays.items()}
    nc = bacc.Bacc("TRN2", target_bir_lowering=False, num_devices=1)
    args = [nc.dram_tensor(name, v.shape, mybir.dt.from_np(v.dtype), kind="ExternalInput").ap() for name, v in arrays.items()]
    out = nc.dram_tensor("out_x", (NT, D), F32, kind="ExternalOutput").ap()
    bass_two_layers(nc, *args, out)
    result = run_bass_kernel_spmd(nc, [arrays], core_ids=[0])
    return result.results[0]["out_x"].reshape(B, S, D)
```

```python
from contextlib import ExitStack

import numpy as np

import concourse.bass as bass
from concourse import mybir

ALU = mybir.AluOpType
ACT = mybir.ActivationFunctionType
AX = mybir.AxisListType
F32 = mybir.dt.float32
F32R = mybir.dt.float32r
I32 = mybir.dt.int32
U8 = mybir.dt.uint8

P = 128
B, S = 16, 64
D = 512
NT = B * S
TILES = NT // P
HALF = NT // 2
HT = TILES // 2
HB = B // 2
KC = D // P
GROUPS, GH, DH = 8, 4, 128
PAIRS = HB // 2
EXPERTS, RANK = 8, 16
STREAMS, CH = 4, 128
MAX_POS = 512
SCALE = 1.0 / float(np.sqrt(np.float32(DH)))
MASKED = float(np.float32(-1e9) * np.sqrt(np.float32(DH)))
LN_EPS = 1e-5
RMS_EPS = 1.1920929e-07
TAU = 0.1
DVE_TILES, ACT_TILES = 4, 3
SEGMENTS, ROUNDS, ROUND = 3, 4, 4
START_LEVELS, SEGMENT_LEVELS = 5, 3 + 6 * ROUNDS * ROUND
RING = 6
FFN0_SET = GROUPS
L1_SET = GROUPS + 1


def bass_two_layers(nc, x_in_ap, ctx_t, pos, mask, wq0, bqkv0, wkv0, wo0, bo0, wbase_t, bbase, gates_t,
                    b_thr, a_t, b_mat, wq1, wk1, wv1, wo1, mix_t, mix_base, gate, w_branch, tables, out):
    with ExitStack() as ctx:
        def sb(name, shape, dt=F32):
            return ctx.enter_context(nc.sbuf_tensor(name, shape, dt))

        def sem(name):
            return ctx.enter_context(nc.semaphore(name))

        x = sb("x", [P, TILES, D])
        ctx_hi = sb("ctx_hi", [P, KC, NT], F32R)
        ctx_lo = sb("ctx_lo", [P, KC, NT], F32R)
        z_hi = sb("z_hi", [P, KC, NT], F32R)
        z_lo = sb("z_lo", [P, KC, NT], F32R)
        wq_raw, wq_hi, wq_lo = sb("wq_raw", [P, KC, D]), sb("wq_hi", [P, KC, D], F32R), sb("wq_lo", [P, KC, D], F32R)
        wk_raw, wk_hi, wk_lo = sb("wk_raw", [P, KC, DH]), sb("wk_hi", [P, KC, DH], F32R), sb("wk_lo", [P, KC, DH], F32R)
        wv_raw, wv_hi, wv_lo = sb("wv_raw", [P, KC, DH]), sb("wv_hi", [P, KC, DH], F32R), sb("wv_lo", [P, KC, DH], F32R)
        wo_raw, wo_hi, wo_lo = sb("wo_raw", [P, GH, D]), sb("wo_hi", [P, GH, D], F32R), sb("wo_lo", [P, GH, D], F32R)
        q = sb("q", [P, GH, HALF])
        k = sb("k", [P, HALF])
        v_t = sb("v_t", [P, HALF])
        v = sb("v", [P, PAIRS, DH])
        probs = sb("probs", [P, 2, HB, S])
        probs_t = sb("probs_t", [P, PAIRS, 2, GH * S])
        o_hi = sb("o_hi", [P, GH, HALF], F32R)
        o_lo = sb("o_lo", [P, GH, HALF], F32R)
        row_max_sb = sb("row_max_sb", [P, 2, HB])
        row_sum_sb = sb("row_sum_sb", [P, 2, HB])
        row_inv_sb = sb("row_inv_sb", [P, 2, HB])
        cos = sb("cos", [P, NT])
        sin = sb("sin", [P, NT])
        rot = sb("rot", [P, 4, HALF])
        masked_out = sb("masked_out", [P, B, S], U8)
        masked_value = sb("masked_value", [P, 1])
        ident = sb("ident", [P, P])
        qk_bias = sb("qk_bias", [P, GH + 1])
        v_bias = sb("v_bias", [P, 2])
        bias_row = sb("bias_row", [P, D])
        pos_col = sb("pos_col", [P, KC])
        stats = sb("stats", [P, HT, 6])
        mean_var = sb("mean_var", [P, HT, 2])
        rstd = sb("rstd", [P, HT])

        gate_w = sb("gate_w", [P, HT, EXPERTS + 1])
        gate_s = sb("gate_s", [P, HT, 4])
        logits = sb("logits", [P, TILES, 24])
        mix_base_sb = sb("mix_base_sb", [P, 24])
        rms = sb("rms", [P, TILES])
        pp = sb("pp", [P, TILES, 2])
        scalars = sb("scalars", [P, 4])

        ring = ctx.enter_context(nc.psum_tensor("ring", [P, RING, 512], F32))
        scores = ctx.enter_context(nc.psum_tensor("scores", [P, 2, 512], F32))

        ident_cleared, ident_made = sem("ident_cleared"), sem("ident_made")
        x_in = [sem(f"x_in{h}") for h in range(2)]
        ctx_in = [sem(f"ctx_in{h}") for h in range(2)]
        tables_in, pos_in, mask_in, small_in = sem("tables_in"), sem("pos_in"), sem("mask_in"), sem("small_in")
        row_in = sem("row_in")
        wq_in, wk_in, wv_in, wo_in = sem("wq_in"), sem("wk_in"), sem("wv_in"), sem("wo_in")
        wq_hi_done, wk_hi_done, wv_hi_done, wo_hi_done = [sem(f"w{c}_hi_done") for c in "qkvo"]
        wq_lo_done, wk_lo_done, wv_lo_done, wo_lo_done = [sem(f"w{c}_lo_done") for c in "qkvo"]
        wq_hi_part, wq_lo_part = sem("wq_hi_part"), sem("wq_lo_part")
        qk_bias_in, v_bias_in = sem("qk_bias_in"), sem("v_bias_in")
        pads_made = sem("pads_made")
        ctx_hi_done, ctx_lo_done = sem("ctx_hi_done"), sem("ctx_lo_done")
        zeros_made = sem("zeros_made")
        pos_order, onehot_ready, tables_ready = sem("pos_order"), sem("onehot_ready"), sem("tables_ready")
        tables_hi_done, tables_lo_done = sem("tables_hi_done"), sem("tables_lo_done")
        tables_out, mask_done = sem("tables_out"), sem("mask_done")
        var_ready, std_ready, norm_order = sem("var_ready"), sem("std_ready"), sem("norm_order")
        z_nat_ready, zt_ready, z_hi_ready, z_split = [sem(n) for n in ("z_nat_ready", "zt_ready", "z_hi_ready", "z_split")]
        bias_added = sem("bias_added")
        base_done = sem("base_done")
        ffn_hg_ready, ffn_hg_out, gate_cols, gate_order = [
            sem(n) for n in ("ffn_hg_ready", "ffn_hg_out", "gate_cols", "gate_order")]
        gate_exp_in, gate_exp_out, gate_wide, gate_wide_t, hw_ready, ffn_sum, ffn_added = [
            sem(n) for n in ("gate_exp_in", "gate_exp_out", "gate_wide", "gate_wide_t", "hw_ready", "ffn_sum", "ffn_added")]
        sq_done, ms_ready, rms_root = sem("sq_done"), sem("ms_ready"), sem("rms_root")
        mix_ready, mix_out, mix_cols, mix_order = [sem(n) for n in ("mix_ready", "mix_out", "mix_cols", "mix_order")]
        pp_exp_in, pp_exp_out, pp_ready, gate_scalar = [
            sem(n) for n in ("pp_exp_in", "pp_exp_out", "pp_ready", "gate_scalar")]
        sink_order, sink_to_act, sink_from_act = sem("sink_order"), sem("sink_to_act"), sem("sink_from_act")
        pre_sum, pre_t_ready, pre_t_out, y_ready, y_out, y_terms, y_added = [
            sem(n) for n in ("pre_sum", "pre_t_ready", "pre_t_out", "y_ready", "y_out", "y_terms", "y_added")]
        h_ready, mixed = sem("h_ready"), sem("mixed")
        act_terms, act_sum, act_mixed = sem("act_terms"), sem("act_sum"), sem("act_mixed")
        pool_order, out_done = sem("pool_order"), sem("out_done")

        att = [{n: sem(f"{n}{layer}") for n in (
            "scores_ready",
            "masked",
            "row_max",
            "shifted",
            "exp_done",
            "row_sum",
            "row_inv",
            "probs_ready",
            "pt_ready",
            "pt_out_act",
            "pt_out_dve",
            "vt_ready",
            "vt_out",
            "vtr_ready",
            "v_out",
            "qk_ready",
            "qk_read",
            "qk_out",
            "pv_ready",
            "o_hi_ready",
            "o_split",
            "op_ready",
            "o_added",
        )} for layer in range(2)]

        def layer_of(a):
            return 1 if a is att[1] else 0

        def bank(s, j):
            return ring[:, (15 * (s % 2) + j) % RING, :]

        def tok(t):
            return slice(t * P, (t + 1) * P)

        def half(h):
            return slice(h * HALF, (h + 1) * HALF)

        def qk_done(a):
            return a["qk_out"] if layer_of(a) else a["qk_read"]

        def probs_t_of(heads, second):
            rows = slice(S * second, S * second + S)
            return probs_t[rows, :, second, heads * P:(heads + 1) * P]

        q_by_seq = q[:].rearrange("p a n -> p (a n)").rearrange("p (b h s) -> p b h s", b=HB, h=GH)

        def by_seq(ap):
            return ap.rearrange("p (b s) -> p b s", s=S)

        def o_view(o, b):
            return o[:, :, tok(b)].rearrange("p h (b q) -> p b h q", b=2)

        tables_raw = probs[:].rearrange("p a b k -> p (a b k)")
        tables_hi, tables_lo = (w[:].rearrange("p h n -> p (h n)")[:, 0:KC * 2 * P] for w in (wo_hi, wo_lo))

        def one_hots(c):
            return (o_hi, o_lo)[c // 2][:, 2 * (c % 2):2 * (c % 2) + 2, :].rearrange("p a n -> p (a n)")

        table_bank = [ring[:, b, :] for b in (3, 4, 5, 1)]
        z_nat_of = [q, rot, q, rot, q, wo_raw, wq_raw, wo_raw]
        Z, T, K = (rot[:, 2, i * P:(i + 1) * P].rearrange("p (t i j) -> p t i j", i=STREAMS, j=STREAMS) for i in range(3))
        lse = rot[:, 3, 0:2 * TILES * STREAMS].rearrange("p (a t n) -> p a t n", a=2, n=STREAMS)
        fac = rot[:, 3, 64:64 + 2 * TILES * STREAMS].rearrange("p (a t n) -> p a t n", a=2, n=STREAMS)
        red = rot[:, 3, 128:128 + 2 * TILES * STREAMS].rearrange("p (a t n) -> p a t n", a=2, n=STREAMS)

        pool_terms = [cos[:].rearrange("p (j n) -> p j n", n=D), probs[:].rearrange("p a b k -> p a (b k)")]
        mix_bank = [ring[:, b, :] for b in (5, 0)]
        sum_bank = [ring[:, b, :] for b in (4, 5, 2)]

        def mix_terms(i):
            return probs_t[:].rearrange("p a b n -> p a (b n)") if i % 2 else q[:]

        def levels_done(c):
            return c * (2 * SEGMENT_LEVELS) + 2 * START_LEVELS

        def halves(ap, h):
            return ap[:, h * HT:(h + 1) * HT]

        def over_rows(ap):
            return ap.unsqueeze(2).broadcast_to([P, HT, STREAMS, STREAMS])

        def over_cols(ap):
            return ap.unsqueeze(3).broadcast_to([P, HT, STREAMS, STREAMS])

        def turned(ap):
            return ap.rearrange("p t i j -> p t j i")

        block = ctx.enter_context(nc.Block())

        @block.sync
        def _(sp):
            wq_of = [w.rearrange("(c p) n -> p c n", p=P) for w in (wq0, wq1)]
            wk_of = [w.rearrange("(c p) n -> p c n", p=P) for w in (wkv0[:, 0:GROUPS * DH], wk1)]
            wv_of = [w.rearrange("(c p) n -> p c n", p=P) for w in (wkv0[:, GROUPS * DH:], wv1)]
            wo_of = [w.rearrange("(g h p) n -> p g h n", p=P, h=GH) for w in (wo0, wo1)]
            x_of = x_in_ap.rearrange("(t p) n -> p t n", p=P)
            out_of = out.rearrange("(t p) n -> p t n", p=P)
            ctx_of = ctx_t.rearrange("(c p) n -> p c n", p=P)

            def qkv_loads(layer):
                return ((wq_raw, wq_of[layer], D, wq_in, wq_lo_done),
                        (wk_raw, wk_of[layer], DH, wk_in, wk_lo_done),
                        (wv_raw, wv_of[layer], DH, wv_in, wv_lo_done))

            def load_w(raw, src, width, arrived, split, g, split_sets):
                if split_sets is not None:
                    sp.wait_ge(split, split_sets)
                sp.dma_start(raw[:], src[:, :, bass.ds(g * width, width)]).then_inc(arrived, 16)

            def load_qkv(layer, g, split_sets):
                for load in qkv_loads(layer):
                    load_w(*load, g, split_sets)

            def load_qk_bias(g):
                sp.dma_start(qk_bias[:], bqkv0[:, bass.ds(g * (GH + 2), GH + 1)]).then_inc(qk_bias_in, 16)

            def load_v_bias(g):
                sp.dma_start(v_bias[:], bqkv0[:, bass.ds(g * (GH + 2) + GH, 2)]).then_inc(v_bias_in, 16)

            def load_wo(layer, g):
                sp.dma_start(wo_raw[:], wo_of[layer][:, bass.ds(g, 1), :, :].rearrange("p a h n -> p (a h) n")).then_inc(wo_in, 16)

            sp.dma_start(x[:, 0:HT, :], x_of[:, 0:HT, :]).then_inc(x_in[0], 16)
            load_w(*qkv_loads(0)[0], 0, None)
            load_qk_bias(0)
            sp.dma_start(probs_t[:].rearrange("p a b n -> p a (b n)"), ctx_of[:, :, half(0)]).then_inc(ctx_in[0], 16)
            sp.dma_start(cos[:].bitcast(I32), pos.partition_broadcast(P)).then_inc(pos_in, 16)
            load_w(*qkv_loads(0)[1], 0, None)
            sp.dma_start(tables_raw.rearrange("p (c n) -> p c n", c=KC), tables.rearrange("(c p) n -> p c n", p=P)).then_inc(tables_in, 16)
            sp.dma_start(x[:, HT:, :], x_of[:, HT:, :]).then_inc(x_in[1], 16)
            load_w(*qkv_loads(0)[2], 0, None)
            sp.dma_start(wo_raw[:], ctx_of[:, :, half(1)]).then_inc(ctx_in[1], 16)
            load_v_bias(0)
            sp.wait_ge(tables_lo_done, 1)
            for i in range(2):
                sp.dma_start(probs[S * i:S * i + S].bitcast(I32).rearrange("p a b k -> p (a b) k"),
                             mask.rearrange("b q k -> q b k")).then_inc(mask_in, 16)
            sp.wait_ge(ctx_lo_done, 2)
            load_wo(0, 0)
            with sp.Fori(1, GROUPS) as g:
                load_qkv(0, g, g)
                sp.wait_ge(att[0]["qk_read"], g * 10)
                load_qk_bias(g)
                sp.wait_ge(wo_lo_done, g)
                load_wo(0, g)
                sp.wait_ge(att[0]["vt_out"], g * 2)
                load_v_bias(g)
            sp.wait_ge(wq_lo_done, GROUPS)
            sp.dma_start(wq_raw[:], wbase_t.rearrange("(c p) n -> p c n", p=P)).then_inc(wq_in, 16)
            sp.wait_ge(wk_lo_done, GROUPS)
            sp.dma_start(wk_raw[:], a_t.rearrange("(c p) n -> p c n", p=P)).then_inc(wk_in, 16)
            sp.wait_ge(pads_made, 1)
            sp.dma_start(wv_raw[:, :, 0:EXPERTS + 1], gates_t.rearrange("(c p) n -> p c n", p=P)).then_inc(wv_in, 16)
            sp.wait_ge(wo_lo_done, GROUPS)
            sp.dma_start(wo_raw[:, 0, :], b_mat).then_inc(wo_in, 16)
            sp.wait_ge(bias_added, TILES)
            sp.dma_start(bias_row[:], bbase.partition_broadcast(P)).then_inc(row_in, 16)
            load_qkv(1, 0, L1_SET)
            sp.wait_ge(zt_ready, HT * 6)
            load_wo(1, 0)
            with sp.Fori(1, GROUPS) as g:
                load_qkv(1, g, g + L1_SET)
                sp.wait_ge(wo_lo_done, g + GROUPS)
                load_wo(1, g)
            sp.wait_ge(wk_lo_done, L1_SET + GROUPS)
            sp.dma_start(wk_raw[:, 0, :], w_branch).then_inc(wk_in, 16)
            sp.wait_ge(pads_made, 2)
            sp.dma_start(wv_raw[:, :, 0:24], mix_t.rearrange("(c p) n -> p c n", p=P)).then_inc(wv_in, 16)
            for t in (0, 4, 1, 7, 5, 2, 3, 6):
                if t < DVE_TILES:
                    sp.wait_ge(mixed, STREAMS * STREAMS * (t + 1))
                elif t < DVE_TILES + ACT_TILES:
                    sp.wait_ge(act_mixed, t - DVE_TILES + 1)
                else:
                    sp.wait_ge(pool_order, 5)
                sp.dma_start(out_of[:, t, :], x[:, t, :]).then_inc(out_done, 16)
            sp.wait_ge(out_done, 16 * TILES)

        @block.tensor
        def _(pe):
            def split_product(dst, hi_a, lo_a, hi_b, lo_b, stop=True):
                n = len(hi_a)
                for c in range(n):
                    pe.matmul(dst, hi_a[c], hi_b[c], start=(c == 0), stop=False)
                    pe.matmul(dst, hi_a[c], lo_b[c], start=False, stop=False)
                    last = pe.matmul(dst, lo_a[c], hi_b[c], start=False, stop=stop and c == n - 1)
                return last

            def chunks(w, cols=slice(0, DH)):
                return [w[:, c, cols] for c in range(w.shape[1])]

            def norm_turn(m, tiles=range(HT)):
                for t in tiles:
                    pe.wait_ge(z_nat_ready, HT * m + t + 1)
                    if HT * m + t >= 2:
                        pe.wait_ge(z_split, HT * m + t - 1)
                    dst = scores[:, t % 2, :]
                    for c in range(KC):
                        last = pe.transpose(dst[:, tok(c)], z_nat_of[m][:, t, tok(c)], ident[:])
                    last.then_inc(zt_ready, 1)

            def project_qk(a, h, dst_of, new_set=None, previous=None, prologue=False):
                if new_set is not None and not prologue:
                    pe.wait_ge(wq_hi_done, new_set + 1)
                    pe.wait_ge(wq_lo_done, new_set + 1)
                for i in range(GH):
                    if prologue and i < GH - 1:
                        pe.wait_ge(wq_hi_part, (GH - 1) * layer_of(a) + i + 1)
                        pe.wait_ge(wq_lo_part, (GH - 1) * layer_of(a) + i + 1)
                    elif prologue:
                        pe.wait_ge(wq_hi_done, new_set + 1)
                        pe.wait_ge(wq_lo_done, new_set + 1)
                    if previous is not None and i >= 1:
                        pe.wait_ge(a["o_split"], previous + i)
                    split_product(dst_of(1 + i), chunks(wq_hi, tok(i)), chunks(wq_lo, tok(i)),
                                  chunks(z_hi, half(h)), chunks(z_lo, half(h))).then_inc(a["qk_ready"], 1)
                if prologue and layer_of(a):
                    norm_turn(5, (0, 1))
                if new_set is not None:
                    pe.wait_ge(wk_hi_done, new_set + 1)
                    pe.wait_ge(wk_lo_done, new_set + 1)
                    pe.wait_ge(ctx_lo_done, 1)
                if previous is not None:
                    pe.wait_ge(a["o_split"], previous + GH)
                split_product(dst_of(1 + GH), chunks(wk_hi), chunks(wk_lo),
                              chunks(ctx_hi, half(h)), chunks(ctx_lo, half(h))).then_inc(a["qk_ready"], 1)

            def project_out(a, dst_of, tiles=range(HT)):
                for i in tiles:
                    split_product(dst_of(7 + i), chunks(o_hi, tok(i)), chunks(o_lo, tok(i)),
                                  chunks(wo_hi, slice(0, D)), chunks(wo_lo, slice(0, D))).then_inc(a["op_ready"], 1)

            def step(a, g, h, first=False, last=False):
                s = g * 2 + h
                n = g + L1_SET * layer_of(a)
                def make_scores():
                    pe.wait_ge(qk_done(a), s * 5 + 5)
                    if first:
                        pe.wait_ge(z_split, HT * (4 * layer_of(a) + 2))
                    else:
                        pe.wait_ge(a["pt_out_act"], s * 2)
                        pe.wait_ge(a["pt_out_dve"], s * 2)
                    for hp in range(2):
                        for b in range(HB):
                            width = 2 * S if b < HB - 1 else S
                            mm = pe.matmul(scores[:, hp, b * S:b * S + width],
                                           q_by_seq[:, b, 2 * hp:2 * hp + 2, :].rearrange("p h s -> p (h s)"),
                                           k[:, b * S:b * S + width], start=True, stop=True)
                        mm.then_inc(a["scores_ready"], 1)

                if not first:
                    make_scores()
                if h == 0:
                    pe.wait_ge(wv_hi_done, n + 1)
                    pe.wait_ge(wv_lo_done, n + 1)
                if first:
                    pe.wait_ge(a["qk_read"], 3)
                elif not (isinstance(s, int) and s == 1):
                    pe.wait_ge(a["o_added"], s * 4 - 4)
                split_product(bank(h, 0), chunks(wv_hi), chunks(wv_lo),
                              chunks(ctx_hi, half(h)), chunks(ctx_lo, half(h))).then_inc(a["vt_ready"], 1)
                if first:
                    make_scores()
                    if not layer_of(a):
                        pe.wait_ge(tables_out, 4)
                        pe.wait_ge(ctx_lo_done, 2)
                if last:
                    pe.wait_ge(a["o_split"], s * 4)
                    pe.wait_ge(wo_hi_done, g + GROUPS * layer_of(a) + 1)
                    pe.wait_ge(wo_lo_done, g + GROUPS * layer_of(a) + 1)
                    project_out(a, lambda j: bank(h, j))
                else:
                    project_qk(a, 1 - h, lambda j: bank(h, j), new_set=(n + 1 if h else None),
                               previous=(None if first else s * 4 - 4))
                for hp in range(2):
                    pe.wait_ge(a["probs_ready"], s * 2 + hp + 1)
                    for b in range(PAIRS):
                        mm = pe.transpose(scores[:, hp, tok(b)],
                                          probs[:, hp, 2 * b:2 * b + 2, :].rearrange("p b k -> p (b k)"), ident[:])
                    mm.then_inc(a["pt_ready"], 1)
                pe.wait_ge(a["vt_out"], s + 1)
                for b in range(PAIRS):
                    mm = pe.transpose(bank(h, 6)[:, tok(b)], v_t[:, tok(b)], ident[:])
                mm.then_inc(a["vtr_ready"], 1)
                if not first and not last:
                    pe.wait_ge(a["o_split"], s * 4)
                    if h:
                        n_wo = g + GROUPS * layer_of(a)
                        pe.wait_ge(wo_hi_done, n_wo + 1)
                        pe.wait_ge(wo_lo_done, n_wo + 1)
                    pe.wait_ge(a["qk_read"], s * 5 + 5 + GH)
                    project_out(a, lambda j: bank(h, j))
                if not last:
                    pe.wait_ge(a["qk_read"], s * 5 + 10)
                pe.wait_ge(a["pt_out_act"], s * 2 + 2)
                pe.wait_ge(a["pt_out_dve"], s * 2 + 2)
                pe.wait_ge(a["v_out"], s + 1)
                for b in range(PAIRS):
                    if b >= 2 and not first:
                        pe.wait_ge(a["o_added"], s * 4 - 4 + b - 1)
                    pe.matmul(bank(h, 11 + b), v[:, b, :], probs_t[:, b, :, :], start=True, stop=True)\
                        .then_inc(a["pv_ready"], 1)

            def look_up_tables():
                pe.wait_ge(att[0]["qk_read"], GH)
                pe.wait_ge(tables_lo_done, 1)
                for c in range(KC):
                    pe.wait_ge(onehot_ready, c + 1)
                    for i, dst in enumerate(table_bank):
                        cols = slice((2 * c + i // 2) * P, (2 * c + i // 2 + 1) * P)
                        pe.matmul(dst, tables_hi[:, cols], one_hots(c)[:, half(i % 2)], start=(c == 0), stop=False)
                        mm = pe.matmul(dst, tables_lo[:, cols], one_hots(c)[:, half(i % 2)], start=False, stop=(c == KC - 1))
                mm.then_inc(tables_ready, 1)

            def attention(layer):
                a = att[layer]
                if not layer:
                    norm_turn(0)
                pe.wait_ge(z_split, HT * (4 * layer + 1))
                project_qk(a, 0, lambda j: bank(1, j), new_set=L1_SET * layer, prologue=True)
                if layer:
                    norm_turn(5, (2, 3))
                else:
                    norm_turn(1)
                    look_up_tables()
                pe.wait_ge(zeros_made, 1)
                step(a, 0, 0, first=True)
                step(a, 0, 1)
                with pe.Fori(1, GROUPS - 1) as g:
                    step(a, g, 0)
                    step(a, g, 1)
                step(a, GROUPS - 1, 0)
                step(a, GROUPS - 1, 1, last=True)
                m = 4 * layer + 2
                norm_turn(m, (0, 1))
                pe.wait_ge(a["o_split"], 8 * GROUPS)
                pe.wait_ge(a["o_added"], 8 * GROUPS - 4)
                project_out(a, lambda j: bank(0, j), (0, 1))
                norm_turn(m, (2, 3))
                project_out(a, lambda j: bank(0, j), (2, 3))

            pe.wait_ge(ident_made, 2)
            attention(0)

            base_bank = [ring[:, b, :] for b in (4, 5, 0, 1)]
            for h in range(2):
                def base(tiles):
                    for t in tiles:
                        if h:
                            pe.wait_ge(ffn_added, t + 1)
                        mm = split_product(base_bank[t], chunks(z_hi, tok(HT * h + t)), chunks(z_lo, tok(HT * h + t)),
                                           chunks(wq_hi, slice(0, D)), chunks(wq_lo, slice(0, D)), stop=False)
                    return mm

                pe.wait_ge(z_split, HT * (3 + h))
                if h == 0:
                    pe.wait_ge(wk_lo_done, FFN0_SET + 1)
                    pe.wait_ge(wv_lo_done, FFN0_SET + 1)
                    pe.wait_ge(att[0]["o_added"], 8 * GROUPS - 1)
                else:
                    pe.wait_ge(hw_ready, 1)
                    pe.wait_ge(gate_wide, 1)
                split_product(ring[:, 2, :], chunks(wk_hi), chunks(wk_lo), chunks(z_hi, half(h)), chunks(z_lo, half(h)))\
                    .then_inc(ffn_hg_ready, 1)
                split_product(ring[:, 3, :], chunks(wv_hi), chunks(wv_lo), chunks(z_hi, half(h)), chunks(z_lo, half(h)))\
                    .then_inc(ffn_hg_ready, 1)
                pe.wait_ge(wq_lo_done, FFN0_SET + 1)
                if h == 0:
                    pe.wait_ge(att[0]["o_added"], 8 * GROUPS)
                base((0, 1))
                pe.wait_ge(ffn_hg_out, 2 * h + 2)
                for t in range(HT):
                    mm = pe.transpose(ring[:, 3, tok(t)], v_t[:, tok(t)], ident[:])
                mm.then_inc(gate_cols, 1)
                norm_turn(3 + h, (0, 1))
                base((2, 3)).then_inc(base_done, 1)
                pe.wait_ge(gate_wide, h + 1)
                for t in range(HT):
                    mm = pe.transpose(ring[:, 2, tok(t)], v[:, t, :], ident[:])
                mm.then_inc(gate_wide_t, 1)
                norm_turn(3 + h, (2, 3))
                pe.wait_ge(hw_ready, h + 1)
                pe.wait_ge(wo_in, 16 * (FFN0_SET + 1))
                for t in range(HT):
                    pe.matmul(base_bank[t], rot[:, 0, tok(t)], wo_raw[:, 0, :], start=False, stop=True)\
                        .then_inc(ffn_sum, 1)

            pe.wait_ge(ffn_added, TILES)
            attention(1)

            for h in range(2):
                if h:
                    norm_turn(7)
                pe.wait_ge(z_split, HT * (7 + h))
                if h == 0:
                    pe.wait_ge(wv_lo_done, L1_SET + GROUPS + 1)
                split_product(mix_bank[h], chunks(wv_hi), chunks(wv_lo), chunks(z_hi, half(h)), chunks(z_lo, half(h)))\
                    .then_inc(mix_ready, 1)
                pe.wait_ge(mix_out, h + 1)
                pe.wait_ge(att[1]["o_added"], 8 * GROUPS - 3 + h)
                for t in range(HT):
                    mm = pe.transpose(ring[:, 1 + h, tok(t)], (k, v_t)[h][:, tok(t)], ident[:])
                mm.then_inc(mix_cols, 1)
            for h in range(2):
                pe.wait_ge(pre_sum, 3 * h + 3)
                for t in range(HT):
                    mm = pe.transpose(ring[:, 2 + h, tok(t)], rot[:, h, tok(t)], ident[:])
                mm.then_inc(pre_t_ready, 1)
                pe.wait_ge(pre_t_out, h + 1)
                pe.wait_ge(wk_in, 16 * (L1_SET + GROUPS + 1))
                for t in range(HT):
                    mm = pe.matmul(ring[:, h, tok(t)], cos[:, tok(HT * h + t)], wk_raw[:, 0, :], start=True, stop=True)
                mm.then_inc(y_ready, 1)
            for i in range(ACT_TILES):
                for j in range(STREAMS):
                    pe.wait_ge(act_terms, STREAMS * i + j + 1)
                    pe.matmul(sum_bank[i], ident[:], mix_terms(i)[:, j, :], start=(j == 0), stop=False)
                pe.matmul(sum_bank[i], ident[:], x[:, DVE_TILES + i, :], start=False, stop=True).then_inc(act_sum, 1)

        @block.scalar
        def _(act):
            def norm_root(m):
                act.wait_ge(var_ready, m + 1)
                act.activation(rstd[:], rstd[:], ACT.Sqrt).then_inc(std_ready, 1)

            def norm_hi(m):
                for t in range(HT):
                    act.wait_ge(zt_ready, HT * m + t + 1)
                    act.activation(z_hi[:, :, tok(HT * (m % 2) + t)],
                                   scores[:, t % 2, :].rearrange("p (c n) -> p c n", c=KC), ACT.Copy)\
                        .then_inc(z_hi_ready, 1)

            def split_wq_hi_parts(loads):
                act.wait_ge(wq_in, loads * 16)
                for i in range(GH):
                    act.activation(wq_hi[:, :, tok(i)], wq_raw[:, :, tok(i)], ACT.Copy)\
                        .then_inc(wq_hi_done if i == GH - 1 else wq_hi_part, 1)

            def split_hi(raw, hi, arrived, loads, done):
                act.wait_ge(arrived, loads * 16)
                act.activation(hi[:], raw[:], ACT.Copy).then_inc(done, 1)

            def copy_qk(a, g, idx, parity):
                act.wait_ge(qk_bias_in, g * 16 + 16)
                for i in range(5):
                    act.wait_ge(a["qk_ready"], idx + i + 1)
                    src = bank(parity, 1 + i)
                    if i < GH:
                        act.activation(q_by_seq[:, :, i, :], by_seq(src), ACT.Identity, bias=qk_bias[:, i:i + 1])\
                            .then_inc(a["qk_read"], 1)
                    else:
                        act.activation(k[:], src, ACT.Identity, bias=qk_bias[:, GH:GH + 1]).then_inc(a["qk_read"], 1)

            def step(a, g, h, last=False):
                s = g * 2 + h
                n = g + L1_SET * layer_of(a)
                n_wo = g + GROUPS * layer_of(a)
                for hp in range(2):
                    act.wait_ge(a["shifted"], s * 2 + hp + 1)
                    act.activation(probs[:, hp], probs[:, hp], ACT.Exp, scale=SCALE).then_inc(a["exp_done"], 1)
                act.wait_ge(a["vt_ready"], s + 1)
                if layer_of(a):
                    act.activation(v_t[:], bank(h, 0), ACT.Copy).then_inc(a["vt_out"], 1)
                else:
                    act.wait_ge(v_bias_in, g * 16 + 16)
                    act.activation(v_t[:], bank(h, 0), ACT.Identity, bias=v_bias[:, 1:2]).then_inc(a["vt_out"], 1)
                if last and not layer_of(a):
                    split_hi(wq_raw, wq_hi, wq_in, FFN0_SET + 1, wq_hi_done)
                    split_hi(wk_raw, wk_hi, wk_in, FFN0_SET + 1, wk_hi_done)
                if last:
                    split_hi(wv_raw, wv_hi, wv_in, n + 2, wv_hi_done)
                if not layer_of(a) and not last:
                    copy_qk(a, g + h, s * 5 + 5, h)
                act.wait_ge(a["pt_ready"], s * 2 + 1)
                for second in range(2):
                    act.activation(probs_t_of(0, second),
                                   scores[S * second:S * second + S, 0, :].rearrange("p (b n) -> p b n", b=PAIRS),
                                   ACT.Copy).then_inc(a["pt_out_act"], 1)
                act.wait_ge(a["vtr_ready"], s + 1)
                act.activation(v[:], bank(h, 6).rearrange("p (b n) -> p b n", b=PAIRS), ACT.Copy).then_inc(a["v_out"], 1)
                if not last:
                    if h == 0:
                        if not (isinstance(g, int) and g == GROUPS - 1):
                            act.wait_ge(a["qk_ready"], s * 5 + 10)
                            split_hi(wq_raw, wq_hi, wq_in, n + 2, wq_hi_done)
                            split_hi(wk_raw, wk_hi, wk_in, n + 2, wk_hi_done)
                    else:
                        split_hi(wv_raw, wv_hi, wv_in, n + 2, wv_hi_done)
                if last:
                    norm_root(4 * layer_of(a) + 2)
                for b in range(PAIRS):
                    act.wait_ge(a["pv_ready"], s * 4 + b + 1)
                    act.activation(o_view(o_hi, b), bank(h, 11 + b).rearrange("p (b h q) -> p b h q", b=2, h=GH), ACT.Copy)\
                        .then_inc(a["o_hi_ready"], 1)
                if h == 0:
                    split_hi(wo_raw, wo_hi, wo_in, n_wo + 1 + layer_of(a), wo_hi_done)

            def attention(layer):
                a = att[layer]
                if layer:
                    act.wait_ge(base_done, 2)
                    split_wq_hi_parts(L1_SET + 1)
                    split_hi(wk_raw, wk_hi, wk_in, L1_SET + 1, wk_hi_done)
                    split_hi(wv_raw, wv_hi, wv_in, L1_SET + 1, wv_hi_done)
                    norm_root(5)
                else:
                    norm_root(0)
                    split_wq_hi_parts(1)
                    norm_hi(0)
                    split_hi(wk_raw, wk_hi, wk_in, 1, wk_hi_done)
                    act.wait_ge(ctx_in[0], 16)
                    act.activation(ctx_hi[:, :, half(0)], probs_t[:].rearrange("p a b n -> p a (b n)"), ACT.Copy).then_inc(ctx_hi_done, 1)
                    act.wait_ge(tables_in, 16)
                    act.activation(tables_hi, tables_raw, ACT.Copy).then_inc(tables_hi_done, 1)
                    split_hi(wv_raw, wv_hi, wv_in, 1, wv_hi_done)
                    act.wait_ge(ctx_in[1], 16)
                    act.activation(ctx_hi[:, :, half(1)], wo_raw[:], ACT.Copy).then_inc(ctx_hi_done, 1)
                    norm_root(1)
                    copy_qk(a, 0, 0, 1)
                norm_hi(4 * layer + 1)
                if not layer:
                    act.wait_ge(tables_ready, 1)
                    for i in range(4):
                        act.activation((cos, sin)[i // 2][:, half(i % 2)], table_bank[i], ACT.Copy).then_inc(tables_out, 1)
                step(a, 0, 0)
                step(a, 0, 1)
                with act.Fori(1, GROUPS - 1) as g:
                    step(a, g, 0)
                    step(a, g, 1)
                step(a, GROUPS - 1, 0)
                step(a, GROUPS - 1, 1, last=True)

            act.dma_start(scalars[:, 0:1], b_thr.partition_broadcast(P)).then_inc(small_in, 16)
            act.dma_start(scalars[:, 1:2], gate.partition_broadcast(P)).then_inc(small_in, 16)
            act.dma_start(mix_base_sb[:], mix_base.partition_broadcast(P)).then_inc(small_in, 16)
            act.dma_start(bias_row[:], bo0.partition_broadcast(P)).then_inc(row_in, 16)
            attention(0)

            norm_hi(2)
            norm_root(3)
            for h in range(2):
                for i, dst in enumerate((k, v_t)):
                    act.wait_ge(ffn_hg_ready, 2 * h + i + 1)
                    act.activation(dst[:], ring[:, 2 + i, :], ACT.Copy).then_inc(ffn_hg_out, 1)
                act.wait_ge(gate_exp_in, h + 1)
                act.activation(gate_w[:], gate_w[:], ACT.Exp).then_inc(gate_exp_out, 1)
                norm_hi(3 + h)
                if h == 0:
                    norm_root(4)
            attention(1)

            def squares(h):
                for t in range(HT * h, HT * h + HT):
                    if t >= 1:
                        act.wait_ge(sq_done, t)
                    act.activation(probs[:].rearrange("p a b k -> p (a b k)")[:, (t % 2) * D:(t % 2 + 1) * D],
                                   (wq_raw, wo_raw)[h][:, t % HT, :], ACT.Square,
                                   accum_out=rms[:, t:t + 1]).then_inc(sq_done, 1)

            def mix_logits_out(h):
                act.wait_ge(mix_ready, h + 1)
                act.activation((k, v_t)[h][:], mix_bank[h], ACT.Copy).then_inc(mix_out, 1)

            norm_hi(6)
            squares(0)
            norm_root(7)
            mix_logits_out(0)
            norm_hi(7)
            squares(1)
            mix_logits_out(1)
            act.wait_ge(ms_ready, 1)
            act.activation(rms[:], rms[:], ACT.Sqrt).then_inc(rms_root, 1)
            act.wait_ge(pp_exp_in, 1)
            lp = logits[:, :, 16:24]
            act.activation(lp, lp, ACT.Exp).then_inc(pp_exp_out, 1)
            act.wait_ge(small_in, 48)
            act.activation(scalars[:, 1:2], scalars[:, 1:2], ACT.Exp, scale=-1.0).then_inc(gate_scalar, 1)

            def mixed_out(i):
                act.wait_ge(act_sum, i + 1)
                act.activation(x[:, DVE_TILES + i, :], sum_bank[i], ACT.Copy).then_inc(act_mixed, 1)

            def exp_k(h):
                return act.activation(halves(K, h), halves(T, h), ACT.Exp)

            for side in range(2):
                for h in range(2):
                    act.wait_ge(sink_to_act, 4 * side + h + 1)
                    exp_k(h).then_inc(sink_from_act, 1)
                for h in range(2):
                    act.wait_ge(sink_to_act, 4 * side + 2 + h + 1)
                    r = halves(red[:, 1], h)
                    act.activation(r, r, ACT.Ln).then_inc(sink_from_act, 1)

            def refresh(c):
                for h in range(2):
                    act.wait_ge(sink_order, levels_done(c) - 1 + h)
                    f = fac[:, :, h * HT:(h + 1) * HT]
                    act.activation(f, f, ACT.Ln).then_inc(sink_from_act, 1)
                for h in range(2):
                    act.wait_ge(sink_to_act, 8 + c * 2 + h + 1)
                    exp_k(h).then_inc(sink_from_act, 1)

            refresh(0)
            for h in range(2):
                act.wait_ge(pre_t_ready, h + 1)
                act.activation(cos[:, half(h)], ring[:, 2 + h, :], ACT.Copy).then_inc(pre_t_out, 1)
                act.wait_ge(y_ready, h + 1)
                act.activation(sin[:, half(h)], ring[:, h, :], ACT.Copy).then_inc(y_out, 1)
            with act.Fori(1, SEGMENTS) as c:
                refresh(c)

            act.wait_ge(h_ready, 1)
            for i in range(ACT_TILES):
                tile = DVE_TILES + i
                if i >= 2:
                    act.wait_ge(act_sum, i - 1)
                for j in range(STREAMS):
                    for n in range(STREAMS):
                        last = act.activation(mix_terms(i)[:, j, tok(n)], wo_raw[:, tile - HT, tok(j)], ACT.Copy,
                                              scale=K[:, tile, n, j:j + 1])
                    last.then_inc(act_terms, 1)
                if i:
                    mixed_out(i - 1)
            mixed_out(ACT_TILES - 1)

        @block.gpsimd
        def _(pool):
            def split_lo(raw, hi, lo, hi_done, sets, done):
                pool.wait_ge(hi_done, sets)
                pool.tensor_tensor(lo[:], raw[:], hi[:], ALU.subtract).then_inc(done, 1)

            def split_wq_lo_parts(sets):
                for i in range(GH):
                    if i < GH - 1:
                        pool.wait_ge(wq_hi_part, (GH - 1) * (sets > 1) + i + 1)
                    else:
                        pool.wait_ge(wq_hi_done, sets)
                    pool.tensor_tensor(wq_lo[:, :, tok(i)], wq_raw[:, :, tok(i)], wq_hi[:, :, tok(i)], ALU.subtract)\
                        .then_inc(wq_lo_done if i == GH - 1 else wq_lo_part, 1)

            def add_bias(m):
                for t in range(HT):
                    tile = HT * (m % 2) + t
                    pool.wait_ge(z_nat_ready, HT * m + t + 1)
                    pool.tensor_tensor(x[:, tile, :], x[:, tile, :], bias_row[:], ALU.add).then_inc(bias_added, 1)

            def turn_add(a, idx, parity):
                for i in range(5):
                    b = (parity + i) % 2
                    pool.wait_ge(a["qk_read"], idx + i + 1)
                    pool.tensor_tensor(q_by_seq[:, :, i, :] if i < GH else by_seq(k[:]),
                                       by_seq(rot[:, b, :]), by_seq(rot[:, 2 + b, :]), ALU.add)\
                        .then_inc(a["qk_out"], 1)

            def step(a, g, h, last=False):
                s = g * 2 + h
                n = g + L1_SET * layer_of(a)
                n_wo = g + GROUPS * layer_of(a)
                if last:
                    pool.wait_ge(wv_lo_done, n + 1)
                    pool.memset(wv_raw[:], 0.0).then_inc(pads_made, 1)
                for hp in range(2):
                    pool.wait_ge(a["row_inv"], s * 2 + hp + 1)
                    pool.tensor_tensor(probs[:, hp], probs[:, hp],
                                       row_inv_sb[:, hp, :].unsqueeze(2).broadcast_to([P, HB, S]), ALU.mult)\
                        .then_inc(a["probs_ready"], 1)
                if layer_of(a) and not last:
                    turn_add(a, s * 5 + 5, 1 - h)
                if not last:
                    if h == 0:
                        if not (isinstance(g, int) and g == GROUPS - 1):
                            split_lo(wq_raw, wq_hi, wq_lo, wq_hi_done, n + 2, wq_lo_done)
                            split_lo(wk_raw, wk_hi, wk_lo, wk_hi_done, n + 2, wk_lo_done)
                    else:
                        split_lo(wv_raw, wv_hi, wv_lo, wv_hi_done, n + 2, wv_lo_done)
                if last and not layer_of(a):
                    split_lo(wq_raw, wq_hi, wq_lo, wq_hi_done, FFN0_SET + 1, wq_lo_done)
                    split_lo(wk_raw, wk_hi, wk_lo, wk_hi_done, FFN0_SET + 1, wk_lo_done)
                if last:
                    split_lo(wv_raw, wv_hi, wv_lo, wv_hi_done, n + 2, wv_lo_done)
                if h == 0:
                    split_lo(wo_raw, wo_hi, wo_lo, wo_hi_done, n_wo + 1, wo_lo_done)

            def attention(layer):
                a = att[layer]
                if layer:
                    turn_add(a, 0, 0)
                step(a, 0, 0)
                step(a, 0, 1)
                with pool.Fori(1, GROUPS - 1) as g:
                    step(a, g, 0)
                    step(a, g, 1)
                step(a, GROUPS - 1, 0)
                step(a, GROUPS - 1, 1, last=True)

            pool.iota(pos_col[:], pattern=[[P, KC]], base=0, channel_multiplier=1,
                      allow_small_or_imprecise_dtypes=True).then_inc(ident_made, 1)
            pool.memset(ident[:], 0.0).then_inc(ident_cleared, 1)
            pool.wait_ge(ident_cleared, 1)
            pool.affine_select(out=ident[:], in_=ident[:], compare_op=ALU.not_equal, fill=1.0, base=0,
                               pattern=[[-1, P]], channel_multiplier=1).then_inc(ident_made, 1)
            split_wq_lo_parts(1)
            split_lo(wk_raw, wk_hi, wk_lo, wk_hi_done, 1, wk_lo_done)
            pool.wait_ge(tables_hi_done, 1)
            pool.tensor_tensor(tables_lo, tables_raw, tables_hi, ALU.subtract).then_inc(tables_lo_done, 1)
            split_lo(wv_raw, wv_hi, wv_lo, wv_hi_done, 1, wv_lo_done)
            pool.wait_ge(ctx_lo_done, 1)
            pool.memset(probs_t[:], 0.0).then_inc(zeros_made, 1)
            pool.wait_ge(row_in, 16)
            add_bias(0)
            add_bias(1)
            attention(0)

            pool.wait_ge(row_in, 32)
            add_bias(2)
            add_bias(3)
            split_wq_lo_parts(L1_SET + 1)
            split_lo(wk_raw, wk_hi, wk_lo, wk_hi_done, L1_SET + 1, wk_lo_done)
            split_lo(wv_raw, wv_hi, wv_lo, wv_hi_done, L1_SET + 1, wv_lo_done)
            attention(1)

            pool.wait_ge(pp_ready, 1)
            for h in range(2):
                if h:
                    pool.wait_ge(pre_sum, 3)
                by_stream = (wq_raw, wo_raw)[h][:].rearrange("p t (n c) -> p t n c", c=P)
                pool.tensor_tensor(q[:].rearrange("p t (n c) -> p t n c", c=P), by_stream,
                                   halves(logits, h)[:, :, 16:20].unsqueeze(3).broadcast_to([P, HT, STREAMS, P]), ALU.mult)\
                    .then_inc(pre_sum, 1)
                pool.wait_ge(pre_sum, 3 * h + 1)
                pool.tensor_tensor(q[:, :, 0:2 * P], q[:, :, 0:2 * P], q[:, :, 2 * P:], ALU.add).then_inc(pre_sum, 1)
                pool.wait_ge(pre_sum, 3 * h + 2)
                pool.tensor_tensor(rot[:, h, :].rearrange("p (t n) -> p t n", n=P), q[:, :, 0:P], q[:, :, P:2 * P], ALU.add)\
                    .then_inc(pre_sum, 1)
            for h in range(2):
                pool.wait_ge(y_out, h + 1)
                if h:
                    pool.wait_ge(y_added, 1)
                pool.tensor_tensor(probs_t[:].rearrange("p a b (n c) -> p a (b n) c", c=P),
                                   sin[:, half(h)].rearrange("p (t c) -> p t c", c=P).unsqueeze(2).broadcast_to([P, HT, STREAMS, P]),
                                   halves(logits, h)[:, :, 20:24].unsqueeze(3).broadcast_to([P, HT, STREAMS, P]), ALU.mult)\
                    .then_inc(y_terms, 1)
                pool.wait_ge(y_terms, h + 1)
                pool.tensor_tensor(x[:, h * HT:(h + 1) * HT, :], x[:, h * HT:(h + 1) * HT, :],
                                   probs_t[:].rearrange("p a b n -> p a (b n)"), ALU.add).then_inc(y_added, 1)
            last = TILES - 1
            pool.wait_ge(h_ready, 1)
            for i, terms in enumerate(pool_terms):
                pool.tensor_tensor(terms.rearrange("p j (i c) -> p j i c", c=P),
                                   wo_raw[:, last - HT, i * 2 * P:(i + 1) * 2 * P].rearrange("p (j c) -> p j c", c=P)
                                   .unsqueeze(2).broadcast_to([P, 2, STREAMS, P]),
                                   K[:, last, :, 2 * i:2 * i + 2].rearrange("p i j -> p j i").unsqueeze(3)
                                   .broadcast_to([P, 2, STREAMS, P]), ALU.mult).then_inc(pool_order, 1)
            pool.wait_ge(pool_order, 2)
            pool.tensor_tensor(pool_terms[0], pool_terms[0], pool_terms[1], ALU.add).then_inc(pool_order, 1)
            pool.wait_ge(pool_order, 3)
            pool.tensor_tensor(pool_terms[0][:, 0], pool_terms[0][:, 0], pool_terms[0][:, 1], ALU.add).then_inc(pool_order, 1)
            pool.wait_ge(pool_order, 4)
            pool.tensor_tensor(x[:, last, :], x[:, last, :], pool_terms[0][:, 0], ALU.add).then_inc(pool_order, 1)

        @block.vector
        def _(dve):
            def norm_stats(m, t):
                tile = HT * (m % 2) + t
                if m and t == 0:
                    dve.wait_ge(norm_order, (2 * HT + 1) * m)
                    dve.wait_ge(z_nat_ready, HT * m)
                if m < 2:
                    dve.wait_ge(x_in[m % 2], 16)
                elif m in (4, 5):
                    dve.wait_ge(ffn_added, tile + 1)
                else:
                    dve.wait_ge(att[m // 4]["o_added"], 8 * GROUPS - 2 * HT + tile + 1)
                dve.bn_stats(stats[:, t, :], x[:, tile, :]).then_inc(norm_order, 1)

            def norm_finish(m):
                base = (2 * HT + 1) * m
                if m == 6:
                    dve.wait_ge(wq_lo_done, L1_SET + GROUPS)
                if m == 7:
                    dve.wait_ge(wo_lo_done, 2 * GROUPS)
                for t in range(HT):
                    dve.wait_ge(norm_order, base + t + 1)
                    dve.bn_aggr(mean_var[:, t, :], stats[:, t, :]).then_inc(norm_order, 1)
                dve.wait_ge(norm_order, base + 2 * HT)
                dve.tensor_scalar(rstd[:], mean_var[:, :, 1], LN_EPS, None, ALU.add).then_inc(var_ready, 1)
                dve.wait_ge(std_ready, m + 1)
                dve.reciprocal(rstd[:], rstd[:]).then_inc(norm_order, 1)
                dve.wait_ge(norm_order, base + 2 * HT + 1)
                for t in range(HT):
                    dve.tensor_scalar(z_nat_of[m][:, t, :], x[:, HT * (m % 2) + t, :], mean_var[:, t, 0:1], rstd[:, t:t + 1],
                                      ALU.subtract, ALU.mult).then_inc(z_nat_ready, 1)

            def norm_nat(m):
                for t in range(HT):
                    norm_stats(m, t)
                norm_finish(m)

            def norm_lo(m, tiles=range(HT)):
                for t in tiles:
                    dve.wait_ge(z_hi_ready, HT * m + t + 1)
                    cols = tok(HT * (m % 2) + t)
                    dve.tensor_tensor(z_lo[:, :, cols], scores[:, t % 2, :].rearrange("p (c n) -> p c n", c=KC),
                                      z_hi[:, :, cols], ALU.subtract).then_inc(z_split, 1)

            def turn_qk(a, idx, parity_bank, parity, h, products=range(5)):
                for i in products:
                    b = (parity + i) % 2
                    src = bank(parity_bank, 1 + i)
                    dve.wait_ge(a["qk_ready"], idx + i + 1)
                    if not (isinstance(idx, int) and idx + i < 2):
                        dve.wait_ge(a["qk_out"], idx + i - 1)
                    dve.tensor_tensor(rot[:, b, :], src, cos[:, half(h)], ALU.mult)
                    dve.tensor_tensor(rot[0:64, 2 + b, :], src[64:128, :], sin[64:128, half(h)], ALU.mult)
                    dve.tensor_tensor(rot[64:128, 2 + b, :], src[0:64, :], sin[0:64, half(h)], ALU.mult)\
                        .then_inc(a["qk_read"], 1)

            def add_out(a, s, h_prev, tiles=range(HT), norm=None):
                for i in tiles:
                    tile = HT * h_prev + i
                    dve.wait_ge(a["op_ready"], s * 4 - 4 + i + 1)
                    dve.tensor_tensor(x[:, tile, :], bank(1 - h_prev, 7 + i), x[:, tile, :], ALU.add).then_inc(a["o_added"], 1)
                    if norm is not None:
                        norm_stats(norm, i)

            def step(a, g, h, first=False, last=False):
                s = g * 2 + h
                for hp in range(2):
                    dve.wait_ge(a["scores_ready"], s * 2 + hp + 1)
                    if layer_of(a):
                        dve.memset(row_max_sb[:, hp, :], 0.0)
                        dve.copy_predicated(scores[:, hp, :], masked_out[:, h * HB:(h + 1) * HB, :].rearrange("p b k -> p (b k)"),
                                            masked_value[:].broadcast_to([P, HB * S])).then_inc(a["masked"], 1)
                        dve.wait_ge(a["masked"], s * 2 + hp + 1)
                    dve.tensor_reduce(row_max_sb[:, hp, :], scores[:, hp, :].rearrange("p (b k) -> p b k", k=S), AX.X, ALU.max)\
                        .then_inc(a["row_max"], 1)
                for hp in range(2):
                    dve.wait_ge(a["row_max"], s * 2 + hp + 1)
                    if not first:
                        dve.wait_ge(a["pt_ready"], s * 2)
                    dve.tensor_tensor(probs[:, hp], scores[:, hp, :].rearrange("p (b k) -> p b k", k=S),
                                      row_max_sb[:, hp, :].unsqueeze(2).broadcast_to([P, HB, S]), ALU.subtract)\
                        .then_inc(a["shifted"], 1)
                for hp in range(2):
                    dve.wait_ge(a["exp_done"], s * 2 + hp + 1)
                    dve.tensor_reduce(row_sum_sb[:, hp, :], probs[:, hp], AX.X, ALU.add).then_inc(a["row_sum"], 1)
                for hp in range(2):
                    dve.wait_ge(a["row_sum"], s * 2 + hp + 1)
                    if not first:
                        dve.wait_ge(a["probs_ready"], s * 2)
                    dve.reciprocal(row_inv_sb[:, hp, :], row_sum_sb[:, hp, :]).then_inc(a["row_inv"], 1)
                if layer_of(a) and not last:
                    turn_qk(a, s * 5 + 5, h, 1 - h, 1 - h)
                if last:
                    add_out(a, s, 0, norm=4 * layer_of(a) + 2)
                dve.wait_ge(a["pt_ready"], s * 2 + 2)
                for second in range(2):
                    dve.tensor_copy(probs_t_of(1, second),
                                    scores[S * second:S * second + S, 1, :].rearrange("p (b n) -> p b n", b=PAIRS))\
                        .then_inc(a["pt_out_dve"], 1)
                if last:
                    norm_finish(4 * layer_of(a) + 2)
                elif not first:
                    add_out(a, s, 1 - h)
                for b in range(PAIRS):
                    dve.wait_ge(a["o_hi_ready"], s * 4 + b + 1)
                    dve.tensor_tensor(o_view(o_lo, b), bank(h, 11 + b).rearrange("p (b h q) -> p b h q", b=2, h=GH),
                                      o_view(o_hi, b), ALU.subtract).then_inc(a["o_split"], 1)

            def attention(layer):
                a = att[layer]
                if layer:
                    turn_qk(a, 0, 1, 0, 0, (0, 1, 2, 3))
                    norm_lo(5, (0, 1))
                    turn_qk(a, 0, 1, 0, 0, (4,))
                    norm_lo(5, (2, 3))
                else:
                    norm_nat(0)
                    norm_lo(0)
                    clamp_positions()
                    split_ctx_lo(0)
                    make_one_hots()
                    norm_nat(1)
                    norm_lo(1)
                    split_ctx_lo(1)
                    dve.wait_ge(mask_in, 32)
                    dve.tensor_scalar(masked_out[:], probs[:].bitcast(I32).rearrange("p a b k -> p (a b) k"), 0, None,
                                      ALU.is_equal).then_inc(mask_done, 1)
                dve.wait_ge(mask_done, 2)
                step(a, 0, 0, first=True)
                if not layer:
                    dve.wait_ge(bias_added, TILES)
                step(a, 0, 1)
                with dve.Fori(1, GROUPS - 1) as g:
                    step(a, g, 0)
                    step(a, g, 1)
                step(a, GROUPS - 1, 0)
                step(a, GROUPS - 1, 1, last=True)
                for tiles in ((0, 1), (2, 3)):
                    norm_lo(4 * layer + 2, tiles)
                    add_out(a, 2 * GROUPS, 1, tiles, norm=4 * layer + 3)
                norm_finish(4 * layer + 3)

            def make_one_hots():
                dve.wait_ge(pos_order, 4)
                dve.wait_ge(ident_made, 1)
                for c in range(KC):
                    dve.tensor_scalar(one_hots(c), sin[:], pos_col[:, c:c + 1], None, ALU.is_equal).then_inc(onehot_ready, 1)

            def clamp_positions():
                dve.wait_ge(pos_in, 16)
                dve.tensor_copy(sin[:], cos[:].bitcast(I32)).then_inc(pos_order, 1)
                dve.wait_ge(pos_order, 1)
                dve.tensor_scalar(cos[:], sin[:], 0.0, float(MAX_POS), ALU.is_lt, ALU.mult).then_inc(pos_order, 1)
                dve.wait_ge(pos_order, 2)
                dve.tensor_tensor(sin[:], sin[:], cos[:], ALU.add).then_inc(pos_order, 1)
                dve.wait_ge(pos_order, 3)
                dve.tensor_scalar(sin[:], sin[:], 0.0, float(MAX_POS - 1), ALU.max, ALU.min).then_inc(pos_order, 1)

            def split_ctx_lo(h):
                raw = wo_raw[:] if h else probs_t[:].rearrange("p a b n -> p a (b n)")
                dve.wait_ge(ctx_hi_done, h + 1)
                dve.tensor_tensor(ctx_lo[:, :, half(h)], raw, ctx_hi[:, :, half(h)], ALU.subtract).then_inc(ctx_lo_done, 1)

            dve.memset(masked_value[:], MASKED).then_inc(mask_done, 1)
            attention(0)

            def gating(h):
                wide = v[:].rearrange("p t (e r) -> p t e r", r=RANK)
                w, wt = gate_w[:, :, 0:EXPERTS], gate_w[:, :, EXPERTS:EXPERTS + 1]
                top, thr, total = (gate_s[:, :, i:i + 1] for i in (0, 1, 2))

                def over_experts(ap):
                    return ap.broadcast_to([P, HT, EXPERTS])

                n = 14 * h
                dve.wait_ge(gate_cols, h + 1)
                dve.tensor_copy(gate_w[:], ring[:, 3, :].rearrange("p (t n) -> p t n", n=P)[:, :, 0:EXPERTS + 1]).then_inc(gate_order, 1)
                dve.wait_ge(gate_order, n + 1)
                dve.tensor_reduce(top, w, AX.X, ALU.max).then_inc(gate_order, 1)
                dve.wait_ge(gate_order, n + 2)
                dve.tensor_tensor(w, w, over_experts(top), ALU.subtract).then_inc(gate_order, 1)
                dve.tensor_scalar(wt, wt, scalars[:, 0:1], -1.0, ALU.add, ALU.mult).then_inc(gate_order, 1)
                dve.wait_ge(gate_order, n + 4)
                dve.tensor_copy(top, top).then_inc(gate_exp_in, 1)
                dve.wait_ge(gate_exp_out, h + 1)
                dve.tensor_reduce(total, w, AX.X, ALU.add).then_inc(gate_order, 1)
                dve.tensor_scalar(thr, wt, 1.0, None, ALU.add).then_inc(gate_order, 1)
                dve.wait_ge(gate_order, n + 6)
                dve.reciprocal(gate_s[:, :, 1:3], gate_s[:, :, 1:3]).then_inc(gate_order, 1)
                dve.wait_ge(gate_order, n + 7)
                dve.tensor_tensor(w, w, over_experts(total), ALU.mult).then_inc(gate_order, 1)
                dve.wait_ge(gate_order, n + 8)
                dve.scalar_tensor_tensor(out=w, in0=over_experts(thr), scalar=-0.125, in1=w, op0=ALU.mult, op1=ALU.add)\
                    .then_inc(gate_order, 1)
                dve.wait_ge(gate_order, n + 9)
                dve.tensor_scalar(w, w, 0.0, None, ALU.max).then_inc(gate_order, 1)
                dve.wait_ge(gate_order, n + 10)
                dve.tensor_reduce(total, w, AX.X, ALU.add).then_inc(gate_order, 1)
                dve.wait_ge(gate_order, n + 11)
                dve.scalar_tensor_tensor(out=total, in0=total, scalar=0.0, in1=total, op0=ALU.is_equal, op1=ALU.add)\
                    .then_inc(gate_order, 1)
                dve.wait_ge(gate_order, n + 12)
                dve.reciprocal(total, total).then_inc(gate_order, 1)
                dve.wait_ge(gate_order, n + 13)
                dve.scalar_tensor_tensor(out=w, in0=w, scalar=2.0, in1=over_experts(total), op0=ALU.mult, op1=ALU.mult)\
                    .then_inc(gate_order, 1)
                dve.wait_ge(gate_order, n + 14)
                dve.tensor_copy(wide, w.unsqueeze(3).broadcast_to([P, HT, EXPERTS, RANK])).then_inc(gate_wide, 1)

            dve.wait_ge(small_in, 48)
            for h in range(2):
                gating(h)
                norm_lo(3 + h, (0, 1))
                dve.wait_ge(gate_wide_t, h + 1)
                if h:
                    dve.wait_ge(ffn_sum, HT)
                dve.tensor_tensor(rot[:, 0, :], ring[:, 2, :], k[:], ALU.mult).then_inc(hw_ready, 1)
                norm_lo(3 + h, (2, 3))
                for t in range(HT):
                    tile = HT * h + t
                    dve.wait_ge(ffn_sum, tile + 1)
                    dve.wait_ge(bias_added, TILES + tile + 1)
                    dve.tensor_tensor(x[:, tile, :], ring[:, (4, 5, 0, 1)[t], :], x[:, tile, :], ALU.add).then_inc(ffn_added, 1)
                    norm_stats(4 + h, t)
                norm_finish(4 + h)

            attention(1)

            norm_lo(7)
            dve.wait_ge(sq_done, TILES)
            dve.tensor_scalar(rms[:], rms[:], 1.0 / D, RMS_EPS, ALU.mult, ALU.add).then_inc(ms_ready, 1)
            dve.wait_ge(rms_root, 1)
            dve.reciprocal(rms[:], rms[:]).then_inc(mix_order, 1)
            dve.wait_ge(mix_order, 1)
            for h in range(2):
                dve.wait_ge(mix_cols, h + 1)
                dve.tensor_tensor(halves(logits, h), ring[:, 1 + h, :].rearrange("p (t n) -> p t n", n=P)[:, :, 0:24],
                                  halves(rms, h).unsqueeze(2).broadcast_to([P, HT, 24]), ALU.mult).then_inc(mix_order, 1)
            dve.wait_ge(mix_order, 3)
            dve.tensor_tensor(logits[:], logits[:], mix_base_sb[:].unsqueeze(1).broadcast_to([P, TILES, 24]), ALU.add)\
                .then_inc(mix_order, 1)
            dve.wait_ge(mix_order, 4)
            lp = logits[:, :, 16:24].rearrange("p t (a n) -> p t a n", n=STREAMS)
            pp4 = pp[:].unsqueeze(3).broadcast_to([P, TILES, 2, STREAMS])
            dve.tensor_scalar(Z.rearrange("p t i j -> p t (i j)"), logits[:, :, 0:16], 1.0 / TAU, None, ALU.mult).then_inc(mix_order, 1)
            dve.memset(fac[:], 1.0).then_inc(mix_order, 1)
            dve.tensor_reduce(pp[:], lp, AX.X, ALU.max).then_inc(mix_order, 1)
            dve.wait_ge(mix_order, 7)
            dve.tensor_tensor(lp, lp, pp4, ALU.subtract).then_inc(pp_exp_in, 1)
            dve.wait_ge(pp_exp_out, 1)
            dve.tensor_reduce(pp[:], lp, AX.X, ALU.add).then_inc(mix_order, 1)
            dve.wait_ge(mix_order, 8)
            dve.reciprocal(pp[:], pp[:]).then_inc(mix_order, 1)
            dve.wait_ge(mix_order, 9)
            dve.tensor_tensor(lp, lp, pp4, ALU.mult).then_inc(pp_ready, 1)
            dve.wait_ge(gate_scalar, 1)
            dve.tensor_scalar(scalars[:, 1:2], scalars[:, 1:2], 1.0, None, ALU.add).then_inc(mix_order, 1)
            dve.wait_ge(mix_order, 10)
            dve.reciprocal(scalars[:, 1:2], scalars[:, 1:2]).then_inc(mix_order, 1)
            dve.wait_ge(mix_order, 11)
            dve.tensor_scalar(scalars[:, 2:3], scalars[:, 1:2], -1.0, 1.0, ALU.mult, ALU.add).then_inc(mix_order, 1)

            def level(after, levels, done, build):
                for h in range(2):
                    dve.wait_ge(after, levels * 2 - 1 + h)
                    build(h).then_inc(done, 1)

            dve.wait_ge(mix_order, 12)
            for side in range(2):
                view = turned if side else (lambda ap: ap)
                over = over_rows if side else over_cols
                src = T if side else Z
                if side:
                    level(sink_order, 2, sink_order,
                          lambda h: dve.tensor_tensor(halves(T, h), halves(Z, h), over_cols(halves(lse[:, 0], h)), ALU.add))
                    level(sink_order, 3, sink_order,
                          lambda h: dve.tensor_reduce(halves(red[:, 0], h), turned(halves(T, h)), AX.X, ALU.max))
                else:
                    for h in range(2):
                        dve.tensor_reduce(halves(red[:, 0], h), halves(Z, h), AX.X, ALU.max).then_inc(sink_order, 1)
                level(sink_order, 3 * side + 1, sink_to_act,
                      lambda h: dve.tensor_tensor(halves(T, h), halves(src, h), over(halves(red[:, 0], h)), ALU.subtract))
                level(sink_from_act, 2 * side + 1, sink_to_act,
                      lambda h: dve.tensor_reduce(halves(red[:, 1], h), view(halves(K, h)), AX.X, ALU.add))
                level(sink_from_act, 2 * side + 2, sink_order,
                      lambda h: dve.scalar_tensor_tensor(out=halves(lse[:, side], h), in0=halves(red[:, 0], h), scalar=-1.0,
                                                         in1=halves(red[:, 1], h), op0=ALU.mult, op1=ALU.subtract))

            def iteration(base):
                for side in range(2):
                    view = turned if side else (lambda ap: ap)
                    over_other = over_cols if side else over_rows
                    level(sink_order, base + 3 * side, sink_order,
                          lambda h: dve.tensor_tensor(halves(T, h), halves(K, h), over_other(halves(fac[:, 1 - side], h)), ALU.mult))
                    level(sink_order, base + 3 * side + 1, sink_order,
                          lambda h: dve.tensor_reduce(halves(red[:, side], h), view(halves(T, h)), AX.X, ALU.add))
                    level(sink_order, base + 3 * side + 2, sink_order,
                          lambda h: dve.reciprocal(halves(fac[:, side], h), halves(red[:, side], h)))

            with dve.Fori(0, SEGMENTS) as c:
                base = c * SEGMENT_LEVELS + START_LEVELS
                level(sink_from_act, c * 2 + 5, sink_order,
                      lambda h: dve.tensor_tensor(lse[:, :, h * HT:(h + 1) * HT], lse[:, :, h * HT:(h + 1) * HT],
                                                  fac[:, :, h * HT:(h + 1) * HT], ALU.add))
                level(sink_order, base + 1, sink_order,
                      lambda h: dve.tensor_tensor(halves(T, h), halves(Z, h), over_cols(halves(lse[:, 0], h)), ALU.add))
                level(sink_order, base + 2, sink_to_act,
                      lambda h: dve.tensor_tensor(halves(T, h), halves(T, h), over_rows(halves(lse[:, 1], h)), ALU.add))
                level(sink_from_act, c * 2 + 6, sink_order, lambda h: dve.memset(halves(fac[:, 1], h), 1.0))
                with dve.Fori(0, ROUNDS) as r:
                    for i in range(ROUND):
                        iteration(c * SEGMENT_LEVELS + (r * (6 * ROUND) + (START_LEVELS + 3 + 6 * i)))
            done = START_LEVELS + SEGMENTS * SEGMENT_LEVELS
            iteration(done)
            level(sink_order, done + 6, sink_order,
                  lambda h: dve.tensor_tensor(halves(K, h), halves(T, h), over_rows(halves(fac[:, 1], h)), ALU.mult))
            level(sink_order, done + 7, sink_order,
                  lambda h: dve.tensor_scalar(halves(K, h), halves(K, h), scalars[:, 1:2], None, ALU.mult))
            dve.wait_ge(sink_order, 2 * (done + 8))
            dve.wait_ge(y_added, 2)
            diagonal = K.rearrange("p t i j -> p t (i j)")[:, :, 0:STREAMS * STREAMS:STREAMS + 1]
            dve.tensor_scalar(diagonal, diagonal, scalars[:, 2:3], None, ALU.add).then_inc(h_ready, 1)
            dve.wait_ge(h_ready, 1)
            for t in range(DVE_TILES):
                for j in range(STREAMS):
                    for i in range(STREAMS):
                        count = (t * STREAMS + j) * STREAMS + i
                        if j:
                            dve.wait_ge(mixed, count - STREAMS + 1)
                        dve.scalar_tensor_tensor(out=x[:, t, tok(i)], in0=wq_raw[:, t, tok(j)],
                                                 scalar=K[:, t, i, j:j + 1], in1=x[:, t, tok(i)],
                                                 op0=ALU.mult, op1=ALU.add).then_inc(mixed, 1)


def rotary_tables():
    inv = (np.float32(1.0) / np.float32(10000.0) ** (np.arange(0, DH, 2, dtype=np.float32) / np.float32(DH))).astype(np.float32)
    angle = np.arange(MAX_POS, dtype=np.float32)[:, None] * inv[None, :]
    c, s = np.cos(angle).astype(np.float32), np.sin(angle).astype(np.float32)
    return np.ascontiguousarray(np.concatenate([c, c, s, -s], axis=1))


def kernel(**inputs):
    import concourse.bacc as bacc
    from concourse.bass_utils import run_bass_kernel_spmd

    a = {name: np.asarray(value) for name, value in inputs.items()}
    bkv = a["L0_xattn_bkv"].reshape(2, GROUPS, 1, DH)
    bqkv0 = np.concatenate([a["L0_xattn_bq"].reshape(GROUPS, GH, DH), bkv[0], bkv[1]], axis=1).transpose(2, 0, 1).reshape(DH, -1)
    arrays = {
        "x": a["x"].reshape(NT, D),
        "ctx_t": a["ctx_4096"].reshape(NT, D).T,
        "pos": a["pos_BxS2"].reshape(NT),
        "mask": a["mask_BxSxS2_ik0"],
        "wq0": a["L0_xattn_Wq"], "bqkv0": bqkv0,
        "wkv0": a["L0_xattn_Wkv"],
        "wo0": a["L0_xattn_Wo"], "bo0": a["L0_xattn_bo"],
        "wbase_t": a["L0_ffn_W_base"].T, "bbase": a["L0_ffn_b_base"],
        "gates_t": np.concatenate([a["L0_ffn_W_gate"], a["L0_ffn_W_thr"]]).T,
        "b_thr": a["L0_ffn_b_thr"],
        "a_t": a["L0_ffn_A"].reshape(EXPERTS * RANK, D).T,
        "b_mat": a["L0_ffn_B"].transpose(0, 2, 1).reshape(EXPERTS * RANK, D),
        "wq1": a["L1_xattn_Wq"], "wk1": a["L1_xattn_Wk"], "wv1": a["L1_xattn_Wv"], "wo1": a["L1_xattn_Wo"],
        "mix_t": np.concatenate([a["L1_ffn_W_res"], a["L1_ffn_W_pre"], a["L1_ffn_W_post"]]).T,
        "mix_base": np.concatenate([a["L1_ffn_H_res_base"].reshape(-1), a["L1_ffn_H_pre_base"], a["L1_ffn_H_post_base"]]),
        "gate": a["L1_ffn_gate"], "w_branch": a["L1_ffn_W_branch"],
        "tables": rotary_tables(),
    }
    arrays = {f"in_{name}": np.ascontiguousarray(value) for name, value in arrays.items()}
    nc = bacc.Bacc("TRN2", target_bir_lowering=False, num_devices=1)
    args = [nc.dram_tensor(name, v.shape, mybir.dt.from_np(v.dtype), kind="ExternalInput").ap() for name, v in arrays.items()]
    out = nc.dram_tensor("out_x", (NT, D), F32, kind="ExternalOutput").ap()
    bass_two_layers(nc, *args, out)
    result = run_bass_kernel_spmd(nc, [arrays], core_ids=[0])
    return result.results[0]["out_x"].reshape(B, S, D)
```

```python
from contextlib import ExitStack

import numpy as np

import concourse.bass as bass
from concourse import mybir

ALU = mybir.AluOpType
ACT = mybir.ActivationFunctionType
AX = mybir.AxisListType
F32 = mybir.dt.float32
F32R = mybir.dt.float32r
I32 = mybir.dt.int32
U8 = mybir.dt.uint8

P = 128
B, S = 16, 64
D = 512
NT = B * S
TILES = NT // P
HALF = NT // 2
HT = TILES // 2
HB = B // 2
KC = D // P
GROUPS, GH, DH = 8, 4, 128
PAIRS = HB // 2
EXPERTS, RANK = 8, 16
STREAMS, CH = 4, 128
MAX_POS = 512
SCALE = 1.0 / float(np.sqrt(np.float32(DH)))
MASKED = float(np.float32(-1e9) * np.sqrt(np.float32(DH)))
LN_EPS = 1e-5
RMS_EPS = 1.1920929e-07
TAU = 0.1
DVE_TILES, ACT_TILES = 4, 3
REFRESHES, ROUNDS, ROUND, LAST_ROUND = 2, 2, 8, 2
START_LEVELS = 4
ROUNDS_LEVELS = 6 * ROUNDS * ROUND
SEGMENT_LEVELS = ROUNDS_LEVELS + 3
RING = 6
FOUR_BANKS = {0: (0, 1), 7: (3, 4)}
FFN0_SET = GROUPS
L1_SET = GROUPS + 1


def bass_two_layers(nc, x_in_ap, ctx_t, pos, mask, wq0, bqkv0, wkv0, wo0, bo0, wbase_t, bbase, gates_t,
                    b_thr, a_t, b_mat, wq1, wk1, wv1, wo1, mix_t, mix_base, gate, w_branch, tables, out):
    with ExitStack() as ctx:
        def sb(name, shape, dt=F32):
            return ctx.enter_context(nc.sbuf_tensor(name, shape, dt))

        def sem(name):
            return ctx.enter_context(nc.semaphore(name))

        x = sb("x", [P, TILES, D])
        ctx_hi = sb("ctx_hi", [P, KC, NT], F32R)
        ctx_lo = sb("ctx_lo", [P, KC, NT], F32R)
        z_hi = sb("z_hi", [P, KC, NT], F32R)
        z_lo = sb("z_lo", [P, KC, NT], F32R)
        wq_raw, wq_hi, wq_lo = sb("wq_raw", [P, KC, D]), sb("wq_hi", [P, KC, D], F32R), sb("wq_lo", [P, KC, D], F32R)
        wk_raw, wk_hi, wk_lo = sb("wk_raw", [P, KC, DH]), sb("wk_hi", [P, KC, DH], F32R), sb("wk_lo", [P, KC, DH], F32R)
        wv_raw, wv_hi, wv_lo = sb("wv_raw", [P, KC, DH]), sb("wv_hi", [P, KC, DH], F32R), sb("wv_lo", [P, KC, DH], F32R)
        wo_raw, wo_hi, wo_lo = sb("wo_raw", [P, GH, D]), sb("wo_hi", [P, GH, D], F32R), sb("wo_lo", [P, GH, D], F32R)
        q = sb("q", [P, GH, HALF])
        k = sb("k", [P, HALF])
        v_t = sb("v_t", [P, HALF])
        v_hi = sb("v_hi", [P, PAIRS, DH], F32R)
        v_lo = sb("v_lo", [P, PAIRS, DH], F32R)
        probs = sb("probs", [P, 2, HB, S])
        probs_t_hi = sb("probs_t_hi", [P, PAIRS, 2, GH * S], F32R)
        probs_t_lo = sb("probs_t_lo", [P, 2, 2, GH * S], F32R)
        o_hi = sb("o_hi", [P, GH, HALF], F32R)
        o_lo = sb("o_lo", [P, GH, HALF], F32R)
        row_max_sb = sb("row_max_sb", [P, 2, HB])
        row_sum_sb = sb("row_sum_sb", [P, 2, HB])
        row_inv_sb = sb("row_inv_sb", [P, 2, HB])
        cos = sb("cos", [P, NT])
        sin = sb("sin", [P, NT])
        rot = sb("rot", [P, 4, HALF])
        masked_out = sb("masked_out", [P, B, S], U8)
        masked_value = sb("masked_value", [P, 1])
        ident = sb("ident", [P, P])
        qk_bias = sb("qk_bias", [P, GH + 1])
        v_bias = sb("v_bias", [P, 2])
        pos_col = sb("pos_col", [P, KC])
        stats = sb("stats", [P, HT, 6])
        mean_var = sb("mean_var", [P, HT, 2])
        rstd = sb("rstd", [P, HT])

        gate_w = sb("gate_w", [P, HT, EXPERTS + 1])
        gate_s = sb("gate_s", [P, HT, 4])
        logits = sb("logits", [P, TILES, 24])
        mix_base_sb = sb("mix_base_sb", [P, 24])
        rms = sb("rms", [P, TILES])
        pp = sb("pp", [P, TILES, 2])
        scalars = sb("scalars", [P, 4])

        ring = ctx.enter_context(nc.psum_tensor("ring", [P, RING, 512], F32))
        scores = ctx.enter_context(nc.psum_tensor("scores", [P, 2, 512], F32))

        ident_cleared, ident_made = sem("ident_cleared"), sem("ident_made")
        x_in = [sem(f"x_in{h}") for h in range(2)]
        ctx_in = [sem(f"ctx_in{h}") for h in range(2)]
        tables_in, pos_in, mask_in, small_in = sem("tables_in"), sem("pos_in"), sem("mask_in"), sem("small_in")
        row_in = sem("row_in")
        wq_in, wk_in, wv_in, wo_in = sem("wq_in"), sem("wk_in"), sem("wv_in"), sem("wo_in")
        wq_hi_done, wk_hi_done, wv_hi_done, wo_hi_done = [sem(f"w{c}_hi_done") for c in "qkvo"]
        wq_lo_done, wk_lo_done, wv_lo_done, wo_lo_done = [sem(f"w{c}_lo_done") for c in "qkvo"]
        wq_hi_part, wq_lo_part = sem("wq_hi_part"), sem("wq_lo_part")
        qk_bias_in, v_bias_in = sem("qk_bias_in"), sem("v_bias_in")
        pads_made = sem("pads_made")
        ctx_hi_done, ctx_lo_done = sem("ctx_hi_done"), sem("ctx_lo_done")
        zeros_made = sem("zeros_made")
        pos_order, onehot_ready, tables_ready = sem("pos_order"), sem("onehot_ready"), sem("tables_ready")
        tables_hi_done, tables_lo_done = sem("tables_hi_done"), sem("tables_lo_done")
        tables_out, mask_done = sem("tables_out"), sem("mask_done")
        var_ready, std_ready, norm_order = sem("var_ready"), sem("std_ready"), sem("norm_order")
        z_nat_ready, zt_ready, z_hi_ready, z_split = [sem(n) for n in ("z_nat_ready", "zt_ready", "z_hi_ready", "z_split")]
        bias_added = sem("bias_added")
        base_done = sem("base_done")
        ffn_hg_ready, ffn_hg_out, gate_cols, gate_order = [
            sem(n) for n in ("ffn_hg_ready", "ffn_hg_out", "gate_cols", "gate_order")]
        gate_exp_in, gate_exp_out, gate_wide, gate_wide_t, hw_ready, ffn_sum, ffn_added = [
            sem(n) for n in ("gate_exp_in", "gate_exp_out", "gate_wide", "gate_wide_t", "hw_ready", "ffn_sum", "ffn_added")]
        sq_done, ms_ready, rms_root = sem("sq_done"), sem("ms_ready"), sem("rms_root")
        mix_ready, mix_out, mix_cols, mix_order = [sem(n) for n in ("mix_ready", "mix_out", "mix_cols", "mix_order")]
        pp_exp_in, pp_exp_out, pp_ready, gate_scalar = [
            sem(n) for n in ("pp_exp_in", "pp_exp_out", "pp_ready", "gate_scalar")]
        sink_order, sink_to_act, sink_from_act = sem("sink_order"), sem("sink_to_act"), sem("sink_from_act")
        pre_sum, pre_t_ready, pre_t_out, y_ready, y_out, y_terms, y_added = [
            sem(n) for n in ("pre_sum", "pre_t_ready", "pre_t_out", "y_ready", "y_out", "y_terms", "y_added")]
        h_ready, mixed = sem("h_ready"), sem("mixed")
        act_terms, act_sum, act_mixed = sem("act_terms"), sem("act_sum"), sem("act_mixed")
        pool_order, out_done = sem("pool_order"), sem("out_done")

        att = [{n: sem(f"{n}{layer}") for n in (
            "scores_ready",
            "masked",
            "row_max",
            "shifted",
            "exp_done",
            "row_sum",
            "row_inv",
            "probs_ready",
            "pt_ready",
            "pt_hi_ready",
            "pt_split",
            "vt_ready",
            "vt_out",
            "vtr_ready",
            "v_hi_ready",
            "v_split",
            "qk_ready",
            "qk_read",
            "qk_out",
            "pv_ready",
            "o_hi_ready",
            "o_split",
            "op_ready",
            "o_added",
        )} for layer in range(2)]

        def layer_of(a):
            return 1 if a is att[1] else 0

        def bank(s, j):
            return ring[:, (15 * (s % 2) + j) % RING, :]

        def turn_bank(m, t):
            return ring[:, FOUR_BANKS[m][t - 2], :] if m in FOUR_BANKS and t >= 2 else scores[:, t % 2, :]

        def tok(t):
            return slice(t * P, (t + 1) * P)

        def half(h):
            return slice(h * HALF, (h + 1) * HALF)

        def qk_done(a):
            return a["qk_out"] if layer_of(a) else a["qk_read"]

        probs_flat = probs[:].rearrange("p a b k -> p (a b k)")
        bias_rows = (v_t[:], probs_flat[:, 0:D])
        gate_wide_sb = probs_flat[:, D:].rearrange("p (t n) -> p t n", n=P)

        q_by_seq = q[:].rearrange("p a n -> p (a n)").rearrange("p (b h s) -> p b h s", b=HB, h=GH)

        def by_seq(ap):
            return ap.rearrange("p (b s) -> p b s", s=S)

        def o_view(o, b):
            return o[:, :, tok(b)].rearrange("p h (b q) -> p b h q", b=2)

        tables_hi, tables_lo = (w[:].rearrange("p h n -> p (h n)")[:, 0:KC * 2 * P] for w in (wo_hi, wo_lo))

        def one_hots(c):
            return (o_hi, o_lo)[c // 2][:, 2 * (c % 2):2 * (c % 2) + 2, :].rearrange("p a n -> p (a n)")

        def mix_term(i, j):
            return (cos, sin)[j // 2][:, half(j % 2)] if i % 2 else q[:, j, :]

        table_bank = [ring[:, b, :] for b in (1, 2, 3, 4)]
        z_nat_of = [q, rot, q, rot, q, wo_raw, wq_raw, wo_raw]
        Z, T, K = (rot[:, 2, i * P:(i + 1) * P].rearrange("p (t i j) -> p t i j", i=STREAMS, j=STREAMS) for i in range(3))
        lse = rot[:, 3, 0:2 * TILES * STREAMS].rearrange("p (a t n) -> p a t n", a=2, n=STREAMS)
        fac = rot[:, 3, 64:64 + 2 * TILES * STREAMS].rearrange("p (a t n) -> p a t n", a=2, n=STREAMS)
        red = rot[:, 3, 128:128 + 2 * TILES * STREAMS].rearrange("p (a t n) -> p a t n", a=2, n=STREAMS)

        pool_terms = [rot[:, 0:2, :], probs[:].rearrange("p a b k -> p a (b k)")]

        mix_bank = [ring[:, b, :] for b in (5, 0)]
        sum_bank = [ring[:, b, :] for b in (4, 5, 2)]

        def levels_done(c):
            return c * (2 * SEGMENT_LEVELS) + 2 * (START_LEVELS + ROUNDS_LEVELS)

        def halves(ap, h):
            return ap[:, h * HT:(h + 1) * HT]

        def over_rows(ap):
            return ap.unsqueeze(2).broadcast_to([P, HT, STREAMS, STREAMS])

        def over_cols(ap):
            return ap.unsqueeze(3).broadcast_to([P, HT, STREAMS, STREAMS])

        def turned(ap):
            return ap.rearrange("p t i j -> p t j i")

        block = ctx.enter_context(nc.Block())

        @block.sync
        def _(sp):
            wq_of = [w.rearrange("(c p) n -> p c n", p=P) for w in (wq0, wq1)]
            wk_of = [w.rearrange("(c p) n -> p c n", p=P) for w in (wkv0[:, 0:GROUPS * DH], wk1)]
            wv_of = [w.rearrange("(c p) n -> p c n", p=P) for w in (wkv0[:, GROUPS * DH:], wv1)]
            wo_of = [w.rearrange("(g h p) n -> p g h n", p=P, h=GH) for w in (wo0, wo1)]
            x_of = x_in_ap.rearrange("(t p) n -> p t n", p=P)
            out_of = out.rearrange("(t p) n -> p t n", p=P)
            ctx_of = ctx_t.rearrange("(c p) n -> p c n", p=P)

            def qkv_loads(layer):
                return ((wq_raw, wq_of[layer], D, wq_in, wq_lo_done),
                        (wk_raw, wk_of[layer], DH, wk_in, wk_lo_done),
                        (wv_raw, wv_of[layer], DH, wv_in, wv_lo_done))

            def load_w(raw, src, width, arrived, split, g, split_sets):
                if split_sets is not None:
                    sp.wait_ge(split, split_sets)
                sp.dma_start(raw[:], src[:, :, bass.ds(g * width, width)]).then_inc(arrived, 16)

            def load_qkv(layer, g, split_sets):
                for load in qkv_loads(layer):
                    load_w(*load, g, split_sets)

            def load_qk_bias(g):
                sp.dma_start(qk_bias[:], bqkv0[:, bass.ds(g * (GH + 2), GH + 1)]).then_inc(qk_bias_in, 16)

            def load_v_bias(g):
                sp.dma_start(v_bias[:], bqkv0[:, bass.ds(g * (GH + 2) + GH, 2)]).then_inc(v_bias_in, 16)

            def load_wo(layer, g):
                sp.dma_start(wo_raw[:], wo_of[layer][:, bass.ds(g, 1), :, :].rearrange("p a h n -> p (a h) n")).then_inc(wo_in, 16)

            sp.dma_start(x[:, 0:HT, :], x_of[:, 0:HT, :]).then_inc(x_in[0], 16)
            load_w(*qkv_loads(0)[0], 0, None)
            load_qk_bias(0)
            sp.dma_start(rot[:], ctx_of[:, :, half(0)]).then_inc(ctx_in[0], 16)
            sp.dma_start(cos[:].bitcast(I32), pos.partition_broadcast(P)).then_inc(pos_in, 16)
            load_w(*qkv_loads(0)[1], 0, None)
            sp.dma_start(probs_flat.rearrange("p (c n) -> p c n", c=KC), tables.rearrange("(c p) n -> p c n", p=P)).then_inc(tables_in, 16)
            sp.dma_start(x[:, HT:, :], x_of[:, HT:, :]).then_inc(x_in[1], 16)
            load_w(*qkv_loads(0)[2], 0, None)
            sp.dma_start(wo_raw[:], ctx_of[:, :, half(1)]).then_inc(ctx_in[1], 16)
            load_v_bias(0)
            sp.wait_ge(tables_lo_done, 1)
            for i in range(2):
                sp.dma_start(probs[S * i:S * i + S].bitcast(I32).rearrange("p a b k -> p (a b) k"),
                             mask.rearrange("b q k -> q b k")).then_inc(mask_in, 16)
            sp.wait_ge(ctx_lo_done, 2)
            load_wo(0, 0)
            with sp.Fori(1, GROUPS) as g:
                load_qkv(0, g, g)
                sp.wait_ge(att[0]["qk_read"], g * 10)
                load_qk_bias(g)
                sp.wait_ge(wo_lo_done, g)
                load_wo(0, g)
                sp.wait_ge(att[0]["vt_out"], g * 2)
                load_v_bias(g)
            sp.wait_ge(wq_lo_done, GROUPS)
            sp.dma_start(wq_raw[:], wbase_t.rearrange("(c p) n -> p c n", p=P)).then_inc(wq_in, 16)
            sp.wait_ge(wk_lo_done, GROUPS)
            sp.dma_start(wk_raw[:], a_t.rearrange("(c p) n -> p c n", p=P)).then_inc(wk_in, 16)
            sp.wait_ge(pads_made, 1)
            sp.dma_start(wv_raw[:, :, 0:EXPERTS + 1], gates_t.rearrange("(c p) n -> p c n", p=P)).then_inc(wv_in, 16)
            sp.wait_ge(wo_lo_done, GROUPS)
            sp.dma_start(wo_raw[:, 0, :], b_mat).then_inc(wo_in, 16)
            sp.wait_ge(att[0]["pt_ready"], 4 * GROUPS)
            sp.dma_start(bias_rows[1], bbase.partition_broadcast(P)).then_inc(row_in, 16)
            load_qkv(1, 0, L1_SET)
            sp.wait_ge(zt_ready, HT * 6)
            load_wo(1, 0)
            with sp.Fori(1, GROUPS) as g:
                load_qkv(1, g, g + L1_SET)
                sp.wait_ge(wo_lo_done, g + GROUPS)
                load_wo(1, g)
            sp.wait_ge(wk_lo_done, L1_SET + GROUPS)
            sp.dma_start(wk_raw[:, 0, :], w_branch).then_inc(wk_in, 16)
            sp.wait_ge(pads_made, 2)
            sp.dma_start(wv_raw[:, :, 0:24], mix_t.rearrange("(c p) n -> p c n", p=P)).then_inc(wv_in, 16)
            for t in (0, 4, 1, 7, 5, 2, 3, 6):
                if t < DVE_TILES:
                    sp.wait_ge(mixed, STREAMS * STREAMS * (t + 1))
                elif t < DVE_TILES + ACT_TILES:
                    sp.wait_ge(act_mixed, t - DVE_TILES + 1)
                else:
                    sp.wait_ge(pool_order, 5)
                sp.dma_start(out_of[:, t, :], x[:, t, :]).then_inc(out_done, 16)
            sp.wait_ge(out_done, 16 * TILES)

        @block.tensor
        def _(pe):
            def split_product(dst, hi_a, lo_a, hi_b, lo_b, stop=True):
                n = len(hi_a)
                for c in range(n):
                    pe.matmul(dst, hi_a[c], hi_b[c], start=(c == 0), stop=False)
                    pe.matmul(dst, hi_a[c], lo_b[c], start=False, stop=False)
                    last = pe.matmul(dst, lo_a[c], hi_b[c], start=False, stop=stop and c == n - 1)
                return last

            def chunks(w, cols=slice(0, DH)):
                return [w[:, c, cols] for c in range(w.shape[1])]

            def norm_turn(m, tiles=range(HT)):
                for t in tiles:
                    pe.wait_ge(z_nat_ready, HT * m + t + 1)
                    if m and not (m in FOUR_BANKS and t >= 2):
                        pe.wait_ge(z_split, HT * m + t - 1)
                    dst = turn_bank(m, t)
                    for c in range(KC):
                        last = pe.transpose(dst[:, tok(c)], z_nat_of[m][:, t, tok(c)], ident[:])
                    last.then_inc(zt_ready, 1)

            def project_qk(a, h, dst_of, new_set=None, previous=None, prologue=False):
                if new_set is not None and not prologue:
                    pe.wait_ge(wq_hi_done, new_set + 1)
                    pe.wait_ge(wq_lo_done, new_set + 1)
                for i in range(GH):
                    if prologue and layer_of(a):
                        pe.wait_ge(ffn_added, HT + i + 1)
                    if prologue and i < GH - 1:
                        pe.wait_ge(wq_hi_part, (GH - 1) * layer_of(a) + i + 1)
                        pe.wait_ge(wq_lo_part, (GH - 1) * layer_of(a) + i + 1)
                    elif prologue:
                        pe.wait_ge(wq_hi_done, new_set + 1)
                        pe.wait_ge(wq_lo_done, new_set + 1)
                    if previous is not None and i >= 1:
                        pe.wait_ge(a["o_split"], previous + i)
                    split_product(dst_of(1 + i), chunks(wq_hi, tok(i)), chunks(wq_lo, tok(i)),
                                  chunks(z_hi, half(h)), chunks(z_lo, half(h))).then_inc(a["qk_ready"], 1)
                if prologue and layer_of(a):
                    norm_turn(5, (0, 1))
                if new_set is not None:
                    pe.wait_ge(wk_hi_done, new_set + 1)
                    pe.wait_ge(wk_lo_done, new_set + 1)
                    pe.wait_ge(ctx_lo_done, 1)
                if previous is not None:
                    pe.wait_ge(a["o_split"], previous + GH)
                split_product(dst_of(1 + GH), chunks(wk_hi), chunks(wk_lo),
                              chunks(ctx_hi, half(h)), chunks(ctx_lo, half(h))).then_inc(a["qk_ready"], 1)

            def project_out(a, dst_of, tiles=range(HT)):
                for i in tiles:
                    split_product(dst_of(7 + i), chunks(o_hi, tok(i)), chunks(o_lo, tok(i)),
                                  chunks(wo_hi, slice(0, D)), chunks(wo_lo, slice(0, D))).then_inc(a["op_ready"], 1)

            def look_up_tables(part):
                pe.wait_ge(tables_lo_done, 1)
                for c in range(KC):
                    pe.wait_ge(onehot_ready, c + 1)
                    for i in range(2):
                        dst = table_bank[2 * part + i]
                        cols = slice((2 * c + part) * P, (2 * c + part + 1) * P)
                        pe.matmul(dst, tables_hi[:, cols], one_hots(c)[:, half(i)], start=(c == 0), stop=False)
                        mm = pe.matmul(dst, tables_lo[:, cols], one_hots(c)[:, half(i)], start=False, stop=(c == KC - 1))
                mm.then_inc(tables_ready, 1)

            def step(a, g, h, first=False, last=False):
                s = g * 2 + h
                n = g + L1_SET * layer_of(a)
                tables_too = first and not layer_of(a)
                def make_scores():
                    pe.wait_ge(qk_done(a), s * 5 + 5)
                    if first:
                        pe.wait_ge(z_split, HT * (4 * layer_of(a) + 2))
                    else:
                        pe.wait_ge(a["pt_split"], s * 4)
                    for hp in range(2):
                        for b in range(HB):
                            width = 2 * S if b < HB - 1 else S
                            mm = pe.matmul(scores[:, hp, b * S:b * S + width],
                                           q_by_seq[:, b, 2 * hp:2 * hp + 2, :].rearrange("p h s -> p (h s)"),
                                           k[:, b * S:b * S + width], start=True, stop=True)
                        mm.then_inc(a["scores_ready"], 1)

                if not first:
                    make_scores()
                if h == 0:
                    pe.wait_ge(wv_hi_done, n + 1)
                    pe.wait_ge(wv_lo_done, n + 1)
                if first:
                    pe.wait_ge(a["qk_read"], 3)
                elif not (isinstance(s, int) and s == 1):
                    pe.wait_ge(a["o_added"], s * 4 - 4)
                elif not layer_of(a):
                    pe.wait_ge(tables_out, 4)
                split_product(bank(h, 0), chunks(wv_hi), chunks(wv_lo),
                              chunks(ctx_hi, half(h)), chunks(ctx_lo, half(h))).then_inc(a["vt_ready"], 1)
                if first:
                    make_scores()
                    if not layer_of(a):
                        pe.wait_ge(ctx_lo_done, 2)
                if last:
                    pe.wait_ge(a["o_split"], s * 4)
                    pe.wait_ge(wo_hi_done, g + GROUPS * layer_of(a) + 1)
                    pe.wait_ge(wo_lo_done, g + GROUPS * layer_of(a) + 1)
                    project_out(a, lambda j: bank(h, j), (0, 1))
                else:
                    project_qk(a, 1 - h, lambda j: bank(h, j), new_set=(n + 1 if h else None),
                               previous=(None if first else s * 4 - 4))
                for hp in range(2):
                    pe.wait_ge(a["probs_ready"], s * 2 + hp + 1)
                    for b in range(PAIRS):
                        mm = pe.transpose(scores[:, hp, tok(b)],
                                          probs[:, hp, 2 * b:2 * b + 2, :].rearrange("p b k -> p (b k)"), ident[:])
                    mm.then_inc(a["pt_ready"], 1)
                pe.wait_ge(a["vt_out"], s + 1)
                for b in range(PAIRS):
                    mm = pe.transpose(bank(h, 6)[:, tok(b)], v_t[:, tok(b)], ident[:])
                mm.then_inc(a["vtr_ready"], 1)
                if not first and not last:
                    pe.wait_ge(a["o_split"], s * 4)
                    if h:
                        n_wo = g + GROUPS * layer_of(a)
                        pe.wait_ge(wo_hi_done, n_wo + 1)
                        pe.wait_ge(wo_lo_done, n_wo + 1)
                    pe.wait_ge(a["qk_read"], s * 5 + 5 + GH)
                    project_out(a, lambda j: bank(h, j), (0, 1))
                if last:
                    project_out(a, lambda j: bank(h, j), (2,))
                if not last:
                    pe.wait_ge(a["qk_read"], s * 5 + 10)
                if tables_too:
                    look_up_tables(0)
                pe.wait_ge(a["v_split"], s + 1)
                for b in range(PAIRS):
                    if b % 2 == 0:
                        pe.wait_ge(a["pt_split"], s * 4 + b + 2)
                    if b >= 2 and not first:
                        pe.wait_ge(a["o_added"], s * 4 - 4 + b - 1)
                    dst = bank(h, 11 + b)
                    pe.matmul(dst, v_hi[:, b, :], probs_t_hi[:, b, :, :], start=True, stop=False)
                    pe.matmul(dst, v_hi[:, b, :], probs_t_lo[:, b % 2, :, :], start=False, stop=False)
                    pe.matmul(dst, v_lo[:, b, :], probs_t_hi[:, b, :, :], start=False, stop=True).then_inc(a["pv_ready"], 1)
                    if b == 1 and not first:
                        project_out(a, lambda j: bank(h, j), (3,) if last else (2, 3))
                    if b == 1 and tables_too:
                        look_up_tables(1)
                        pe.wait_ge(tables_out, 2)

            def attention(layer):
                a = att[layer]
                if not layer:
                    norm_turn(0)
                pe.wait_ge(z_split, HT * (4 * layer + 1))
                project_qk(a, 0, lambda j: bank(1, j), new_set=L1_SET * layer, prologue=True)
                if layer:
                    norm_turn(5, (2, 3))
                else:
                    norm_turn(1)
                pe.wait_ge(zeros_made, 2)
                step(a, 0, 0, first=True)
                step(a, 0, 1)
                with pe.Fori(1, GROUPS - 1) as g:
                    step(a, g, 0)
                    step(a, g, 1)
                step(a, GROUPS - 1, 0)
                step(a, GROUPS - 1, 1, last=True)
                m = 4 * layer + 2
                pe.wait_ge(a["o_split"], 8 * GROUPS - 2)
                pe.wait_ge(a["o_added"], 8 * GROUPS - 4)
                project_out(a, lambda j: bank(0, j), (0, 1))
                norm_turn(m, (0, 1))
                pe.wait_ge(a["o_split"], 8 * GROUPS)
                project_out(a, lambda j: bank(0, j), (2,))
                norm_turn(m, (2, 3))
                project_out(a, lambda j: bank(0, j), (3,))

            pe.wait_ge(ident_made, 2)
            attention(0)

            base_bank = [ring[:, b, :] for b in (4, 5, 0, 1)]
            for h in range(2):
                def base(tiles):
                    for t in tiles:
                        if h:
                            pe.wait_ge(ffn_added, t + 1)
                        mm = split_product(base_bank[t], chunks(z_hi, tok(HT * h + t)), chunks(z_lo, tok(HT * h + t)),
                                           chunks(wq_hi, slice(0, D)), chunks(wq_lo, slice(0, D)), stop=False)
                    return mm

                pe.wait_ge(z_split, HT * (3 + h))
                if h == 0:
                    pe.wait_ge(wk_lo_done, FFN0_SET + 1)
                    pe.wait_ge(wv_lo_done, FFN0_SET + 1)
                    pe.wait_ge(att[0]["o_added"], 8 * GROUPS - 1)
                else:
                    pe.wait_ge(hw_ready, 1)
                    pe.wait_ge(gate_wide, 1)
                split_product(ring[:, 2, :], chunks(wk_hi), chunks(wk_lo), chunks(z_hi, half(h)), chunks(z_lo, half(h)))\
                    .then_inc(ffn_hg_ready, 1)
                split_product(ring[:, 3, :], chunks(wv_hi), chunks(wv_lo), chunks(z_hi, half(h)), chunks(z_lo, half(h)))\
                    .then_inc(ffn_hg_ready, 1)
                pe.wait_ge(wq_lo_done, FFN0_SET + 1)
                if h == 0:
                    pe.wait_ge(att[0]["o_added"], 8 * GROUPS)
                base((0, 1))
                pe.wait_ge(ffn_hg_out, 2 * h + 2)
                for t in range(HT):
                    mm = pe.transpose(ring[:, 3, tok(t)], v_t[:, tok(t)], ident[:])
                mm.then_inc(gate_cols, 1)
                norm_turn(3 + h, (0, 1))
                base((2, 3)).then_inc(base_done, 1)
                pe.wait_ge(gate_wide, h + 1)
                for t in range(HT):
                    mm = pe.transpose(ring[:, 2, tok(t)], gate_wide_sb[:, t, :], ident[:])
                mm.then_inc(gate_wide_t, 1)
                norm_turn(3 + h, (2, 3))
                pe.wait_ge(hw_ready, h + 1)
                pe.wait_ge(wo_in, 16 * (FFN0_SET + 1))
                for t in range(HT):
                    pe.matmul(base_bank[t], rot[:, 0, tok(t)], wo_raw[:, 0, :], start=False, stop=True)\
                        .then_inc(ffn_sum, 1)

            attention(1)

            for h in range(2):
                if h:
                    norm_turn(7)
                pe.wait_ge(z_split, HT * (7 + h))
                if h == 0:
                    pe.wait_ge(wv_lo_done, L1_SET + GROUPS + 1)
                split_product(mix_bank[h], chunks(wv_hi), chunks(wv_lo), chunks(z_hi, half(h)), chunks(z_lo, half(h)))\
                    .then_inc(mix_ready, 1)
                pe.wait_ge(mix_out, h + 1)
                pe.wait_ge(att[1]["o_added"], 8 * GROUPS - 3 + h)
                for t in range(HT):
                    mm = pe.transpose(ring[:, 1 + h, tok(t)], (k, v_t)[h][:, tok(t)], ident[:])
                mm.then_inc(mix_cols, 1)
            for h in range(2):
                pe.wait_ge(pre_sum, 3 * h + 3)
                for t in range(HT):
                    mm = pe.transpose(ring[:, 2 + h, tok(t)], rot[:, h, tok(t)], ident[:])
                mm.then_inc(pre_t_ready, 1)
                pe.wait_ge(pre_t_out, h + 1)
                pe.wait_ge(wk_in, 16 * (L1_SET + GROUPS + 1))
                for t in range(HT):
                    mm = pe.matmul(ring[:, h, tok(t)], cos[:, tok(HT * h + t)], wk_raw[:, 0, :], start=True, stop=True)
                mm.then_inc(y_ready, 1)
            for i in range(ACT_TILES):
                for j in range(STREAMS):
                    pe.wait_ge(act_terms, STREAMS * i + j + 1)
                    pe.matmul(sum_bank[i], ident[:], mix_term(i, j), start=(j == 0), stop=False)
                pe.matmul(sum_bank[i], ident[:], x[:, DVE_TILES + i, :], start=False, stop=True).then_inc(act_sum, 1)

        @block.scalar
        def _(act):
            def norm_root(m):
                act.wait_ge(var_ready, m + 1)
                act.activation(rstd[:], rstd[:], ACT.Sqrt).then_inc(std_ready, 1)

            def norm_hi(m):
                for t in range(HT):
                    act.wait_ge(zt_ready, HT * m + t + 1)
                    act.activation(z_hi[:, :, tok(HT * (m % 2) + t)],
                                   turn_bank(m, t).rearrange("p (c n) -> p c n", c=KC), ACT.Copy)\
                        .then_inc(z_hi_ready, 1)

            def split_wq_hi_parts(loads):
                act.wait_ge(wq_in, loads * 16)
                for i in range(GH):
                    act.activation(wq_hi[:, :, tok(i)], wq_raw[:, :, tok(i)], ACT.Copy)\
                        .then_inc(wq_hi_done if i == GH - 1 else wq_hi_part, 1)

            def split_hi(raw, hi, arrived, loads, done):
                act.wait_ge(arrived, loads * 16)
                act.activation(hi[:], raw[:], ACT.Copy).then_inc(done, 1)

            def copy_qk(a, g, idx, parity):
                act.wait_ge(qk_bias_in, g * 16 + 16)
                for i in range(5):
                    act.wait_ge(a["qk_ready"], idx + i + 1)
                    src = bank(parity, 1 + i)
                    if i < GH:
                        act.activation(q_by_seq[:, :, i, :], by_seq(src), ACT.Identity, bias=qk_bias[:, i:i + 1])\
                            .then_inc(a["qk_read"], 1)
                    else:
                        act.activation(k[:], src, ACT.Identity, bias=qk_bias[:, GH:GH + 1]).then_inc(a["qk_read"], 1)

            def tables_result(part):
                act.wait_ge(tables_ready, part + 1)
                for i in range(2):
                    act.activation((cos, sin)[part][:, half(i)], table_bank[2 * part + i], ACT.Copy).then_inc(tables_out, 1)

            def step(a, g, h, first=False, last=False):
                s = g * 2 + h
                n = g + L1_SET * layer_of(a)
                n_wo = g + GROUPS * layer_of(a)
                for hp in range(2):
                    act.wait_ge(a["shifted"], s * 2 + hp + 1)
                    act.activation(probs[:, hp], probs[:, hp], ACT.Exp, scale=SCALE).then_inc(a["exp_done"], 1)
                act.wait_ge(a["vt_ready"], s + 1)
                if layer_of(a):
                    act.activation(v_t[:], bank(h, 0), ACT.Copy).then_inc(a["vt_out"], 1)
                else:
                    act.wait_ge(v_bias_in, g * 16 + 16)
                    act.activation(v_t[:], bank(h, 0), ACT.Identity, bias=v_bias[:, 1:2]).then_inc(a["vt_out"], 1)
                if last and not layer_of(a):
                    split_hi(wq_raw, wq_hi, wq_in, FFN0_SET + 1, wq_hi_done)
                    split_hi(wk_raw, wk_hi, wk_in, FFN0_SET + 1, wk_hi_done)
                if last:
                    split_hi(wv_raw, wv_hi, wv_in, n + 2, wv_hi_done)
                if not layer_of(a) and not last:
                    copy_qk(a, g + h, s * 5 + 5, h)
                act.wait_ge(a["pt_ready"], s * 2 + 2)
                for second in range(2):
                    rows = slice(S * second, S * second + S)
                    act.activation(probs_t_hi[rows, :, second, :].rearrange("p b (a n) -> p b a n", a=2),
                                   scores[rows, :, :].rearrange("p a (b n) -> p b a n", b=PAIRS),
                                   ACT.Copy).then_inc(a["pt_hi_ready"], 1)
                act.wait_ge(a["vtr_ready"], s + 1)
                act.activation(v_hi[:], bank(h, 6).rearrange("p (b n) -> p b n", b=PAIRS), ACT.Copy).then_inc(a["v_hi_ready"], 1)
                tables_too = first and not layer_of(a)
                if tables_too:
                    tables_result(0)
                if not last:
                    if h == 0:
                        if not (isinstance(g, int) and g == GROUPS - 1):
                            act.wait_ge(a["qk_ready"], s * 5 + 10)
                            split_hi(wq_raw, wq_hi, wq_in, n + 2, wq_hi_done)
                            split_hi(wk_raw, wk_hi, wk_in, n + 2, wk_hi_done)
                    else:
                        split_hi(wv_raw, wv_hi, wv_in, n + 2, wv_hi_done)
                if tables_too:
                    tables_result(1)
                for b in range(PAIRS):
                    if last and b == 2:
                        norm_root(4 * layer_of(a) + 2)
                    act.wait_ge(a["pv_ready"], s * 4 + b + 1)
                    act.activation(o_view(o_hi, b), bank(h, 11 + b).rearrange("p (b h q) -> p b h q", b=2, h=GH), ACT.Copy)\
                        .then_inc(a["o_hi_ready"], 1)
                    if h == 0 and b == 2:
                        split_hi(wo_raw, wo_hi, wo_in, n_wo + 1 + layer_of(a), wo_hi_done)

            def attention(layer):
                a = att[layer]
                if layer:
                    act.wait_ge(base_done, 2)
                    split_wq_hi_parts(L1_SET + 1)
                    split_hi(wk_raw, wk_hi, wk_in, L1_SET + 1, wk_hi_done)
                    split_hi(wv_raw, wv_hi, wv_in, L1_SET + 1, wv_hi_done)
                    norm_root(5)
                else:
                    norm_root(0)
                    split_wq_hi_parts(1)
                    norm_hi(0)
                    split_hi(wk_raw, wk_hi, wk_in, 1, wk_hi_done)
                    act.wait_ge(ctx_in[0], 16)
                    act.activation(ctx_hi[:, :, half(0)], rot[:], ACT.Copy).then_inc(ctx_hi_done, 1)
                    act.wait_ge(tables_in, 16)
                    act.activation(tables_hi, probs_flat, ACT.Copy).then_inc(tables_hi_done, 1)
                    split_hi(wv_raw, wv_hi, wv_in, 1, wv_hi_done)
                    act.wait_ge(ctx_in[1], 16)
                    act.activation(ctx_hi[:, :, half(1)], wo_raw[:], ACT.Copy).then_inc(ctx_hi_done, 1)
                    norm_root(1)
                    copy_qk(a, 0, 0, 1)
                norm_hi(4 * layer + 1)
                if not layer:
                    act.wait_ge(bias_added, TILES)
                step(a, 0, 0, first=True)
                step(a, 0, 1)
                with act.Fori(1, GROUPS - 1) as g:
                    step(a, g, 0)
                    step(a, g, 1)
                step(a, GROUPS - 1, 0)
                step(a, GROUPS - 1, 1, last=True)

            act.dma_start(scalars[:, 0:1], b_thr.partition_broadcast(P)).then_inc(small_in, 16)
            act.dma_start(scalars[:, 1:2], gate.partition_broadcast(P)).then_inc(small_in, 16)
            act.dma_start(mix_base_sb[:], mix_base.partition_broadcast(P)).then_inc(small_in, 16)
            act.dma_start(bias_rows[0], bo0.partition_broadcast(P)).then_inc(row_in, 16)
            attention(0)

            norm_hi(2)
            norm_root(3)
            for h in range(2):
                for i, dst in enumerate((k, v_t)):
                    act.wait_ge(ffn_hg_ready, 2 * h + i + 1)
                    act.activation(dst[:], ring[:, 2 + i, :], ACT.Copy).then_inc(ffn_hg_out, 1)
                act.wait_ge(gate_exp_in, h + 1)
                act.activation(gate_w[:], gate_w[:], ACT.Exp).then_inc(gate_exp_out, 1)
                if h:
                    act.wait_ge(small_in, 48)
                    act.activation(scalars[:, 1:2], scalars[:, 1:2], ACT.Exp, scale=-1.0).then_inc(gate_scalar, 1)
                norm_hi(3 + h)
                if h == 0:
                    norm_root(4)
            attention(1)

            def squares(h):
                for t in range(HT * h, HT * h + HT):
                    if t >= 1:
                        act.wait_ge(sq_done, t)
                    act.activation(probs_flat[:, (t % 2) * D:(t % 2 + 1) * D],
                                   (wq_raw, wo_raw)[h][:, t % HT, :], ACT.Square,
                                   accum_out=rms[:, t:t + 1]).then_inc(sq_done, 1)

            def mix_logits_out(h):
                act.wait_ge(mix_ready, h + 1)
                act.activation((k, v_t)[h][:], mix_bank[h], ACT.Copy).then_inc(mix_out, 1)

            norm_hi(6)
            squares(0)
            norm_root(7)
            mix_logits_out(0)
            norm_hi(7)
            squares(1)
            mix_logits_out(1)
            act.wait_ge(ms_ready, 1)
            act.activation(rms[:], rms[:], ACT.Sqrt).then_inc(rms_root, 1)

            def mixed_out(i):
                act.wait_ge(act_sum, i + 1)
                act.activation(x[:, DVE_TILES + i, :], sum_bank[i], ACT.Copy).then_inc(act_mixed, 1)

            def exp_k(h):
                return act.activation(halves(K, h), halves(T, h), ACT.Exp)

            for h in range(2):
                act.wait_ge(sink_to_act, h + 1)
                exp_k(h).then_inc(sink_from_act, 1)
            for h in range(2):
                act.activation(halves(fac[:, 1], h), halves(red[:, 1], h), ACT.Exp).then_inc(sink_from_act, 1)
            act.wait_ge(pp_exp_in, 1)
            lp = logits[:, :, 16:24]
            act.activation(lp, lp, ACT.Exp).then_inc(pp_exp_out, 1)

            def refresh(c):
                for h in range(2):
                    act.wait_ge(sink_order, levels_done(c) - 1 + h)
                    f = fac[:, :, h * HT:(h + 1) * HT]
                    act.activation(f, f, ACT.Ln).then_inc(sink_from_act, 1)
                for h in range(2):
                    act.wait_ge(sink_to_act, 2 + c * 2 + h + 1)
                    exp_k(h).then_inc(sink_from_act, 1)

            for h in range(2):
                act.wait_ge(pre_t_ready, h + 1)
                act.activation(cos[:, half(h)], ring[:, 2 + h, :], ACT.Copy).then_inc(pre_t_out, 1)
                act.wait_ge(y_ready, h + 1)
                act.activation(sin[:, half(h)], ring[:, h, :], ACT.Copy).then_inc(y_out, 1)
            with act.Fori(0, REFRESHES) as c:
                refresh(c)

            act.wait_ge(h_ready, 1)
            for i in range(ACT_TILES):
                tile = DVE_TILES + i
                if i >= 2:
                    act.wait_ge(act_sum, i - 1)
                for j in range(STREAMS):
                    for n in range(STREAMS):
                        last = act.activation(mix_term(i, j)[:, tok(n)], wo_raw[:, tile - HT, tok(j)], ACT.Copy,
                                              scale=K[:, tile, n, j:j + 1])
                    last.then_inc(act_terms, 1)
                if i:
                    mixed_out(i - 1)
            mixed_out(ACT_TILES - 1)

        @block.gpsimd
        def _(pool):
            def split_lo(raw, hi, lo, hi_done, sets, done):
                pool.wait_ge(hi_done, sets)
                pool.tensor_tensor(lo[:], raw[:], hi[:], ALU.subtract).then_inc(done, 1)

            def split_wq_lo_parts(sets):
                for i in range(GH):
                    if i < GH - 1:
                        pool.wait_ge(wq_hi_part, (GH - 1) * (sets > 1) + i + 1)
                    else:
                        pool.wait_ge(wq_hi_done, sets)
                    pool.tensor_tensor(wq_lo[:, :, tok(i)], wq_raw[:, :, tok(i)], wq_hi[:, :, tok(i)], ALU.subtract)\
                        .then_inc(wq_lo_done if i == GH - 1 else wq_lo_part, 1)

            def add_bias(m):
                for t in range(HT):
                    tile = HT * (m % 2) + t
                    pool.wait_ge(z_nat_ready, HT * m + t + 1)
                    pool.tensor_tensor(x[:, tile, :], x[:, tile, :], bias_rows[m // 2], ALU.add).then_inc(bias_added, 1)

            def turn_add(a, idx, parity):
                for i in range(5):
                    b = (parity + i) % 2
                    pool.wait_ge(a["qk_read"], idx + i + 1)
                    pool.tensor_tensor(q_by_seq[:, :, i, :] if i < GH else by_seq(k[:]),
                                       by_seq(rot[:, b, :]), by_seq(rot[:, 2 + b, :]), ALU.add)\
                        .then_inc(a["qk_out"], 1)

            def step(a, g, h, last=False):
                s = g * 2 + h
                n = g + L1_SET * layer_of(a)
                n_wo = g + GROUPS * layer_of(a)
                if last:
                    pool.wait_ge(wv_lo_done, n + 1)
                    pool.memset(wv_raw[:], 0.0).then_inc(pads_made, 1)
                for hp in range(2):
                    pool.wait_ge(a["row_inv"], s * 2 + hp + 1)
                    pool.tensor_tensor(probs[:, hp], probs[:, hp],
                                       row_inv_sb[:, hp, :].unsqueeze(2).broadcast_to([P, HB, S]), ALU.mult)\
                        .then_inc(a["probs_ready"], 1)
                if layer_of(a) and not last:
                    turn_add(a, s * 5 + 5, 1 - h)
                if not last:
                    if h == 0:
                        if not (isinstance(g, int) and g == GROUPS - 1):
                            split_lo(wq_raw, wq_hi, wq_lo, wq_hi_done, n + 2, wq_lo_done)
                            split_lo(wk_raw, wk_hi, wk_lo, wk_hi_done, n + 2, wk_lo_done)
                    else:
                        split_lo(wv_raw, wv_hi, wv_lo, wv_hi_done, n + 2, wv_lo_done)
                if last and not layer_of(a):
                    split_lo(wq_raw, wq_hi, wq_lo, wq_hi_done, FFN0_SET + 1, wq_lo_done)
                    split_lo(wk_raw, wk_hi, wk_lo, wk_hi_done, FFN0_SET + 1, wk_lo_done)
                if last:
                    split_lo(wv_raw, wv_hi, wv_lo, wv_hi_done, n + 2, wv_lo_done)
                if h == 0:
                    split_lo(wo_raw, wo_hi, wo_lo, wo_hi_done, n_wo + 1, wo_lo_done)

            def attention(layer):
                a = att[layer]
                if layer:
                    turn_add(a, 0, 0)
                step(a, 0, 0)
                step(a, 0, 1)
                with pool.Fori(1, GROUPS - 1) as g:
                    step(a, g, 0)
                    step(a, g, 1)
                step(a, GROUPS - 1, 0)
                step(a, GROUPS - 1, 1, last=True)

            pool.iota(pos_col[:], pattern=[[P, KC]], base=0, channel_multiplier=1,
                      allow_small_or_imprecise_dtypes=True).then_inc(ident_made, 1)
            pool.memset(ident[:], 0.0).then_inc(ident_cleared, 1)
            pool.wait_ge(ident_cleared, 1)
            pool.affine_select(out=ident[:], in_=ident[:], compare_op=ALU.not_equal, fill=1.0, base=0,
                               pattern=[[-1, P]], channel_multiplier=1).then_inc(ident_made, 1)
            split_wq_lo_parts(1)
            split_lo(wk_raw, wk_hi, wk_lo, wk_hi_done, 1, wk_lo_done)
            pool.wait_ge(tables_hi_done, 1)
            pool.tensor_tensor(tables_lo, probs_flat, tables_hi, ALU.subtract).then_inc(tables_lo_done, 1)
            split_lo(wv_raw, wv_hi, wv_lo, wv_hi_done, 1, wv_lo_done)
            pool.memset(probs_t_hi[:].bitcast(F32), 0.0).then_inc(zeros_made, 1)
            pool.memset(probs_t_lo[:].bitcast(F32), 0.0).then_inc(zeros_made, 1)
            pool.wait_ge(row_in, 16)
            add_bias(0)
            add_bias(1)
            attention(0)

            pool.wait_ge(row_in, 32)
            add_bias(2)
            add_bias(3)
            split_wq_lo_parts(L1_SET + 1)
            split_lo(wk_raw, wk_hi, wk_lo, wk_hi_done, L1_SET + 1, wk_lo_done)
            split_lo(wv_raw, wv_hi, wv_lo, wv_hi_done, L1_SET + 1, wv_lo_done)
            attention(1)

            pool.wait_ge(pp_ready, 1)
            for h in range(2):
                if h:
                    pool.wait_ge(pre_sum, 3)
                by_stream = (wq_raw, wo_raw)[h][:].rearrange("p t (n c) -> p t n c", c=P)
                pool.tensor_tensor(q[:].rearrange("p t (n c) -> p t n c", c=P), by_stream,
                                   halves(logits, h)[:, :, 16:20].unsqueeze(3).broadcast_to([P, HT, STREAMS, P]), ALU.mult)\
                    .then_inc(pre_sum, 1)
                pool.wait_ge(pre_sum, 3 * h + 1)
                pool.tensor_tensor(q[:, :, 0:2 * P], q[:, :, 0:2 * P], q[:, :, 2 * P:], ALU.add).then_inc(pre_sum, 1)
                pool.wait_ge(pre_sum, 3 * h + 2)
                pool.tensor_tensor(rot[:, h, :].rearrange("p (t n) -> p t n", n=P), q[:, :, 0:P], q[:, :, P:2 * P], ALU.add)\
                    .then_inc(pre_sum, 1)
            for h in range(2):
                pool.wait_ge(y_out, h + 1)
                if h:
                    pool.wait_ge(y_added, 1)
                else:
                    pool.wait_ge(pre_sum, 6)
                pool.tensor_tensor(q[:].rearrange("p t (n c) -> p t n c", c=P),
                                   sin[:, half(h)].rearrange("p (t c) -> p t c", c=P).unsqueeze(2).broadcast_to([P, HT, STREAMS, P]),
                                   halves(logits, h)[:, :, 20:24].unsqueeze(3).broadcast_to([P, HT, STREAMS, P]), ALU.mult)\
                    .then_inc(y_terms, 1)
                pool.wait_ge(y_terms, h + 1)
                pool.tensor_tensor(x[:, h * HT:(h + 1) * HT, :], x[:, h * HT:(h + 1) * HT, :],
                                   q[:], ALU.add).then_inc(y_added, 1)
            last = TILES - 1
            pool.wait_ge(h_ready, 1)
            for i, terms in enumerate(pool_terms):
                pool.tensor_tensor(terms.rearrange("p j (i c) -> p j i c", c=P),
                                   wo_raw[:, last - HT, i * 2 * P:(i + 1) * 2 * P].rearrange("p (j c) -> p j c", c=P)
                                   .unsqueeze(2).broadcast_to([P, 2, STREAMS, P]),
                                   K[:, last, :, 2 * i:2 * i + 2].rearrange("p i j -> p j i").unsqueeze(3)
                                   .broadcast_to([P, 2, STREAMS, P]), ALU.mult).then_inc(pool_order, 1)
            pool.wait_ge(pool_order, 2)
            pool.tensor_tensor(pool_terms[0], pool_terms[0], pool_terms[1], ALU.add).then_inc(pool_order, 1)
            pool.wait_ge(pool_order, 3)
            pool.tensor_tensor(pool_terms[0][:, 0], pool_terms[0][:, 0], pool_terms[0][:, 1], ALU.add).then_inc(pool_order, 1)
            pool.wait_ge(pool_order, 4)
            pool.tensor_tensor(x[:, last, :], x[:, last, :], pool_terms[0][:, 0], ALU.add).then_inc(pool_order, 1)

        @block.vector
        def _(dve):
            def norm_stats(m, t):
                tile = HT * (m % 2) + t
                if m and t == 0:
                    dve.wait_ge(norm_order, (2 * HT + 1) * m)
                    dve.wait_ge(z_nat_ready, HT * m)
                if m < 2:
                    dve.wait_ge(x_in[m % 2], 16)
                elif m in (4, 5):
                    dve.wait_ge(ffn_added, tile + 1)
                else:
                    dve.wait_ge(att[m // 4]["o_added"], 8 * GROUPS - 2 * HT + tile + 1)
                dve.bn_stats(stats[:, t, :], x[:, tile, :]).then_inc(norm_order, 1)

            def norm_finish(m):
                base = (2 * HT + 1) * m
                if m == 6:
                    dve.wait_ge(wq_lo_done, L1_SET + GROUPS)
                if m == 7:
                    dve.wait_ge(wo_lo_done, 2 * GROUPS)
                for t in range(HT):
                    dve.wait_ge(norm_order, base + t + 1)
                    dve.bn_aggr(mean_var[:, t, :], stats[:, t, :]).then_inc(norm_order, 1)
                dve.wait_ge(norm_order, base + 2 * HT)
                dve.tensor_scalar(rstd[:], mean_var[:, :, 1], LN_EPS, None, ALU.add).then_inc(var_ready, 1)
                dve.wait_ge(std_ready, m + 1)
                dve.reciprocal(rstd[:], rstd[:]).then_inc(norm_order, 1)
                dve.wait_ge(norm_order, base + 2 * HT + 1)
                for t in range(HT):
                    dve.tensor_scalar(z_nat_of[m][:, t, :], x[:, HT * (m % 2) + t, :], mean_var[:, t, 0:1], rstd[:, t:t + 1],
                                      ALU.subtract, ALU.mult).then_inc(z_nat_ready, 1)

            def norm_nat(m):
                for t in range(HT):
                    norm_stats(m, t)
                norm_finish(m)

            def norm_lo(m, tiles=range(HT)):
                for t in tiles:
                    dve.wait_ge(z_hi_ready, HT * m + t + 1)
                    cols = tok(HT * (m % 2) + t)
                    dve.tensor_tensor(z_lo[:, :, cols], turn_bank(m, t).rearrange("p (c n) -> p c n", c=KC),
                                      z_hi[:, :, cols], ALU.subtract).then_inc(z_split, 1)

            def turn_qk(a, idx, parity_bank, parity, h, products=range(5)):
                for i in products:
                    b = (parity + i) % 2
                    src = bank(parity_bank, 1 + i)
                    dve.wait_ge(a["qk_ready"], idx + i + 1)
                    if not (isinstance(idx, int) and idx + i < 2):
                        dve.wait_ge(a["qk_out"], idx + i - 1)
                    dve.tensor_tensor(rot[:, b, :], src, cos[:, half(h)], ALU.mult)
                    dve.tensor_tensor(rot[0:64, 2 + b, :], src[64:128, :], sin[64:128, half(h)], ALU.mult)
                    dve.tensor_tensor(rot[64:128, 2 + b, :], src[0:64, :], sin[0:64, half(h)], ALU.mult)\
                        .then_inc(a["qk_read"], 1)

            def add_out(a, s, h_prev, tiles=range(HT), norm=None):
                for i in tiles:
                    tile = HT * h_prev + i
                    dve.wait_ge(a["op_ready"], s * 4 - 4 + i + 1)
                    dve.tensor_tensor(x[:, tile, :], bank(1 - h_prev, 7 + i), x[:, tile, :], ALU.add).then_inc(a["o_added"], 1)
                    if norm is not None:
                        norm_stats(norm, i)

            def step(a, g, h, first=False, last=False):
                s = g * 2 + h
                for hp in range(2):
                    dve.wait_ge(a["scores_ready"], s * 2 + hp + 1)
                    if layer_of(a):
                        dve.memset(row_max_sb[:, hp, :], 0.0)
                        dve.copy_predicated(scores[:, hp, :], masked_out[:, h * HB:(h + 1) * HB, :].rearrange("p b k -> p (b k)"),
                                            masked_value[:].broadcast_to([P, HB * S])).then_inc(a["masked"], 1)
                        dve.wait_ge(a["masked"], s * 2 + hp + 1)
                    dve.tensor_reduce(row_max_sb[:, hp, :], scores[:, hp, :].rearrange("p (b k) -> p b k", k=S), AX.X, ALU.max)\
                        .then_inc(a["row_max"], 1)
                for hp in range(2):
                    dve.wait_ge(a["row_max"], s * 2 + hp + 1)
                    if not first:
                        dve.wait_ge(a["pt_ready"], s * 2)
                    dve.tensor_tensor(probs[:, hp], scores[:, hp, :].rearrange("p (b k) -> p b k", k=S),
                                      row_max_sb[:, hp, :].unsqueeze(2).broadcast_to([P, HB, S]), ALU.subtract)\
                        .then_inc(a["shifted"], 1)
                for hp in range(2):
                    dve.wait_ge(a["exp_done"], s * 2 + hp + 1)
                    dve.tensor_reduce(row_sum_sb[:, hp, :], probs[:, hp], AX.X, ALU.add).then_inc(a["row_sum"], 1)
                for hp in range(2):
                    dve.wait_ge(a["row_sum"], s * 2 + hp + 1)
                    if not first:
                        dve.wait_ge(a["probs_ready"], s * 2)
                    dve.reciprocal(row_inv_sb[:, hp, :], row_sum_sb[:, hp, :]).then_inc(a["row_inv"], 1)
                if layer_of(a) and not last:
                    turn_qk(a, s * 5 + 5, h, 1 - h, 1 - h)
                if last:
                    add_out(a, s, 0, (0, 1), norm=4 * layer_of(a) + 2)

                def probs_t_low(two):
                    for second in range(2):
                        rows = slice(S * second, S * second + S)
                        dve.wait_ge(a["pt_hi_ready"], s * 2 + second + 1)
                        dve.tensor_tensor(probs_t_lo[rows, :, second, :].rearrange("p b (a n) -> p b a n", a=2),
                                          scores[rows, :, two * 2 * P:(two + 1) * 2 * P].rearrange("p a (b n) -> p b a n", b=2),
                                          probs_t_hi[rows, 2 * two:2 * two + 2, second, :].rearrange("p b (a n) -> p b a n", a=2),
                                          ALU.subtract).then_inc(a["pt_split"], 1)

                def o_low(pairs):
                    for b in pairs:
                        dve.wait_ge(a["o_hi_ready"], s * 4 + b + 1)
                        dve.tensor_tensor(o_view(o_lo, b), bank(h, 11 + b).rearrange("p (b h q) -> p b h q", b=2, h=GH),
                                          o_view(o_hi, b), ALU.subtract).then_inc(a["o_split"], 1)

                probs_t_low(0)
                dve.wait_ge(a["v_hi_ready"], s + 1)
                dve.tensor_tensor(v_lo[:], bank(h, 6).rearrange("p (b n) -> p b n", b=PAIRS), v_hi[:], ALU.subtract)\
                    .then_inc(a["v_split"], 1)
                if last:
                    add_out(a, s, 0, (2,), norm=4 * layer_of(a) + 2)
                elif not first:
                    add_out(a, s, 1 - h, (0, 1))
                dve.wait_ge(a["pv_ready"], s * 4 + 2)
                probs_t_low(1)
                o_low((0, 1))
                if last:
                    add_out(a, s, 0, (3,), norm=4 * layer_of(a) + 2)
                    norm_finish(4 * layer_of(a) + 2)
                if not first and not last:
                    add_out(a, s, 1 - h, (2, 3))
                o_low((2, 3))

            def attention(layer):
                a = att[layer]
                if layer:
                    turn_qk(a, 0, 1, 0, 0, (0, 1, 2, 3))
                    norm_lo(5, (0, 1))
                    turn_qk(a, 0, 1, 0, 0, (4,))
                    norm_lo(5, (2, 3))
                else:
                    norm_nat(0)
                    norm_lo(0)
                    clamp_positions()
                    split_ctx_lo(0)
                    make_one_hots()
                    norm_nat(1)
                    norm_lo(1)
                    split_ctx_lo(1)
                    dve.wait_ge(mask_in, 32)
                    dve.tensor_scalar(masked_out[:], probs[:].bitcast(I32).rearrange("p a b k -> p (a b) k"), 0, None,
                                      ALU.is_equal).then_inc(mask_done, 1)
                dve.wait_ge(mask_done, 2)
                step(a, 0, 0, first=True)
                if not layer:
                    dve.wait_ge(bias_added, TILES)
                step(a, 0, 1)
                with dve.Fori(1, GROUPS - 1) as g:
                    step(a, g, 0)
                    step(a, g, 1)
                step(a, GROUPS - 1, 0)
                step(a, GROUPS - 1, 1, last=True)
                for projected, turned_tiles in (((0, 1), (0, 1)), ((2,), (2, 3)), ((3,), ())):
                    add_out(a, 2 * GROUPS, 1, projected, norm=4 * layer + 3)
                    norm_lo(4 * layer + 2, turned_tiles)
                norm_finish(4 * layer + 3)

            def make_one_hots():
                dve.wait_ge(pos_order, 4)
                dve.wait_ge(ident_made, 1)
                for c in range(KC):
                    dve.tensor_scalar(one_hots(c), sin[:], pos_col[:, c:c + 1], None, ALU.is_equal).then_inc(onehot_ready, 1)

            def clamp_positions():
                dve.wait_ge(pos_in, 16)
                dve.tensor_copy(sin[:], cos[:].bitcast(I32)).then_inc(pos_order, 1)
                dve.wait_ge(pos_order, 1)
                dve.tensor_scalar(cos[:], sin[:], 0.0, float(MAX_POS), ALU.is_lt, ALU.mult).then_inc(pos_order, 1)
                dve.wait_ge(pos_order, 2)
                dve.tensor_tensor(sin[:], sin[:], cos[:], ALU.add).then_inc(pos_order, 1)
                dve.wait_ge(pos_order, 3)
                dve.tensor_scalar(sin[:], sin[:], 0.0, float(MAX_POS - 1), ALU.max, ALU.min).then_inc(pos_order, 1)

            def split_ctx_lo(h):
                raw = wo_raw[:] if h else rot[:]
                dve.wait_ge(ctx_hi_done, h + 1)
                dve.tensor_tensor(ctx_lo[:, :, half(h)], raw, ctx_hi[:, :, half(h)], ALU.subtract).then_inc(ctx_lo_done, 1)

            dve.memset(masked_value[:], MASKED).then_inc(mask_done, 1)
            attention(0)

            def gating(h):
                wide = gate_wide_sb.rearrange("p t (e r) -> p t e r", r=RANK)
                w, wt = gate_w[:, :, 0:EXPERTS], gate_w[:, :, EXPERTS:EXPERTS + 1]
                top, thr, total = (gate_s[:, :, i:i + 1] for i in (0, 1, 2))

                def over_experts(ap):
                    return ap.broadcast_to([P, HT, EXPERTS])

                n = 14 * h
                dve.wait_ge(gate_cols, h + 1)
                dve.tensor_copy(gate_w[:], ring[:, 3, :].rearrange("p (t n) -> p t n", n=P)[:, :, 0:EXPERTS + 1]).then_inc(gate_order, 1)
                dve.wait_ge(gate_order, n + 1)
                dve.tensor_reduce(top, w, AX.X, ALU.max).then_inc(gate_order, 1)
                dve.wait_ge(gate_order, n + 2)
                dve.tensor_tensor(w, w, over_experts(top), ALU.subtract).then_inc(gate_order, 1)
                dve.tensor_scalar(wt, wt, scalars[:, 0:1], -1.0, ALU.add, ALU.mult).then_inc(gate_order, 1)
                dve.wait_ge(gate_order, n + 4)
                dve.tensor_copy(top, top).then_inc(gate_exp_in, 1)
                dve.wait_ge(gate_exp_out, h + 1)
                dve.tensor_reduce(total, w, AX.X, ALU.add).then_inc(gate_order, 1)
                dve.tensor_scalar(thr, wt, 1.0, None, ALU.add).then_inc(gate_order, 1)
                dve.wait_ge(gate_order, n + 6)
                dve.reciprocal(gate_s[:, :, 1:3], gate_s[:, :, 1:3]).then_inc(gate_order, 1)
                dve.wait_ge(gate_order, n + 7)
                dve.tensor_tensor(w, w, over_experts(total), ALU.mult).then_inc(gate_order, 1)
                dve.wait_ge(gate_order, n + 8)
                dve.scalar_tensor_tensor(out=w, in0=over_experts(thr), scalar=-0.125, in1=w, op0=ALU.mult, op1=ALU.add)\
                    .then_inc(gate_order, 1)
                dve.wait_ge(gate_order, n + 9)
                dve.tensor_scalar(w, w, 0.0, None, ALU.max).then_inc(gate_order, 1)
                dve.wait_ge(gate_order, n + 10)
                dve.tensor_reduce(total, w, AX.X, ALU.add).then_inc(gate_order, 1)
                dve.wait_ge(gate_order, n + 11)
                dve.scalar_tensor_tensor(out=total, in0=total, scalar=0.0, in1=total, op0=ALU.is_equal, op1=ALU.add)\
                    .then_inc(gate_order, 1)
                dve.wait_ge(gate_order, n + 12)
                dve.reciprocal(total, total).then_inc(gate_order, 1)
                dve.wait_ge(gate_order, n + 13)
                dve.scalar_tensor_tensor(out=w, in0=w, scalar=2.0, in1=over_experts(total), op0=ALU.mult, op1=ALU.mult)\
                    .then_inc(gate_order, 1)
                dve.wait_ge(gate_order, n + 14)
                dve.tensor_copy(wide, w.unsqueeze(3).broadcast_to([P, HT, EXPERTS, RANK])).then_inc(gate_wide, 1)

            dve.wait_ge(small_in, 48)
            for h in range(2):
                gating(h)
                norm_lo(3 + h, (0, 1))
                dve.wait_ge(gate_wide_t, h + 1)
                if h:
                    dve.wait_ge(ffn_sum, HT)
                dve.tensor_tensor(rot[:, 0, :], ring[:, 2, :], k[:], ALU.mult).then_inc(hw_ready, 1)
                norm_lo(3 + h, (2, 3))
                for t in range(HT):
                    tile = HT * h + t
                    dve.wait_ge(ffn_sum, tile + 1)
                    dve.wait_ge(bias_added, TILES + tile + 1)
                    dve.tensor_tensor(x[:, tile, :], ring[:, (4, 5, 0, 1)[t], :], x[:, tile, :], ALU.add).then_inc(ffn_added, 1)
                    norm_stats(4 + h, t)
                norm_finish(4 + h)

            attention(1)

            norm_lo(7)
            dve.wait_ge(gate_scalar, 1)
            dve.tensor_scalar(scalars[:, 1:2], scalars[:, 1:2], 1.0, None, ALU.add).then_inc(gate_scalar, 1)
            dve.wait_ge(gate_scalar, 2)
            dve.reciprocal(scalars[:, 1:2], scalars[:, 1:2]).then_inc(gate_scalar, 1)
            dve.wait_ge(gate_scalar, 3)
            dve.tensor_scalar(scalars[:, 2:3], scalars[:, 1:2], -1.0, 1.0, ALU.mult, ALU.add).then_inc(gate_scalar, 1)
            dve.wait_ge(sq_done, TILES)
            dve.tensor_scalar(rms[:], rms[:], 1.0 / D, RMS_EPS, ALU.mult, ALU.add).then_inc(ms_ready, 1)
            dve.wait_ge(rms_root, 1)
            dve.reciprocal(rms[:], rms[:]).then_inc(mix_order, 1)
            dve.wait_ge(mix_order, 1)
            dve.wait_ge(gate_scalar, 4)
            for h in range(2):
                dve.wait_ge(mix_cols, h + 1)
                dve.tensor_tensor(halves(logits, h), ring[:, 1 + h, :].rearrange("p (t n) -> p t n", n=P)[:, :, 0:24],
                                  halves(rms, h).unsqueeze(2).broadcast_to([P, HT, 24]), ALU.mult).then_inc(mix_order, 1)
            dve.wait_ge(mix_order, 3)
            dve.tensor_tensor(logits[:], logits[:], mix_base_sb[:].unsqueeze(1).broadcast_to([P, TILES, 24]), ALU.add)\
                .then_inc(mix_order, 1)
            dve.wait_ge(mix_order, 4)
            dve.tensor_scalar(Z.rearrange("p t i j -> p t (i j)"), logits[:, :, 0:16], 1.0 / TAU, None, ALU.mult).then_inc(mix_order, 1)

            def level(after, levels, done, build):
                for h in range(2):
                    dve.wait_ge(after, levels * 2 - 1 + h)
                    build(h).then_inc(done, 1)

            dve.wait_ge(mix_order, 5)
            for h in range(2):
                dve.tensor_reduce(halves(red[:, 0], h), halves(Z, h), AX.X, ALU.max).then_inc(sink_order, 1)
            level(sink_order, 1, sink_order,
                  lambda h: dve.tensor_tensor(halves(T, h), halves(Z, h), over_cols(halves(red[:, 0], h)), ALU.subtract))
            level(sink_order, 2, sink_order,
                  lambda h: dve.tensor_reduce(halves(red[:, 1], h), turned(halves(T, h)), AX.X, ALU.max))
            level(sink_order, 3, sink_to_act,
                  lambda h: dve.tensor_tensor(halves(T, h), halves(T, h), over_rows(halves(red[:, 1], h)), ALU.subtract))
            lp = logits[:, :, 16:24].rearrange("p t (a n) -> p t a n", n=STREAMS)
            pp4 = pp[:].unsqueeze(3).broadcast_to([P, TILES, 2, STREAMS])
            dve.tensor_reduce(pp[:], lp, AX.X, ALU.max).then_inc(mix_order, 1)
            dve.wait_ge(mix_order, 6)
            dve.tensor_tensor(lp, lp, pp4, ALU.subtract).then_inc(pp_exp_in, 1)
            level(sink_from_act, 2, sink_order,
                  lambda h: dve.tensor_scalar(lse[:, :, h * HT:(h + 1) * HT], red[:, :, h * HT:(h + 1) * HT], -1.0, None, ALU.mult))

            dve.wait_ge(pp_exp_out, 1)
            dve.tensor_reduce(pp[:], lp, AX.X, ALU.add).then_inc(mix_order, 1)
            dve.wait_ge(mix_order, 7)
            dve.reciprocal(pp[:], pp[:]).then_inc(mix_order, 1)
            dve.wait_ge(mix_order, 8)
            dve.tensor_tensor(lp, lp, pp4, ALU.mult).then_inc(pp_ready, 1)

            def iteration(base):
                for side in range(2):
                    view = turned if side else (lambda ap: ap)
                    over_other = over_cols if side else over_rows
                    level(sink_order, base + 3 * side, sink_order,
                          lambda h: dve.tensor_tensor(halves(T, h), halves(K, h), over_other(halves(fac[:, 1 - side], h)), ALU.mult))
                    level(sink_order, base + 3 * side + 1, sink_order,
                          lambda h: dve.tensor_reduce(halves(red[:, side], h), view(halves(T, h)), AX.X, ALU.add))
                    level(sink_order, base + 3 * side + 2, sink_order,
                          lambda h: dve.reciprocal(halves(fac[:, side], h), halves(red[:, side], h)))

            def segment(base):
                with dve.Fori(0, ROUNDS) as r:
                    for i in range(ROUND):
                        iteration(r * (6 * ROUND) + (base + 6 * i))

            with dve.Fori(0, REFRESHES) as c:
                segment(c * SEGMENT_LEVELS + START_LEVELS)
                base = c * SEGMENT_LEVELS + (START_LEVELS + ROUNDS_LEVELS)
                level(sink_from_act, c * 2 + 3, sink_order,
                      lambda h: dve.tensor_tensor(lse[:, :, h * HT:(h + 1) * HT], lse[:, :, h * HT:(h + 1) * HT],
                                                  fac[:, :, h * HT:(h + 1) * HT], ALU.add))
                level(sink_order, base + 1, sink_order,
                      lambda h: dve.tensor_tensor(halves(T, h), halves(Z, h), over_cols(halves(lse[:, 0], h)), ALU.add))
                level(sink_order, base + 2, sink_to_act,
                      lambda h: dve.tensor_tensor(halves(T, h), halves(T, h), over_rows(halves(lse[:, 1], h)), ALU.add))
                level(sink_from_act, c * 2 + 4, sink_order, lambda h: dve.memset(halves(fac[:, 1], h), 1.0))
            done = START_LEVELS + REFRESHES * SEGMENT_LEVELS
            segment(done)
            done += ROUNDS_LEVELS
            for i in range(LAST_ROUND):
                iteration(done)
                done += 6
            level(sink_order, done, sink_order,
                  lambda h: dve.tensor_tensor(halves(K, h), halves(T, h), over_rows(halves(fac[:, 1], h)), ALU.mult))
            level(sink_order, done + 1, sink_order,
                  lambda h: dve.tensor_scalar(halves(K, h), halves(K, h), scalars[:, 1:2], None, ALU.mult))
            dve.wait_ge(sink_order, 2 * (done + 2))
            dve.wait_ge(y_added, 2)
            diagonal = K.rearrange("p t i j -> p t (i j)")[:, :, 0:STREAMS * STREAMS:STREAMS + 1]
            dve.tensor_scalar(diagonal, diagonal, scalars[:, 2:3], None, ALU.add).then_inc(h_ready, 1)
            dve.wait_ge(h_ready, 1)
            for t in range(DVE_TILES):
                for j in range(STREAMS):
                    for i in range(STREAMS):
                        count = (t * STREAMS + j) * STREAMS + i
                        if j:
                            dve.wait_ge(mixed, count - STREAMS + 1)
                        dve.scalar_tensor_tensor(out=x[:, t, tok(i)], in0=wq_raw[:, t, tok(j)],
                                                 scalar=K[:, t, i, j:j + 1], in1=x[:, t, tok(i)],
                                                 op0=ALU.mult, op1=ALU.add).then_inc(mixed, 1)


def rotary_tables():
    inv = (np.float32(1.0) / np.float32(10000.0) ** (np.arange(0, DH, 2, dtype=np.float32) / np.float32(DH))).astype(np.float32)
    angle = np.arange(MAX_POS, dtype=np.float32)[:, None] * inv[None, :]
    c, s = np.cos(angle).astype(np.float32), np.sin(angle).astype(np.float32)
    return np.ascontiguousarray(np.concatenate([c, c, s, -s], axis=1))


def kernel(**inputs):
    import concourse.bacc as bacc
    from concourse.bass_utils import run_bass_kernel_spmd

    a = {name: np.asarray(value) for name, value in inputs.items()}
    bkv = a["L0_xattn_bkv"].reshape(2, GROUPS, 1, DH)
    bqkv0 = np.concatenate([a["L0_xattn_bq"].reshape(GROUPS, GH, DH), bkv[0], bkv[1]], axis=1).transpose(2, 0, 1).reshape(DH, -1)
    arrays = {
        "x": a["x"].reshape(NT, D),
        "ctx_t": a["ctx_4096"].reshape(NT, D).T,
        "pos": a["pos_BxS2"].reshape(NT),
        "mask": a["mask_BxSxS2_ik0"],
        "wq0": a["L0_xattn_Wq"], "bqkv0": bqkv0,
        "wkv0": a["L0_xattn_Wkv"],
        "wo0": a["L0_xattn_Wo"], "bo0": a["L0_xattn_bo"],
        "wbase_t": a["L0_ffn_W_base"].T, "bbase": a["L0_ffn_b_base"],
        "gates_t": np.concatenate([a["L0_ffn_W_gate"], a["L0_ffn_W_thr"]]).T,
        "b_thr": a["L0_ffn_b_thr"],
        "a_t": a["L0_ffn_A"].reshape(EXPERTS * RANK, D).T,
        "b_mat": a["L0_ffn_B"].transpose(0, 2, 1).reshape(EXPERTS * RANK, D),
        "wq1": a["L1_xattn_Wq"], "wk1": a["L1_xattn_Wk"], "wv1": a["L1_xattn_Wv"], "wo1": a["L1_xattn_Wo"],
        "mix_t": np.concatenate([a["L1_ffn_W_res"], a["L1_ffn_W_pre"], a["L1_ffn_W_post"]]).T,
        "mix_base": np.concatenate([a["L1_ffn_H_res_base"].reshape(-1), a["L1_ffn_H_pre_base"], a["L1_ffn_H_post_base"]]),
        "gate": a["L1_ffn_gate"], "w_branch": a["L1_ffn_W_branch"],
        "tables": rotary_tables(),
    }
    arrays = {f"in_{name}": np.ascontiguousarray(value) for name, value in arrays.items()}
    nc = bacc.Bacc("TRN2", target_bir_lowering=False, num_devices=1)
    args = [nc.dram_tensor(name, v.shape, mybir.dt.from_np(v.dtype), kind="ExternalInput").ap() for name, v in arrays.items()]
    out = nc.dram_tensor("out_x", (NT, D), F32, kind="ExternalOutput").ap()
    bass_two_layers(nc, *args, out)
    result = run_bass_kernel_spmd(nc, [arrays], core_ids=[0])
    return result.results[0]["out_x"].reshape(B, S, D)
```
